# Optimizing a Trainium2 kernel written in Bass

```python
import numpy as np
import jax
import jax.numpy as jnp

def _softmax(x, axis=-1):
    return jax.nn.softmax(x, axis=axis)

def _gelu(x):
    return jax.nn.gelu(x, approximate=True)

def _silu(x):
    return jax.nn.silu(x)

def _sigmoid(x):
    return jax.nn.sigmoid(x)

def _layernorm(x, axis=-1, eps=1e-05):
    m = jnp.mean(x, axis=axis, keepdims=True)
    v = jnp.var(x, axis=axis, keepdims=True)
    return (x - m) / jnp.sqrt(v + eps)

def _scatter_add(tgt, idx, src, axis=0):
    return tgt.at[idx].add(src)

def _segment_sum(src, seg, n):
    return jax.ops.segment_sum(src, seg, n)
kernel_name = 'mk_gnn_preln_d2_gnn_r64_c79a39'

def setup_inputs(seed: int=0):
    np.random.seed(seed)
    _w = jnp.asarray

    def _rec_inputs():
        import jax
        import jax.numpy as jnp
        _gk = jax.random.key(seed)
        x = -0.000202 + 1 * jax.random.normal(jax.random.fold_in(_gk, 1), (100000, 128), jnp.float32)
        src = jax.random.randint(jax.random.fold_in(_gk, 2), (25000,), 0, 100000, jnp.int32)
        dst = jax.random.randint(jax.random.fold_in(_gk, 3), (25000,), 0, 100000, jnp.int32)
        _o = jnp.argsort(dst, stable=True)
        src = src[_o]
        dst = dst[_o]
        edge_attr_128 = -8.513e-05 + 0.999844 * jax.random.normal(jax.random.fold_in(_gk, 12), (25000, 128), jnp.float32)
        edge_attr_32 = jax.random.uniform(jax.random.fold_in(_gk, 13), (25000, 32), jnp.float32, 0.0, 1)
        edge_weight = jax.random.uniform(jax.random.fold_in(_gk, 15), (25000,), jnp.float32, 0.0, 0.999998)
        return (x, src, dst, edge_attr_128, edge_attr_32, edge_weight)
    x, src, dst, edge_attr_128, edge_attr_32, edge_weight = _rec_inputs()

    def _L0_gnn_setup():
        import jax, jax.numpy as jnp
        import numpy as np
        N, E, D, H = (50000, 10000, 128, 8)
        d = D // H

        def layernorm(x, g, b, eps=1e-05):
            mu = jnp.mean(x, axis=-1, keepdims=True)
            var = jnp.var(x, axis=-1, keepdims=True)
            return (x - mu) * jax.lax.rsqrt(var + eps) * g + b
        key = jax.random.key(seed)
        ks = jax.random.split(key, 14)
        s = 0.05
        return {'node_emb': jax.random.normal(ks[0], (N, D), jnp.float32), 'bond_emb': jax.random.normal(ks[1], (E, D), jnp.float32), 'basic_attn': jax.random.uniform(ks[2], (E,), jnp.float32), 'src': jax.random.randint(ks[3], (E,), 0, N), 'dst': jax.random.randint(ks[4], (E,), 0, N), 'Wk': jax.random.normal(ks[5], (D, D), jnp.float32) * s, 'Wq': jax.random.normal(ks[6], (D, D), jnp.float32) * s, 'Wv': jax.random.normal(ks[7], (D, D), jnp.float32) * s, 'W_dis': jax.random.normal(ks[8], (1, H), jnp.float32) * s, 'W_beta': jax.random.normal(ks[9], (3 * D, 1), jnp.float32) * s, 'ln1_g': jnp.ones((D,), jnp.float32), 'ln1_b': jnp.zeros((D,), jnp.float32), 'W_ff1': jax.random.normal(ks[10], (D, 2 * D), jnp.float32) * s, 'W_ff2': jax.random.normal(ks[11], (2 * D, D), jnp.float32) * s}
    _L0_gnn_all = _L0_gnn_setup()
    _L0_gnn_in = {k: v for k, v in _L0_gnn_all.items() if k in ('Wk', 'Wq', 'Wv', 'W_dis', 'W_beta', 'ln1_g', 'ln1_b', 'W_ff1', 'W_ff2')}
    del _L0_gnn_all

    def _L1_gnn_setup():
        import jax, jax.numpy as jnp
        import numpy as np
        LOG2 = float(np.log(2.0))

        def ssp(v):
            return jax.nn.softplus(v) - jnp.asarray(LOG2, v.dtype)
        key = jax.random.key(seed)
        ks = jax.random.split(key, 16)
        N, B, F, R, P = (100000, 128, 64, 32, 25000)
        inp = {'x': jax.random.normal(ks[0], (N, B), jnp.float32), 'f_ij': jax.random.uniform(ks[1], (P, R), jnp.float32), 'rcut_ij': jax.random.uniform(ks[2], (P,), jnp.float32), 'pairlist': jax.random.randint(ks[3], (2, P), 0, N, jnp.int64), 'w_in': jax.random.normal(ks[4], (B, F), jnp.float32) * (1.0 / np.sqrt(B)), 'b_in': jnp.zeros((F,), jnp.float32), 'w_f1': jax.random.normal(ks[5], (R, F), jnp.float32) * (1.0 / np.sqrt(R)), 'b_f1': jnp.zeros((F,), jnp.float32), 'w_f2': jax.random.normal(ks[6], (F, F), jnp.float32) * (1.0 / np.sqrt(F)), 'b_f2': jnp.zeros((F,), jnp.float32), 'w_o1': jax.random.normal(ks[7], (F, B), jnp.float32) * (1.0 / np.sqrt(F)), 'b_o1': jnp.zeros((B,), jnp.float32), 'w_o2': jax.random.normal(ks[8], (B, B), jnp.float32) * (1.0 / np.sqrt(B)), 'b_o2': jnp.zeros((B,), jnp.float32)}
        return inp
    _L1_gnn_all = _L1_gnn_setup()
    _L1_gnn_in = {k: v for k, v in _L1_gnn_all.items() if k in ('w_in', 'b_in', 'w_f1', 'b_f1', 'w_f2', 'b_f2', 'w_o1', 'b_o1', 'w_o2', 'b_o2')}
    del _L1_gnn_all
    return {'x': x, 'src': src, 'dst': dst, 'edge_attr_128': edge_attr_128, 'edge_attr_32': edge_attr_32, 'edge_weight': edge_weight, 'L0_gnn_Wk': _L0_gnn_in['Wk'], 'L0_gnn_Wq': _L0_gnn_in['Wq'], 'L0_gnn_Wv': _L0_gnn_in['Wv'], 'L0_gnn_W_dis': _L0_gnn_in['W_dis'], 'L0_gnn_W_beta': _L0_gnn_in['W_beta'], 'L0_gnn_ln1_g': _L0_gnn_in['ln1_g'], 'L0_gnn_ln1_b': _L0_gnn_in['ln1_b'], 'L0_gnn_W_ff1': _L0_gnn_in['W_ff1'], 'L0_gnn_W_ff2': _L0_gnn_in['W_ff2'], 'L1_gnn_w_in': _L1_gnn_in['w_in'], 'L1_gnn_b_in': _L1_gnn_in['b_in'], 'L1_gnn_w_f1': _L1_gnn_in['w_f1'], 'L1_gnn_b_f1': _L1_gnn_in['b_f1'], 'L1_gnn_w_f2': _L1_gnn_in['w_f2'], 'L1_gnn_b_f2': _L1_gnn_in['b_f2'], 'L1_gnn_w_o1': _L1_gnn_in['w_o1'], 'L1_gnn_b_o1': _L1_gnn_in['b_o1'], 'L1_gnn_w_o2': _L1_gnn_in['w_o2'], 'L1_gnn_b_o2': _L1_gnn_in['b_o2']}

def reference(x, src, dst, edge_attr_128, edge_attr_32, edge_weight, L0_gnn_Wk, L0_gnn_Wq, L0_gnn_Wv, L0_gnn_W_dis, L0_gnn_W_beta, L0_gnn_ln1_g, L0_gnn_ln1_b, L0_gnn_W_ff1, L0_gnn_W_ff2, L1_gnn_w_in, L1_gnn_b_in, L1_gnn_w_f1, L1_gnn_b_f1, L1_gnn_w_f2, L1_gnn_b_f2, L1_gnn_w_o1, L1_gnn_b_o1, L1_gnn_w_o2, L1_gnn_b_o2):
    import jax
    import jax.numpy as jnp

    def _L0_gnn_ref(node_emb, bond_emb, basic_attn, src, dst, Wk, Wq, Wv, W_dis, W_beta, ln1_g, ln1_b, W_ff1, W_ff2):
        import jax, jax.numpy as jnp
        import numpy as np
        N, E, D, H = (50000, 10000, 128, 8)
        d = D // H

        def layernorm(x, g, b, eps=1e-05):
            mu = jnp.mean(x, axis=-1, keepdims=True)
            var = jnp.var(x, axis=-1, keepdims=True)
            return (x - mu) * jax.lax.rsqrt(var + eps) * g + b
        n = node_emb.shape[0]
        k = (node_emb @ Wk).reshape(n, H, d)
        q = (node_emb @ Wq).reshape(n, H, d)
        v = (bond_emb @ Wv).reshape(-1, H, d)
        scores = jnp.einsum('ehd,ehd->eh', k[src], q[dst])
        scores = scores / jnp.sqrt(jnp.asarray(d, scores.dtype))
        dist = basic_attn[:, None] @ W_dis
        logits = scores + dist
        mx = jax.ops.segment_max(logits, dst, num_segments=n)
        mx = jnp.where(jnp.isfinite(mx), mx, 0.0)
        e = jnp.exp(logits - mx[dst])
        den = jax.ops.segment_sum(e, dst, num_segments=n)
        att = e / (den[dst] + 1e-16)
        ft = jax.ops.segment_sum(v * att[:, :, None], dst, num_segments=n)
        he = ft.reshape(n, D)
        beta = jax.nn.sigmoid(jnp.concatenate([he, node_emb, he - node_emb], axis=-1) @ W_beta)
        he = beta * node_emb + (1.0 - beta) * he
        h = layernorm(he, ln1_g, ln1_b)
        out = jax.nn.relu(h @ W_ff1) @ W_ff2
        ones = jnp.ones((D,), he.dtype)
        zeros = jnp.zeros((D,), he.dtype)
        return layernorm(out + he, ones, zeros)

    def _L1_gnn_ref(x, f_ij, rcut_ij, pairlist, w_in, b_in, w_f1, b_f1, w_f2, b_f2, w_o1, b_o1, w_o2, b_o2):
        import jax, jax.numpy as jnp
        import numpy as np
        LOG2 = float(np.log(2.0))

        def ssp(v):
            return jax.nn.softplus(v) - jnp.asarray(LOG2, v.dtype)
        n_atoms = x.shape[0]
        h = x @ w_in + b_in
        Wij = ssp(f_ij @ w_f1 + b_f1) @ w_f2 + b_f2
        Wij = Wij * rcut_ij[:, None]
        idx_i, idx_j = (pairlist[0], pairlist[1])
        x_ij = h[idx_j] * Wij
        agg = jax.ops.segment_sum(x_ij, idx_i, num_segments=n_atoms)
        out = ssp(agg @ w_o1 + b_o1) @ w_o2 + b_o2
        return out
    edge_index = jnp.stack([src, dst])
    h = jnp.maximum(_layernorm(x, axis=-1), 0.0)
    x = x + _L0_gnn_ref(h, edge_attr_128, edge_weight, src, dst, L0_gnn_Wk, L0_gnn_Wq, L0_gnn_Wv, L0_gnn_W_dis, L0_gnn_W_beta, L0_gnn_ln1_g, L0_gnn_ln1_b, L0_gnn_W_ff1, L0_gnn_W_ff2)
    h = jnp.maximum(_layernorm(x, axis=-1), 0.0)
    x = x + _L1_gnn_ref(h, edge_attr_32, edge_weight, edge_index, L1_gnn_w_in, L1_gnn_b_in, L1_gnn_w_f1, L1_gnn_b_f1, L1_gnn_w_f2, L1_gnn_b_f2, L1_gnn_w_o1, L1_gnn_b_o1, L1_gnn_w_o2, L1_gnn_b_o2)
    return x

_drawn_inputs = setup_inputs


def setup_inputs(seed=0):
    import zlib

    import numpy as np

    out = dict(_drawn_inputs(seed))
    spreads = {'L0_gnn_ln1_g': (1.0, 0.2),
     'L0_gnn_ln1_b': (0.0, 0.1),
     'L1_gnn_b_in': (0.0, 0.8),
     'L1_gnn_b_f1': (0.0, 0.8),
     'L1_gnn_b_f2': (0.0, 0.8),
     'L1_gnn_b_o1': (0.0, 0.1),
     'L1_gnn_b_o2': (0.0, 0.1)}
    factors = {'edge_attr_32': 6.164,
     'edge_weight': 5.68,
     'L0_gnn_Wk': 8.0,
     'L0_gnn_Wq': 8.0,
     'L0_gnn_W_dis': 8.0,
     'L1_gnn_w_in': 2.843,
     'L1_gnn_w_f1': 3.085,
     'L1_gnn_w_f2': 2.82,
     'L1_gnn_w_o1': 2.868}
    for name, (base, spread) in spreads.items():
        noise = np.random.default_rng([zlib.crc32(name.encode()), seed]).standard_normal(out[name].shape)
        drawn = base * np.exp(spread * noise) if base else spread * noise
        out[name] = jnp.asarray(drawn.astype(out[name].dtype))
    for name, factor in factors.items():
        out[name] = (out[name] * factor).astype(out[name].dtype)
    return out
```

```python
import concourse.bass as bass
from concourse import mybir
from contextlib import ExitStack

F32 = mybir.dt.float32
I32 = mybir.dt.int32
ALU = mybir.AluOpType
ACT = mybir.ActivationFunctionType

P = 128
T = 4
R = P * T
U = 4
EPS = 1e-5
FAR = 1e30


class At:

    def __init__(self, rounds, m, ones, sixteens):
        self.rounds, self.m, self.ones, self.sixteens = rounds, m, ones, sixteens

    def slot(self, n, back=0):
        return (self.m - back) % n

    def done(self, back=0):
        return self.ones(self.m - back + 1)

    def landed(self, back=0, parts=1):
        return self.sixteens((self.m - back) // U + 1, parts)

    def count(self, per, j, back=0):
        return self.rounds * (U * per) + ((self.m - back) * per + j)

    def row(self, eng, per):
        if isinstance(self.rounds, int):
            return self.m * per
        return eng.snap(self.rounds * (U * per) + self.m * per)

    def row_back(self, eng, groups, per):
        if isinstance(self.rounds, int):
            return (groups - 1 - self.m) * per
        return eng.snap((groups - 1 - self.m) * per - self.rounds * (U * per))


def walk(eng, count, step, lags, parts=(1,), depth=5):
    last = max(lags)
    first = -(-(last + depth) // U)
    rounds = (count - 1) // U

    def peeled(n):
        for lag in lags:
            if 0 <= n - lag < count:
                step(At(0, n - lag, lambda c: c, lambda c, parts: 16 * parts * c), lag)

    if rounds <= first:
        for n in range(count + last):
            peeled(n)
        return
    for n in range(first * U):
        peeled(n)
    with eng.Fori(first, rounds) as q:
        ones = {c: eng.snap(q * U + c) for c in range(-last - depth + 1, U + 1)}
        sixteens = {(c, n): eng.snap(q * (16 * n) + 16 * n * c) for c in range(-1, 2) for n in parts}
        for m in range(U):
            for lag in lags:
                step(At(q, m - lag, ones.__getitem__, lambda c, n: sixteens[c, n]), lag)
    for n in range(rounds * U, count + last):
        peeled(n)


def after(eng, sem, value):
    if not isinstance(value, int) or value > 0:
        eng.wait_ge(sem, value)


def held(eng, passed, sem, value):
    if not isinstance(value, int):
        eng.wait_ge(sem, value)
        eng.sem_inc(passed, 1)
    elif value > 0:
        eng.wait_ge(sem, value)


def build(nc, x, attrT, fT, w_col, w_row, src_col, dst_col, next_col, src_row, dst_row,
          Wk, Wq, Wv, W_dis, W_beta, ln1_g, ln1_b, W_ff1, W_ff2,
          w_in, b_in, w_f1, b_f1, w_f2, b_f2, w_o1, b_o1, w_o2, b_o2, out):
    N, D = x.shape
    HEADS = W_dis.shape[1]
    F = W_ff1.shape[1]
    H2 = F // P
    FW, FF = w_f1.shape
    GROUPS = -(-N // R)
    EG = src_col.shape[0] // P
    TRASH = N + 1
    AGG_ROWS = -(-(TRASH + R) // (P * 8)) * P * 8

    agg = nc.dram_tensor("agg", [AGG_ROWS, FF], F32, kind="Internal").ap()
    xd_dram = nc.dram_tensor("xd_dram", [EG * P, T * D], F32, kind="Internal").ap()
    q_dram = nc.dram_tensor("q_dram", [P, EG * R], F32, kind="Internal").ap()
    lead_dram = nc.dram_tensor("lead_dram", [EG * P, T], I32, kind="Internal").ap()
    y_dram = nc.dram_tensor("y_dram", [EG * P, T * D], F32, kind="Internal").ap()

    ctx = ExitStack()
    with ctx:
        def sb(name, shape, dt=F32):
            return ctx.enter_context(nc.sbuf_tensor(name, shape, dt))

        signals = []

        def sem(name):
            signals.append(nc.alloc_semaphore(name=name))
            return signals[-1]

        def sems(*names):
            return [sem(n) for n in names]

        bank = ctx.enter_context(nc.psum_tensor("bank", [P, 8, R], F32))

        class Stats:

            def __init__(self, name, n, sb):
                self.n = n
                self.bn = sb(name + "_bn", [P, 2, n, 6])
                self.dif = sb(name + "_dif", [P, 2, n])
                self.spread = sb(name + "_spread", [P, 2, n])
                self.sq = sb(name + "_sq", [P, 2, n])
                self.mean = sb(name + "_mean", [P, 2, n])
                self.var = sb(name + "_var", [P, 2, n])
                self.ln = sb(name + "_ln", [P, 2, n])
                self.rstd = sb(name + "_rstd", [P, 2, n])
                self.steps, self.roots = sems(name + "_steps", name + "_roots")

            def on_vector(self, dve, a, src):
                s = a.slot(2)
                for j in range(self.n):
                    last = dve.bn_stats(self.bn[:, s, j], src[:, j])
                last.then_inc(self.steps, 1)
                dve.wait_ge(self.steps, a.count(4, 1))
                of = lambda c: self.bn[:, s, :, c]
                dve.tensor_tensor(self.dif[:, s], of(1), of(4), ALU.subtract).then_inc(self.steps, 1)
                dve.tensor_tensor(self.spread[:, s], of(2), of(5), ALU.add)
                dve.wait_ge(self.steps, a.count(4, 2))
                dve.scalar_tensor_tensor(self.mean[:, s], self.dif[:, s], -0.5, of(1), ALU.mult, ALU.add)
                dve.scalar_tensor_tensor(self.sq[:, s], self.dif[:, s], 0.25, self.dif[:, s], ALU.mult, ALU.mult)\
                   .then_inc(self.steps, 1)
                dve.wait_ge(self.steps, a.count(4, 3))
                dve.scalar_tensor_tensor(self.var[:, s], self.spread[:, s], 1.0 / D, self.sq[:, s], ALU.mult, ALU.add)\
                   .then_inc(self.steps, 1)

            def on_scalar(self, act, a, var=None):
                s = a.slot(2)
                act.activation(self.ln[:, s], (self.var if var is None else var)[:, s], ACT.Ln, bias=eps_col[:, 0:1])\
                   .then_inc(self.roots, 1)
                act.wait_ge(self.roots, a.count(2, 1))
                act.activation(self.rstd[:, s], self.ln[:, s], ACT.Exp, scale=-0.5).then_inc(self.roots, 1)

            def wait_mean(self, eng, a):
                eng.wait_ge(self.steps, a.count(4, 4))

            def wait_rstd(self, eng, a):
                eng.wait_ge(self.roots, a.count(2, 2))

        ident = sb("ident", [P, P])
        upper = sb("upper", [P, P])
        ones_col = sb("ones_col", [P, 1])
        head_of = sb("head_of", [P, HEADS])
        head_to = sb("head_to", [HEADS, P])
        trash = sb("trash", [P, T])
        trash_i = sb("trash_i", [P, T], I32)
        w1_raw = sb("w1_raw", [P, F])
        w1_g = sb("w1_g", [P, F])
        w2_sb = sb("w2_sb", [P, H2, D])
        g_col = sb("g_col", [P, 1])
        b_col = sb("b_col", [P, 1])
        z_bias = sb("z_bias", [P, H2])
        eps_col = sb("eps_col", [P, 1])
        half_col = sb("half_col", [P, 1])
        wb_x = sb("wb_x", [P, D])
        wb_d = sb("wb_d", [P, D])
        wb_row = sb("wb_row", [P, D])
        wb_he = sb("wb_he", [P, 2])
        wb_he_col = sb("wb_he_col", [P, 1])
        w_o2_sb = sb("w_o2_sb", [P, D])
        b_o1_col = sb("b_o1_col", [P, 1])
        b_o2_row = sb("b_o2_row", [P, D])
        ssp_abs = sb("ssp_abs", [P, 1])
        ssp_exp = sb("ssp_exp", [P, 1])
        ssp_ln = sb("ssp_ln", [P, 1])
        ssp_b = sb("ssp_b", [P, 1])
        ssp_rep = sb("ssp_rep", [P, P])
        c_row = sb("c_row", [P, D])
        wk_sb = sb("wk_sb", [P, D])
        wq_sb = sb("wq_sb", [P, D])
        wv_sb = sb("wv_sb", [P, D])
        wdis_sb = sb("wdis_sb", [1, HEADS])
        w_in_sb = sb("w_in_sb", [P, FF])
        b_in_row = sb("b_in_row", [P, FF])
        wf1_sb = sb("wf1_sb", [FW, FF])
        bf1_col = sb("bf1_col", [FF, 1])
        wf2_sb = sb("wf2_sb", [FF + 1, FF])
        wo1_sb = sb("wo1_sb", [FF, D])
        zeros = sb("zeros", [P, 32 * FF])
        consts_loaded, made, sp_passed, pool_passed, pe_passed, made_too, c_dve, c_act, c_pe, zeroed, agg_zero = sems(
            "consts_loaded", "made", "sp_passed", "pool_passed", "pe_passed", "made_too", "c_dve", "c_act", "c_pe", "zeroed", "agg_zero")

        def row(v):
            return v.rearrange("(a d) -> a d", a=1).partition_broadcast(P)

        def col(v):
            return v.rearrange("(p a) -> p a", a=1)

        LOADS = ((w1_raw[:], W_ff1), (w2_sb[:], W_ff2.rearrange("(h p) d -> p h d", p=P)), (g_col[:], col(ln1_g)),
                 (b_col[:], col(ln1_b)), (wb_x[:], W_beta[D:2 * D, :].rearrange("d a -> a d").partition_broadcast(P)),
                 (wb_d[:], W_beta[2 * D:3 * D, :].rearrange("d a -> a d").partition_broadcast(P)),
                 (wb_he[:, 0:1], W_beta[0:D, :]), (wb_he[:, 1:2], W_beta[2 * D:3 * D, :]),
                 (w_o2_sb[:], w_o2), (b_o1_col[:], col(b_o1)), (b_o2_row[:], row(b_o2)),
                 (wk_sb[:], Wk), (wq_sb[:], Wq), (wv_sb[:], Wv), (wdis_sb[:], W_dis), (w_in_sb[:], w_in),
                 (b_in_row[:], row(b_in)), (wf1_sb[:], w_f1), (bf1_col[:], col(b_f1)), (wf2_sb[0:FF, :], w_f2),
                 (wf2_sb[FF:FF + 1, :], b_f2.rearrange("(a d) -> a d", a=1)), (wo1_sb[:], w_o1))
        ALL_LOADED = 16 * len(LOADS)

        def ring(name):
            return [sem(f"{name}{k}") for k in range(U)]

        def named(prefix, words):
            return sems(*(f"{prefix}_{w}" for w in words.split()))

        ROOM = 41 * 1024
        room = sb("room", [P, ROOM])
        taken = [0]

        def fsb(name, shape, dt=F32):
            sizes = dict(zip("abc", shape[1:]))
            width = 1
            for n in sizes.values():
                width *= n
            part = room[0:shape[0], taken[0]:taken[0] + width]
            taken[0] += width
            assert taken[0] <= ROOM, name
            part = part if dt == F32 else part.bitcast(dt)
            names = " ".join(sizes)
            return part.rearrange(f"p ({names}) -> p {names}", **sizes) if len(sizes) > 1 else part

        f_idx = fsb("f_idx", [P, U, 2, T], I32)
        f_dst = fsb("f_dst", [HEADS, U, R + 2], I32)
        f_w = fsb("f_w", [1, U, R])
        f_attr = fsb("f_attr", [P, U, R])
        f_x = fsb("f_x", [P, 2, 2 * T, D])
        f_xn = fsb("f_xn", [P, 2 * T, D])
        f_hT = fsb("f_hT", [P, 2, R])
        f_kT = fsb("f_kT", [P, R])
        f_vT = fsb("f_vT", [P, 2, R])
        f_prod = fsb("f_prod", [P, R])
        f_same = fsb("f_same", [HEADS, R])
        f_last = fsb("f_last", [HEADS, R])
        f_pen = fsb("f_pen", [HEADS, R])
        f_max = fsb("f_max", [HEADS, 2, R + 1])
        f_was = fsb("f_was", [HEADS, R])
        f_arg = fsb("f_arg", [HEADS, 2, R])
        f_ae = fsb("f_ae", [HEADS, 2, R])
        f_den = fsb("f_den", [HEADS, 2, R])
        f_dene = fsb("f_dene", [HEADS, R])
        f_rden = fsb("f_rden", [HEADS, R])
        f_rlast = fsb("f_rlast", [HEADS, R])
        f_ev = fsb("f_ev", [P, R])
        f_sum = fsb("f_sum", [P, 2, R])
        f_q = fsb("f_q", [P, 2, R])
        f_st = Stats("f_st", 2 * T, fsb)
        f_loaded, f_got, f_xd_out, f_q_out = ring("f_loaded"), ring("f_got"), ring("f_xd_out"), ring("f_q_out")
        (f_xn_done, f_tr_done, f_h_done, f_kqv_done, f_kv_done, f_flags_done, f_prod_done, f_l_done, f_pen_done,
         f_carry_done, f_max_done, f_was_done, f_args_done, f_exps_done, f_den_done, f_dene_done, f_rden_done,
         f_rlast_done, f_spread_done, f_ev_done, f_sum_done, f_q_done) = named("f", (
             "xn_done tr_done h_done kqv_done kv_done flags_done prod_done l_done pen_done carry_done max_done was_done "
             "args_done exps_done den_done dene_done rden_done rlast_done spread_done ev_done sum_done q_done"))
        TR_S, TR_D, K_R, Q_, V_, L_, A_, E_ = range(8)

        d_x = fsb("d_x", [P, U, T, D])
        d_xc = fsb("d_xc", [P, U, T, D])
        d_out = fsb("d_out", [P, 2, T, D])
        d_u = fsb("d_u", [P, 2, T, D])
        d_un = fsb("d_un", [P, 2, T, D])
        d_unT = fsb("d_unT", [P, R])
        d_rz = fsb("d_rz", [P, H2, R])
        d_y = fsb("d_y", [P, 2, T, D])
        d_yn = fsb("d_yn", [P, 2, T, D])
        d_junk = fsb("d_junk", [P, T, D])
        (d_dot, d_arg, d_ex, d_exp1, d_beta, d_scale, d_scale2, d_uvar, d_t, d_nm) = (
            fsb("d_" + n, [P, 2, T]) for n in "dot arg ex exp1 beta scale scale2 uvar t nm".split())
        d_xst, d_ust, d_yst = Stats("d_xst", T, fsb), Stats("d_ust", T, fsb), Stats("d_yst", T, fsb)
        d_loaded, d_stored = ring("d_loaded"), ring("d_stored")
        (d_u_done, d_dot_done, d_arg_done, d_ex_done, d_exp1_done, d_beta_done, d_scale_done, d_scale2_done, d_uvar_done,
         d_t_done, d_un_done, d_tr_done, d_unT_done, d_z_done, d_rz_done, d_o_done, d_y_done, d_nm_done, d_yn_done,
         d_xc_done, d_out_done) = named("d", (
             "u_done dot_done arg_done ex_done exp1_done beta_done scale_done scale2_done uvar_done t_done un_done "
             "tr_done unT_done z_done rz_done o_done y_done nm_done yn_done xc_done out_done"))
        D_TR, D_Z, D_O = 0, 1, 3



        def all_of(eng, ring, count, parts=1):
            for k in range(U):
                eng.wait_ge(ring[k], 16 * parts * ((count - 1 - k) // U + 1))

        def nodes_stored(eng):
            all_of(eng, f_q_out, EG)
            all_of(eng, f_xd_out, EG)
            all_of(eng, d_stored, GROUPS)

        def edges_over(eng):
            for done in (b_totc_done, b_out_done, b_idx_done):
                eng.wait_ge(done, EG)

        def node_rows(dram, at):
            at = min(at, N - R) if isinstance(at, int) else at
            return dram[bass.ds(at, R), :].rearrange("(p j) d -> p j d", j=T)

        def spill(dram, at):
            return dram[bass.ds(at, P), :].rearrange("p (j d) -> p j d", j=T)

        def col_of(dram, at):
            return dram[bass.ds(at, P), :]

        def tiles(b):
            return bank[:, b].rearrange("p (j d) -> p j d", j=T)

        def gather(pool, to, dram, index, last_row, signal):
            pool.indirect_dma_start(to, None, dram, bass.IndirectOffsetOnAxis(ap=index, axis=0),
                                    bounds_check=last_row, oob_is_err=False).then_inc(signal, 16)

        def scatter(pool, dram, index, rows, last_row, signal):
            pool.indirect_dma_start(dram, bass.IndirectOffsetOnAxis(ap=index, axis=0), rows, None,
                                    bounds_check=last_row, oob_is_err=False).then_inc(signal, 16)

        c_b = c_row[:].rearrange("p (a d) -> p a d", a=1).to_broadcast([P, T, D])

        with nc.Block() as block:
            @block.sync
            def _(sp):
                for dst, src in LOADS:
                    sp.dma_start(dst, src).then_inc(consts_loaded, 16)
                sp.wait_ge(zeroed, 1)
                table = agg.rearrange("(p c) f -> p (c f)", p=P)
                per, piece = AGG_ROWS // P * FF, 32 * FF
                for lo in range(0, per, piece):
                    hi = min(lo + piece, per)
                    sp.dma_start(table[:, lo:hi], zeros[:, 0:hi - lo]).then_inc(agg_zero, 16)
                sp.wait_ge(agg_zero, 16 * -(-per // piece))

                def f_step(a, lag):
                    k = a.slot(U)
                    if lag == 0:
                        at_p, at_r = a.row(sp, P), a.row(sp, R)
                        held(sp, sp_passed, f_q_done, a.done(U))
                        sp.dma_start(f_idx[:, k, 0], col_of(src_col, at_p)).then_inc(f_loaded[k], 16)
                        sp.dma_start(f_idx[:, k, 1], col_of(dst_col, at_p)).then_inc(f_loaded[k], 16)
                        sp.dma_start(f_dst[:, k], dst_row[:, bass.ds(at_r, R + 2)].partition_broadcast(HEADS)).then_inc(f_loaded[k], 16)
                        sp.dma_start(f_w[:, k], w_row[:, bass.ds(at_r, R)]).then_inc(f_loaded[k], 16)
                        sp.dma_start(f_attr[:, k], attrT[:, bass.ds(at_r, R)]).then_inc(f_loaded[k], 16)
                    if lag == 1:
                        at_p = a.row(sp, P)
                        held(sp, sp_passed, f_got[k], a.landed(parts=2 * T))
                        sp.dma_start(spill(xd_dram, at_p), f_x[:, a.slot(2), T:]).then_inc(f_xd_out[k], 16)
                    if lag == 3:
                        at_r = a.row(sp, R)
                        held(sp, sp_passed, f_q_done, a.done())
                        sp.dma_start(q_dram[:, bass.ds(at_r, R)], f_q[:, a.slot(2)]).then_inc(f_q_out[k], 16)
                walk(sp, EG, f_step, [0, 1, 3], parts=(1, 2 * T))

                def d_step(a, lag):
                    k = a.slot(U)
                    at = a.row(sp, R)
                    if lag == 0:
                        held(sp, sp_passed, d_u_done, a.done(U))
                        held(sp, sp_passed, d_xc_done, a.done(U))
                        sp.dma_start(d_x[:, k], node_rows(x, at)).then_inc(d_loaded[k], 16)
                    if lag == 6:
                        held(sp, sp_passed, d_out_done, a.done())
                        if isinstance(at, int) and at > N - R:
                            held(sp, sp_passed, d_stored[a.slot(U, 1)], a.landed(1))
                        sp.dma_start(node_rows(out, at), d_out[:, a.slot(2)]).then_inc(d_stored[k], 16)
                walk(sp, GROUPS, d_step, [0, 6])
                nodes_stored(sp)

            @block.gpsimd
            def _(pool):
                pool.memset(ident[:], 0.0)
                pool.memset(upper[:], 1.0)
                pool.memset(head_of[:], float(D // HEADS) ** -0.5)
                pool.memset(head_to[:], 1.0)
                pool.memset(zeros[:], 0.0).then_inc(zeroed, 1)
                pool.iota(trash_i[:], pattern=[[P, T]], base=TRASH, channel_multiplier=1).then_inc(made, 1)
                pool.wait_ge(zeroed, 1)
                pool.affine_select(out=ident[:], in_=ident[:], compare_op=ALU.not_equal, fill=1.0, base=0,
                                   pattern=[[-1, P]], channel_multiplier=1).then_inc(made, 1)
                pool.affine_select(out=upper[:], in_=upper[:], compare_op=ALU.is_gt, fill=0.0, base=0,
                                   pattern=[[1, P]], channel_multiplier=-1).then_inc(made, 1)
                wide = D // HEADS
                pool.affine_select(out=head_of[:], in_=head_of[:], compare_op=ALU.is_ge, fill=0.0, base=0,
                                   pattern=[[-wide, HEADS]], channel_multiplier=1)
                pool.affine_select(out=head_to[:], in_=head_to[:], compare_op=ALU.is_ge, fill=0.0, base=0,
                                   pattern=[[1, P]], channel_multiplier=-wide).then_inc(made, 1)
                pool.wait_ge(made, 4)
                pool.affine_select(out=head_of[:], in_=head_of[:], compare_op=ALU.is_ge, fill=0.0, base=wide - 1,
                                   pattern=[[wide, HEADS]], channel_multiplier=-1)
                pool.affine_select(out=head_to[:], in_=head_to[:], compare_op=ALU.is_ge, fill=0.0, base=wide - 1,
                                   pattern=[[-1, P]], channel_multiplier=wide)
                pool.tensor_copy(trash[:], trash_i[:]).then_inc(made_too, 1)

                def f_step(a, lag):
                    k = a.slot(U)
                    held(pool, pool_passed, f_loaded[k], a.landed(0, 5))
                    held(pool, pool_passed, f_xn_done, a.done(2))
                    held(pool, pool_passed, f_xd_out[a.slot(U, 2)], a.landed(2))
                    for e in range(2):
                        for j in range(T):
                            gather(pool, f_x[:, a.slot(2), e * T + j], x, f_idx[:, k, e, j:j + 1], N - 1, f_got[k])
                walk(pool, EG, f_step, [0], parts=(1, 5))

                pool.wait_ge(c_dve, 5)

                def d_step(a, lag):
                    if lag == 0:
                        held(pool, pool_passed, d_out_done, a.done(U))
                        held(pool, pool_passed, d_loaded[a.slot(U)], a.landed())
                        pool.tensor_tensor(d_xc[:, a.slot(U)], d_x[:, a.slot(U)], c_b, ALU.add).then_inc(d_xc_done, 1)
                    if lag == 2:
                        held(pool, pool_passed, d_yn_done, a.done())
                        held(pool, pool_passed, d_xc_done, a.done())
                        held(pool, pool_passed, d_stored[a.slot(U, 2)], a.landed(2))
                        pool.tensor_tensor(d_out[:, a.slot(2)], d_yn[:, a.slot(2)], d_xc[:, a.slot(U)], ALU.add)\
                            .then_inc(d_out_done, 1)
                walk(pool, GROUPS, d_step, [0, 2])

            @block.vector
            def _(dve):
                dve.memset(eps_col[:], EPS)
                dve.memset(ones_col[:], 1.0)
                dve.memset(half_col[:], 0.5).then_inc(c_dve, 1)
                dve.wait_ge(consts_loaded, ALL_LOADED)
                dve.tensor_scalar(w1_g[:], w1_raw[:], g_col[:, 0:1], None, ALU.mult)
                dve.tensor_tensor(wb_he_col[:], wb_he[:, 0:1], wb_he[:, 1:2], ALU.add)
                dve.tensor_tensor(wb_row[:], wb_x[:], wb_d[:], ALU.subtract).then_inc(c_dve, 1)
                dve.wait_ge(c_act, 3)
                dve.scalar_tensor_tensor(ssp_b[:], b_o1_col[:], 0.0, ssp_ln[:], ALU.max, ALU.add).then_inc(c_dve, 1)
                dve.wait_ge(c_dve, 3)
                dve.tensor_copy(ssp_rep[:], ssp_b[:, 0:1].to_broadcast([P, P])).then_inc(c_dve, 1)
                dve.wait_ge(c_pe, 1)
                dve.tensor_copy(z_bias[:], bank[:, 0, 0:H2])
                dve.tensor_tensor(c_row[:], bank[:, 1, 0:D], b_o2_row[:], ALU.add).then_inc(c_dve, 1)

                def f_step(a, lag):
                    s, k = a.slot(2), a.slot(U)
                    if lag == 0:
                        dve.wait_ge(f_got[k], a.landed(0, 2 * T))
                        f_st.on_vector(dve, a, f_x[:, s])
                        f_st.wait_rstd(dve, a)
                        after(dve, f_tr_done, a.done(1))
                        for j in range(2 * T):
                            last = dve.tensor_scalar(f_xn[:, j], f_x[:, s, j], f_st.mean[:, s, j:j + 1],
                                                     f_st.rstd[:, s, j:j + 1], ALU.subtract, ALU.mult)
                        last.then_inc(f_xn_done, 1)
                    if lag == 1:
                        first = isinstance(a.rounds, int) and a.m == 0
                        dve.wait_ge(f_loaded[k], a.landed(0, 5))
                        after(dve, f_rlast_done, a.done(1))
                        dve.tensor_tensor(f_same[:], f_dst[:, k, 1:R + 1], f_dst[:, k, 0:R], ALU.is_equal)
                        dve.tensor_tensor(f_last[:], f_dst[:, k, 1:R + 1], f_dst[:, k, 2:R + 2], ALU.not_equal)\
                           .then_inc(f_flags_done, 1)
                        if first:
                            dve.memset(f_max[:, s, 0:1], -FAR).then_inc(f_carry_done, 1)
                        else:
                            dve.wait_ge(f_max_done, a.done(1))
                            dve.tensor_copy(f_max[:, s, 0:1], f_max[:, 1 - s, R:R + 1]).then_inc(f_carry_done, 1)
                        dve.wait_ge(f_flags_done, a.done())
                        dve.tensor_scalar(f_pen[:], f_same[:], 1.0, FAR, ALU.subtract, ALU.mult).then_inc(f_pen_done, 1)
                        dve.wait_ge(f_kv_done, a.done())
                        after(dve, f_l_done, a.done(1))
                        dve.tensor_tensor(f_prod[:], f_kT[:], bank[:, Q_], ALU.mult).then_inc(f_prod_done, 1)
                        dve.wait_ge(f_l_done, a.done())
                        dve.wait_ge(f_pen_done, a.done())
                        dve.wait_ge(f_carry_done, a.done())
                        dve.tensor_tensor_scan(f_max[:, s, 1:R + 1], f_pen[:], bank[0:HEADS, L_], f_max[:, s, 0:1], ALU.add,
                                               ALU.max).then_inc(f_max_done, 1)
                        dve.tensor_tensor(f_was[:, 0:1], f_max[:, s, 0:1], f_pen[:, 0:1], ALU.add)
                        dve.wait_ge(f_max_done, a.done())
                        dve.tensor_tensor(f_was[:, 1:R], f_max[:, s, 1:R], f_pen[:, 1:R], ALU.add).then_inc(f_was_done, 1)
                        after(dve, f_exps_done, a.done(1))
                        dve.tensor_tensor(f_arg[:, 1], bank[0:HEADS, L_], f_max[:, s, 1:R + 1], ALU.subtract)
                        dve.wait_ge(f_was_done, a.done())
                        dve.tensor_tensor(f_arg[:, 0], f_was[:], f_max[:, s, 1:R + 1], ALU.subtract).then_inc(f_args_done, 1)
                        dve.wait_ge(f_exps_done, a.done())
                        dve.tensor_tensor_scan(f_den[:, s], f_ae[:, 0], f_ae[:, 1], 0.0 if first else f_den[:, 1 - s, R - 1:R],
                                               ALU.mult, ALU.add).then_inc(f_den_done, 1)
                        dve.wait_ge(f_den_done, a.done())
                        dve.tensor_scalar(f_dene[:], f_den[:, s], 1e-16, None, ALU.add).then_inc(f_dene_done, 1)
                        dve.wait_ge(f_dene_done, a.done())
                        dve.reciprocal(f_rden[:], f_dene[:]).then_inc(f_rden_done, 1)
                        dve.wait_ge(f_rden_done, a.done())
                        after(dve, f_spread_done, a.done(1))
                        dve.tensor_tensor(f_rlast[:], f_rden[:], f_last[:], ALU.mult).then_inc(f_rlast_done, 1)
                    if lag == 2:
                        first = isinstance(a.rounds, int) and a.m == 0
                        dve.wait_ge(f_spread_done, a.done())
                        after(dve, f_sum_done, a.done(1))
                        dve.tensor_tensor(f_ev[:], f_vT[:, s], bank[:, E_], ALU.mult).then_inc(f_ev_done, 1)
                        dve.wait_ge(f_ev_done, a.done())
                        after(dve, f_q_done, a.done(2))
                        dve.tensor_tensor_scan(f_sum[:, s], bank[:, A_], f_ev[:], 0.0 if first else f_sum[:, 1 - s, R - 1:R],
                                               ALU.mult, ALU.add).then_inc(f_sum_done, 1)
                        dve.wait_ge(f_sum_done, a.done())
                        after(dve, f_q_out[a.slot(U, 2)], a.landed(2))
                        dve.tensor_tensor(f_q[:, s], f_sum[:, s], bank[:, K_R], ALU.mult).then_inc(f_q_done, 1)
                walk(dve, EG, f_step, [2, 0, 1], parts=(1, 5, 2 * T))

                def d_step(a, lag):
                    s = a.slot(2)
                    if lag == 0:
                        xs = d_x[:, a.slot(U)]
                        dve.wait_ge(d_loaded[a.slot(U)], a.landed())
                        d_xst.on_vector(dve, a, xs)
                        d_xst.wait_mean(dve, a)
                        after(dve, d_y_done, a.done(2))
                        for j in range(T):
                            last = dve.tensor_scalar(d_u[:, s, j], xs[:, j], d_xst.mean[:, s, j:j + 1], 0.0, ALU.subtract, ALU.max)
                        last.then_inc(d_u_done, 1)
                        dve.wait_ge(d_u_done, a.done())
                        d_ust.on_vector(dve, a, d_u[:, s])
                        for j in range(T):
                            last = dve.scalar_tensor_tensor(d_junk[:, j], d_u[:, s, j], 1.0, wb_row[:], ALU.mult, ALU.mult,
                                                            accum_out=d_dot[:, s, j:j + 1])
                        last.then_inc(d_dot_done, 1)
                        dve.wait_ge(d_dot_done, a.done())
                        d_xst.wait_rstd(dve, a)
                        dve.tensor_tensor(d_arg[:, s], d_dot[:, s], d_xst.rstd[:, s], ALU.mult).then_inc(d_arg_done, 1)
                        dve.wait_ge(d_ex_done, a.done())
                        dve.tensor_scalar(d_exp1[:, s], d_ex[:, s], 1.0, None, ALU.add).then_inc(d_exp1_done, 1)
                        dve.wait_ge(d_exp1_done, a.done())
                        dve.reciprocal(d_beta[:, s], d_exp1[:, s]).then_inc(d_beta_done, 1)
                        dve.wait_ge(d_beta_done, a.done())
                        dve.tensor_tensor(d_scale[:, s], d_beta[:, s], d_xst.rstd[:, s], ALU.mult).then_inc(d_scale_done, 1)
                        dve.wait_ge(d_scale_done, a.done())
                        dve.tensor_tensor(d_scale2[:, s], d_scale[:, s], d_scale[:, s], ALU.mult).then_inc(d_scale2_done, 1)
                        dve.wait_ge(d_scale2_done, a.done())
                        d_ust.wait_mean(dve, a)
                        dve.tensor_tensor(d_uvar[:, s], d_scale2[:, s], d_ust.var[:, s], ALU.mult).then_inc(d_uvar_done, 1)
                        d_ust.wait_rstd(dve, a)
                        dve.tensor_tensor(d_t[:, s], d_scale[:, s], d_ust.rstd[:, s], ALU.mult).then_inc(d_t_done, 1)
                        dve.wait_ge(d_t_done, a.done())
                        for j in range(T):
                            last = dve.tensor_scalar(d_un[:, s, j], d_u[:, s, j], d_ust.mean[:, s, j:j + 1], d_t[:, s, j:j + 1],
                                                     ALU.subtract, ALU.mult)
                        last.then_inc(d_un_done, 1)
                    if lag == 1:
                        dve.wait_ge(d_o_done, a.done())
                        for j in range(T):
                            last = dve.scalar_tensor_tensor(d_y[:, s, j], d_u[:, s, j], d_scale[:, s, j:j + 1],
                                                            tiles(D_O + s)[:, j], ALU.mult, ALU.add)
                        last.then_inc(d_y_done, 1)
                        dve.wait_ge(d_y_done, a.done())
                        d_yst.on_vector(dve, a, d_y[:, s])
                        d_yst.wait_rstd(dve, a)
                        dve.scalar_tensor_tensor(d_nm[:, s], d_yst.mean[:, s], -1.0, d_yst.rstd[:, s], ALU.mult, ALU.mult)\
                           .then_inc(d_nm_done, 1)
                walk(dve, GROUPS, d_step, [0, 1])

            @block.scalar
            def _(act):
                act.preload_act_table_set("natural_log_exp_and_others")
                act.wait_ge(consts_loaded, ALL_LOADED)
                act.wait_ge(c_dve, 1)
                act.activation(ssp_abs[:], b_o1_col[:], ACT.Abs).then_inc(c_act, 1)
                act.wait_ge(c_act, 1)
                act.activation(ssp_exp[:], ssp_abs[:], ACT.Exp, scale=-1.0).then_inc(c_act, 1)
                act.wait_ge(c_act, 2)
                act.activation(ssp_ln[:], ssp_exp[:], ACT.Ln, scale=0.5, bias=half_col[:, 0:1]).then_inc(c_act, 1)
                act.wait_ge(c_dve, 5)

                def f_step(a, lag):
                    s = a.slot(2)
                    if lag == 0:
                        f_st.wait_mean(act, a)
                        f_st.on_scalar(act, a)
                    if lag == 1:
                        act.wait_ge(f_tr_done, a.done())
                        act.activation(f_hT[:, 0], bank[:, TR_S], ACT.Relu)
                        act.activation(f_hT[:, 1], bank[:, TR_D], ACT.Relu).then_inc(f_h_done, 1)
                        act.wait_ge(f_kqv_done, a.done())
                        after(act, f_prod_done, a.done(1))
                        after(act, f_ev_done, a.done(2))
                        act.activation(f_kT[:], bank[:, K_R], ACT.Copy)
                        act.activation(f_vT[:, s], bank[:, V_], ACT.Copy).then_inc(f_kv_done, 1)
                        act.wait_ge(f_args_done, a.done())
                        after(act, f_spread_done, a.done(1))
                        act.activation(f_ae[:], f_arg[:], ACT.Exp).then_inc(f_exps_done, 1)
                walk(act, EG, f_step, [0, 1])

                def d_step(a, lag):
                    s = a.slot(2)
                    if lag == 0:
                        d_xst.wait_mean(act, a)
                        d_xst.on_scalar(act, a)
                        act.wait_ge(d_arg_done, a.done())
                        act.activation(d_ex[:, s], d_arg[:, s], ACT.Exp, scale=-1.0).then_inc(d_ex_done, 1)
                        act.wait_ge(d_uvar_done, a.done())
                        d_ust.on_scalar(act, a, d_uvar)
                        act.wait_ge(d_tr_done, a.done())
                        act.activation(d_unT[:], bank[:, D_TR], ACT.Copy).then_inc(d_unT_done, 1)
                        act.wait_ge(d_z_done, a.done())
                        after(act, d_o_done, a.done(1))
                        for h in range(H2):
                            last = act.activation(d_rz[:, h], bank[:, D_Z + h], ACT.Relu, bias=z_bias[:, h:h + 1])
                        last.then_inc(d_rz_done, 1)
                    if lag == 1:
                        d_yst.wait_mean(act, a)
                        d_yst.on_scalar(act, a)
                        act.wait_ge(d_nm_done, a.done())
                        after(act, d_out_done, a.done(2))
                        for j in range(T):
                            last = act.activation(d_yn[:, s, j], d_y[:, s, j], ACT.Identity, bias=d_nm[:, s, j:j + 1],
                                                  scale=d_yst.rstd[:, s, j:j + 1])
                        last.then_inc(d_yn_done, 1)
                walk(act, GROUPS, d_step, [0, 1])

            @block.tensor
            def _(pe):
                pe.wait_ge(consts_loaded, ALL_LOADED)
                pe.wait_ge(c_dve, 4)
                pe.wait_ge(made_too, 1)
                for h in range(H2):
                    pe.matmul(bank[:, 0, h:h + 1], w1_raw[:, h * P:(h + 1) * P], b_col[:], start=True, stop=True)
                pe.matmul(bank[:, 1, 0:D], ssp_rep[:], w_o2_sb[:], start=True, stop=True).then_inc(c_pe, 1)
                pe.wait_ge(c_dve, 5)

                def f_step(a, lag):
                    s, k = a.slot(2), a.slot(U)
                    if lag == 2:
                        pe.wait_ge(f_rlast_done, a.done())
                        after(pe, f_q_done, a.done(1))
                        pe.matmul(bank[:, A_], head_to[:], f_ae[:, 0], start=True, stop=True)
                        pe.matmul(bank[:, E_], head_to[:], f_ae[:, 1], start=True, stop=True)
                        pe.matmul(bank[:, K_R], head_to[:], f_rlast[:], start=True, stop=True).then_inc(f_spread_done, 1)
                    if lag == 1:
                        pe.wait_ge(f_xn_done, a.done())
                        after(pe, f_h_done, a.done(1))
                        for j in range(T):
                            pe.transpose(bank[:, TR_S, j * P:(j + 1) * P], f_xn[:, j], ident[:])
                        for j in range(T):
                            last = pe.transpose(bank[:, TR_D, j * P:(j + 1) * P], f_xn[:, T + j], ident[:])
                        last.then_inc(f_tr_done, 1)
                        pe.wait_ge(f_loaded[k], a.landed(0, 5))
                        after(pe, f_kv_done, a.done(1))
                        pe.matmul(bank[:, V_], wv_sb[:], f_attr[:, k], start=True, stop=True)
                        pe.wait_ge(f_h_done, a.done())
                        after(pe, f_prod_done, a.done(1))
                        pe.matmul(bank[:, Q_], wq_sb[:], f_hT[:, 1], start=True, stop=True)
                        after(pe, f_q_done, a.done(1))
                        pe.matmul(bank[:, K_R], wk_sb[:], f_hT[:, 0], start=True, stop=True).then_inc(f_kqv_done, 1)
                        pe.wait_ge(f_prod_done, a.done())
                        after(pe, f_args_done, a.done(1))
                        pe.matmul(bank[0:HEADS, L_], head_of[:], f_prod[:], start=True, stop=False)
                        pe.matmul(bank[0:HEADS, L_], wdis_sb[:], f_w[:, k], start=False, stop=True).then_inc(f_l_done, 1)
                walk(pe, EG, f_step, [2, 1], parts=(1, 5))
                pe.wait_ge(f_q_done, EG)

                def d_step(a, lag):
                    s = a.slot(2)
                    pe.wait_ge(d_un_done, a.done())
                    after(pe, d_unT_done, a.done(1))
                    for j in range(T):
                        last = pe.transpose(bank[:, D_TR, j * P:(j + 1) * P], d_un[:, s, j], ident[:])
                    last.then_inc(d_tr_done, 1)
                    pe.wait_ge(d_unT_done, a.done())
                    after(pe, d_rz_done, a.done(1))
                    for h in range(H2):
                        last = pe.matmul(bank[:, D_Z + h], w1_g[:, h * P:(h + 1) * P], d_unT[:], start=True, stop=True)
                    last.then_inc(d_z_done, 1)
                    pe.wait_ge(d_rz_done, a.done())
                    after(pe, d_y_done, a.done(2))
                    for j in range(T):
                        for h in range(H2):
                            last = pe.matmul(tiles(D_O + s)[:, j], d_rz[:, h, j * P:(j + 1) * P], w2_sb[:, h],
                                             start=(h == 0), stop=(h == H2 - 1))
                    last.then_inc(d_o_done, 1)
                walk(pe, GROUPS, d_step, [0])



        nc.clear_and_free_semaphores(signals)
        nc.all_engine_barrier()
        signals.clear()
        taken[0] = 0
        sp_passed, pool_passed, pe_passed = sems("sp_passed_too", "pool_passed_too", "pe_passed_too")

        b_q = fsb("b_q", [P, U, R])
        b_x = fsb("b_x", [P, U, T, D])
        b_dst = fsb("b_dst", [P, U, R + 1], I32)
        b_src = fsb("b_src", [P, U, R], I32)
        b_idx = fsb("b_idx", [P, U, 3, T], I32)
        b_more = fsb("b_more", [P, T])
        b_out_idx = fsb("b_out_idx", [P, U, T], I32)
        b_wc = fsb("b_wc", [P, U, T])
        b_f = fsb("b_f", [FW, U, R])
        b_next = fsb("b_next", [P, R])
        b_g = fsb("b_g", [P, 2, R])
        b_u = fsb("b_u", [P, T, D])
        b_a = fsb("b_a", [P, T, D])
        b_w = fsb("b_w", [P, 2, T, D])
        b_un = fsb("b_un", [P, T, D])
        b_unT = fsb("b_unT", [P, R])
        b_rz = fsb("b_rz", [P, H2, R])
        b_y = fsb("b_y", [P, T, D])
        b_yn = fsb("b_yn", [P, T, D])
        b_x1 = fsb("b_x1", [P, T, D])
        b_out = fsb("b_out", [P, 2, T, D])
        b_u1 = fsb("b_u1", [P, T, D])
        b_u1T = fsb("b_u1T", [P, R])
        b_junk = fsb("b_junk", [P, T, D])
        b_abs = fsb("b_abs", [FF, R])
        b_exp = fsb("b_exp", [FF, R])
        b_ln = fsb("b_ln", [FF, R])
        b_pos = fsb("b_pos", [FF, R])
        b_ssp = fsb("b_ssp", [FF + 1, R])
        b_hh = fsb("b_hh", [P, T, FF])
        b_xij = fsb("b_xij", [P, T, FF])
        b_eq = fsb("b_eq", [P, T, R])
        b_tri = fsb("b_tri", [P, T, P])
        b_tot = fsb("b_tot", [P, 2, T, FF])
        b_srcf = fsb("b_srcf", [P, T])
        b_agg_idx = fsb("b_agg_idx", [P, U, T], I32)
        (b_dot, b_arg0, b_arg, b_ex, b_exp1, b_beta, b_nbeta, b_scale, b_nm, b_flag, b_away, b_jump) = (
            fsb("b_" + n, [P, T]) for n in "dot arg0 arg ex exp1 beta nbeta scale nm flag away jump".split())
        b_xst, b_wst, b_yst, b_zst = (Stats(n, T, fsb) for n in ("b_xst", "b_wst", "b_yst", "b_zst"))
        b_loaded, b_put, b_added, b_lead_out = ring("b_loaded"), ring("b_put"), ring("b_added"), ring("b_lead_out")
        (b_next_done, b_g_done, b_tr_done, b_u_done, b_dot_done, b_arg0_done, b_arg_done, b_ex_done, b_exp1_done,
         b_beta_done, b_nbeta_done, b_a_done, b_w_done, b_un_done, b_utr_done, b_unT_done, b_z_done,
         b_rz_done, b_o_done, b_y_done, b_nm_done, b_yn_done, b_x1_done, b_out_done, b_u1_done, b_u1tr_done, b_u1T_done,
         b_hh_done, b_fl_done, b_abs_done, b_exp_done, b_ln_done, b_pos_done, b_ssp_done, b_w2_done, b_hb_done,
         b_xij_done, b_srcf_done, b_eq_done, b_tri_done, b_tot_done, b_totc_done, b_away_done,
         b_jump_done, b_idx_done, b_more_done, b_out_idx_done) = named("b", (
             "next_done g_done tr_done u_done dot_done arg0_done arg_done ex_done exp1_done beta_done nbeta_done "
             "a_done w_done un_done utr_done unT_done z_done rz_done o_done y_done nm_done yn_done x1_done "
             "out_done u1_done u1tr_done u1T_done hh_done fl_done abs_done exp_done ln_done pos_done ssp_done w2_done "
             "hb_done xij_done srcf_done eq_done tri_done tot_done totc_done away_done jump_done idx_done more_done out_idx_done"))
        B_HE, B_TR, B_Z, B_O, B_F, B_W, B_T = 0, 1, 2, 4, 5, 6, 7
        CNT, GATE = T * FF, T * FF + T

        c_idx = fsb("c_idx", [P, U, T], I32)
        c_y = fsb("c_y", [P, U, T, D])
        c_idx2 = fsb("c_idx2", [P, U, T], I32)
        c_lead = fsb("c_lead", [P, U, T], I32)
        c_agg = fsb("c_agg", [P, U, T, FF])
        c_y2 = fsb("c_y2", [P, U, T, D])
        c_aT = fsb("c_aT", [FF, R])
        c_abs = fsb("c_abs", [P, R])
        c_exp = fsb("c_exp", [P, R])
        c_ln = fsb("c_ln", [P, R])
        c_pos = fsb("c_pos", [P, R])
        c_ssp = fsb("c_ssp", [P, R])
        c_res = fsb("c_res", [P, 2, T, D])
        c_ready, c_got, c_spilled = ring("c_ready"), ring("c_got"), ring("c_spilled")
        c_ready2, c_got2, c_stored = ring("c_ready2"), ring("c_got2"), ring("c_stored")
        (c_tr_done, c_aT_done, c_z_done, c_abs_done, c_exp_done, c_ln_done, c_pos_done, c_ssp_done, c_o_done,
         c_res_done) = named("c", "tr_done aT_done z_done abs_done exp_done ln_done pos_done ssp_done o_done res_done")
        C_TR, C_Z, C_O = 0, 1, 2

        with nc.Block() as block:
            @block.sync
            def _(sp):

                def b_step(a, lag):
                    k = a.slot(U)
                    at_p, at_r = a.row_back(sp, EG, P), a.row_back(sp, EG, R)
                    held(sp, sp_passed, b_idx_done, a.done(U))
                    held(sp, sp_passed, b_put[k], a.landed(U, T))
                    sp.dma_start(b_q[:, k], q_dram[:, bass.ds(at_r, R)]).then_inc(b_loaded[k], 16)
                    sp.dma_start(b_x[:, k], spill(xd_dram, at_p)).then_inc(b_loaded[k], 16)
                    sp.dma_start(b_dst[:, k], dst_row[:, bass.ds(at_r + 1, R + 1)].partition_broadcast(P)).then_inc(b_loaded[k], 16)
                    sp.dma_start(b_src[:, k], src_row[:, bass.ds(at_r, R)].partition_broadcast(P)).then_inc(b_loaded[k], 16)
                    sp.dma_start(b_idx[:, k, 0], col_of(src_col, at_p)).then_inc(b_loaded[k], 16)
                    sp.dma_start(b_idx[:, k, 1], col_of(dst_col, at_p)).then_inc(b_loaded[k], 16)
                    sp.dma_start(b_idx[:, k, 2], col_of(next_col, at_p)).then_inc(b_loaded[k], 16)
                    sp.dma_start(b_wc[:, k], col_of(w_col, at_p)).then_inc(b_loaded[k], 16)
                    sp.dma_start(b_f[:, k], fT[:, bass.ds(at_r, R)]).then_inc(b_loaded[k], 16)

                def lead_step(a, lag):
                    at_p = a.row_back(sp, EG, P)
                    held(sp, sp_passed, b_idx_done, a.done())
                    sp.dma_start(col_of(lead_dram, at_p), b_agg_idx[:, a.slot(U)]).then_inc(b_lead_out[a.slot(U)], 16)

                def b_both(a, lag):
                    if lag == 0:
                        b_step(a, lag)
                    else:
                        lead_step(a, lag)
                walk(sp, EG, b_both, [0, 4], parts=(1, T))
                all_of(sp, b_lead_out, EG)

                def c1_step(a, lag):
                    k = a.slot(U)
                    at_p = a.row(sp, P)
                    if lag == 0:
                        held(sp, sp_passed, c_got[k], a.landed(U, T))
                        sp.dma_start(c_idx[:, k], col_of(src_col, at_p)).then_inc(c_ready[k], 16)
                    if lag == 3:
                        held(sp, sp_passed, c_got[k], a.landed(0, T))
                        sp.dma_start(spill(y_dram, at_p), c_y[:, k]).then_inc(c_spilled[k], 16)
                walk(sp, EG, c1_step, [0, 3], parts=(1, T))
                all_of(sp, c_spilled, EG)

                def c2_step(a, lag):
                    k = a.slot(U)
                    at_p = a.row(sp, P)
                    held(sp, sp_passed, c_stored[k], a.landed(U, T))
                    sp.dma_start(c_idx2[:, k], col_of(src_col, at_p)).then_inc(c_ready2[k], 16)
                    sp.dma_start(c_y2[:, k], spill(y_dram, at_p)).then_inc(c_ready2[k], 16)
                    sp.dma_start(c_lead[:, k], col_of(lead_dram, at_p)).then_inc(c_ready2[k], 16)
                walk(sp, EG, c2_step, [0], parts=(1, T))
                all_of(sp, c_stored, EG, T)

            @block.gpsimd
            def _(pool):

                def b_step(a, lag):
                    k = a.slot(U)
                    s = a.slot(2)
                    held(pool, pool_passed, b_x1_done, a.done())
                    held(pool, pool_passed, b_put[a.slot(U, 2)], a.landed(2, T))
                    pool.tensor_tensor(b_out[:, s], b_x1[:], c_b, ALU.add).then_inc(b_out_done, 1)
                    held(pool, pool_passed, b_out_done, a.done())
                    held(pool, pool_passed, b_out_idx_done, a.done())
                    for j in range(T):
                        scatter(pool, out, b_out_idx[:, k, j:j + 1], b_out[:, s, j], N - 1, b_put[k])
                    held(pool, pool_passed, b_idx_done, a.done())
                    held(pool, pool_passed, b_totc_done, a.done())
                    held(pool, pool_passed, b_added[a.slot(U, 1)], a.landed(1, T))
                    for j in range(T):
                        pool.indirect_dma_start(agg, bass.IndirectOffsetOnAxis(ap=b_agg_idx[:, k, j:j + 1], axis=0),
                                                b_tot[:, s, j], None, bounds_check=AGG_ROWS - 1, oob_is_err=True,
                                                compute_op=ALU.add).then_inc(b_added[k], 16)
                walk(pool, EG, b_step, [0], parts=(1, T))
                all_of(pool, b_put, EG, T)
                all_of(pool, b_added, EG, T)

                def c1_step(a, lag):
                    k = a.slot(U)
                    held(pool, pool_passed, c_ready[k], a.landed())
                    held(pool, pool_passed, c_spilled[k], a.landed(U))
                    for j in range(T):
                        gather(pool, c_y[:, k, j], out, c_idx[:, k, j:j + 1], N - 1, c_got[k])
                walk(pool, EG, c1_step, [0])
                all_of(pool, c_got, EG, T)

                def c2_step(a, lag):
                    k = a.slot(U)
                    if lag == 0:
                        held(pool, pool_passed, c_ready2[k], a.landed(0, 3))
                        held(pool, pool_passed, c_tr_done, a.done(U))
                        for j in range(T):
                            gather(pool, c_agg[:, k, j], agg, c_idx2[:, k, j:j + 1], N - 1, c_got2[k])
                    if lag == 2:
                        held(pool, pool_passed, c_res_done, a.done())
                        held(pool, pool_passed, c_stored[a.slot(U, 1)], a.landed(1, T))
                        for j in range(T):
                            scatter(pool, out, c_lead[:, k, j:j + 1], c_res[:, a.slot(2), j], N - 1, c_stored[k])
                walk(pool, EG, c2_step, [0, 2], parts=(1, 3, T))

            @block.vector
            def _(dve):
                dve.memset(b_ssp[FF:FF + 1, :], 1.0)

                def b_step(a, lag):
                    s, k = a.slot(2), a.slot(U)
                    first = isinstance(a.rounds, int) and a.m == 0
                    xs = b_x[:, k]
                    if lag == 0:
                        dve.wait_ge(b_loaded[k], a.landed(0, 9))
                        after(dve, b_g_done, a.done(1))
                        dve.tensor_tensor(b_next[:], b_dst[:, k, 0:R], b_dst[:, k, 1:R + 1], ALU.is_equal).then_inc(b_next_done, 1)
                        dve.wait_ge(b_next_done, a.done())
                        after(dve, b_tr_done, a.done(2))
                        dve.tensor_tensor_scan(b_g[:, s, ::-1], b_next[:, ::-1], b_q[:, k, ::-1],
                                               0.0 if first else b_g[:, 1 - s, 0:1], ALU.mult, ALU.add).then_inc(b_g_done, 1)
                        b_xst.on_vector(dve, a, xs)
                        b_xst.wait_rstd(dve, a)
                        after(dve, b_w_done, a.done(1))
                        for j in range(T):
                            last = dve.tensor_scalar(b_u[:, j], xs[:, j], b_xst.mean[:, s, j:j + 1], 0.0, ALU.subtract, ALU.max)
                        last.then_inc(b_u_done, 1)
                        dve.wait_ge(b_u_done, a.done())
                        for j in range(T):
                            last = dve.scalar_tensor_tensor(b_junk[:, j], b_u[:, j], 1.0, wb_row[:], ALU.mult, ALU.mult,
                                                            accum_out=b_dot[:, j:j + 1])
                        last.then_inc(b_dot_done, 1)
                        dve.wait_ge(b_dot_done, a.done())
                        dve.tensor_tensor(b_arg0[:], b_dot[:], b_xst.rstd[:, s], ALU.mult).then_inc(b_arg0_done, 1)
                        dve.wait_ge(b_arg0_done, a.done())
                        dve.wait_ge(b_tr_done, a.done())
                        dve.tensor_tensor(b_arg[:], b_arg0[:], bank[:, B_T, GATE:GATE + T], ALU.add).then_inc(b_arg_done, 1)
                        dve.wait_ge(b_ex_done, a.done())
                        dve.tensor_scalar(b_exp1[:], b_ex[:], 1.0, None, ALU.add).then_inc(b_exp1_done, 1)
                        dve.wait_ge(b_exp1_done, a.done())
                        dve.reciprocal(b_beta[:], b_exp1[:]).then_inc(b_beta_done, 1)
                        dve.wait_ge(b_beta_done, a.done())
                        dve.tensor_tensor(b_scale[:], b_beta[:], b_xst.rstd[:, s], ALU.mult)
                        dve.tensor_scalar(b_nbeta[:], b_beta[:], -1.0, 1.0, ALU.mult, ALU.add).then_inc(b_nbeta_done, 1)
                        dve.wait_ge(b_nbeta_done, a.done())
                        for j in range(T):
                            last = dve.tensor_scalar(b_a[:, j], tiles(B_HE)[:, j], b_nbeta[:, j:j + 1], None, ALU.mult)
                        last.then_inc(b_a_done, 1)
                        dve.wait_ge(b_a_done, a.done())
                        after(dve, b_y_done, a.done(2))
                        for j in range(T):
                            last = dve.scalar_tensor_tensor(b_w[:, s, j], b_u[:, j], b_scale[:, j:j + 1], b_a[:, j],
                                                            ALU.mult, ALU.add)
                        last.then_inc(b_w_done, 1)
                        dve.wait_ge(b_w_done, a.done())
                        b_wst.on_vector(dve, a, b_w[:, s])
                        b_wst.wait_rstd(dve, a)
                        after(dve, b_utr_done, a.done(1))
                        for j in range(T):
                            last = dve.tensor_scalar(b_un[:, j], b_w[:, s, j], b_wst.mean[:, s, j:j + 1],
                                                     b_wst.rstd[:, s, j:j + 1], ALU.subtract, ALU.mult)
                        last.then_inc(b_un_done, 1)
                    if lag == 1:
                        dve.wait_ge(b_o_done, a.done())
                        after(dve, b_yn_done, a.done(1))
                        dve.tensor_tensor(b_y[:], b_w[:, s], tiles(B_O), ALU.add).then_inc(b_y_done, 1)
                        dve.wait_ge(b_y_done, a.done())
                        b_yst.on_vector(dve, a, b_y)
                        dve.wait_ge(b_loaded[k], a.landed(0, 9))
                        dve.tensor_copy(b_srcf[:], b_idx[:, k, 0]).then_inc(b_srcf_done, 1)
                        dve.tensor_tensor(b_more[:], b_idx[:, k, 1], b_idx[:, k, 2], ALU.is_equal).then_inc(b_more_done, 1)
                        dve.wait_ge(b_more_done, a.done())
                        after(dve, b_put[k], a.landed(U, T))
                        dve.scalar_tensor_tensor(b_out_idx[:, k], b_more[:], float(N + 1), b_idx[:, k, 1], ALU.mult, ALU.add)\
                           .then_inc(b_out_idx_done, 1)
                        dve.wait_ge(b_srcf_done, a.done())
                        after(dve, b_tot_done, a.done(1))
                        for j in range(T):
                            last = dve.tensor_scalar(b_eq[:, j], b_src[:, k], b_srcf[:, j:j + 1], None, ALU.is_equal)
                        last.then_inc(b_eq_done, 1)
                        dve.wait_ge(b_eq_done, a.done())
                        for j in range(T):
                            last = dve.tensor_tensor(b_tri[:, j], b_eq[:, j, j * P:(j + 1) * P], upper[:], ALU.mult)
                        last.then_inc(b_tri_done, 1)
                        dve.wait_ge(b_ln_done, a.done())
                        after(dve, b_w2_done, a.done(1))
                        dve.tensor_tensor(b_ssp[0:FF, :], b_pos[:], b_ln[:], ALU.add).then_inc(b_ssp_done, 1)
                        b_yst.wait_rstd(dve, a)
                        dve.scalar_tensor_tensor(b_nm[:], b_yst.mean[:, s], -1.0, b_yst.rstd[:, s], ALU.mult, ALU.mult)\
                           .then_inc(b_nm_done, 1)
                        dve.wait_ge(b_yn_done, a.done())
                        after(dve, b_out_done, a.done(1))
                        dve.tensor_tensor(b_x1[:], b_yn[:], xs, ALU.add).then_inc(b_x1_done, 1)
                        dve.wait_ge(b_x1_done, a.done())
                        b_zst.on_vector(dve, a, b_x1)
                        b_zst.wait_mean(dve, a)
                        after(dve, b_u1tr_done, a.done(1))
                        for j in range(T):
                            last = dve.tensor_scalar(b_u1[:, j], b_x1[:, j], b_zst.mean[:, s, j:j + 1], 0.0, ALU.subtract, ALU.max)
                        last.then_inc(b_u1_done, 1)
                        dve.wait_ge(b_hh_done, a.done())
                        b_zst.wait_rstd(dve, a)
                        for j in range(T):
                            last = dve.scalar_tensor_tensor(b_hh[:, j], bank[:, B_W, j * FF:(j + 1) * FF],
                                                            b_zst.rstd[:, s, j:j + 1], b_in_row[:], ALU.mult, ALU.add)
                        last.then_inc(b_hb_done, 1)
                        dve.wait_ge(b_hb_done, a.done())
                        for j in range(T):
                            last = dve.scalar_tensor_tensor(b_xij[:, j], bank[:, B_W, (T + j) * FF:(T + j + 1) * FF],
                                                            b_wc[:, k, j:j + 1], b_hh[:, j], ALU.mult, ALU.mult)
                        last.then_inc(b_xij_done, 1)
                        dve.wait_ge(b_totc_done, a.done())
                        dve.tensor_scalar(b_flag[:], bank[:, B_T, CNT:CNT + T], 1.0, None, ALU.min)
                        dve.tensor_tensor(b_away[:], trash[:], b_srcf[:], ALU.subtract).then_inc(b_away_done, 1)
                        dve.wait_ge(b_away_done, a.done())
                        dve.tensor_tensor(b_jump[:], b_flag[:], b_away[:], ALU.mult).then_inc(b_jump_done, 1)
                        dve.wait_ge(b_jump_done, a.done())
                        after(dve, b_added[k], a.landed(U, T))
                        after(dve, b_lead_out[k], a.landed(U))
                        dve.tensor_tensor(b_agg_idx[:, k], b_srcf[:], b_jump[:], ALU.add).then_inc(b_idx_done, 1)
                walk(dve, EG, b_step, [0, 1], parts=(1, T, 9))
                edges_over(dve)

                def c_step(a, lag):
                    k, s = a.slot(U), a.slot(2)
                    dve.wait_ge(c_ln_done, a.done())
                    after(dve, c_o_done, a.done(1))
                    dve.scalar_tensor_tensor(c_ssp[:], c_ln[:], ssp_b[:, 0:1], c_pos[:], ALU.subtract, ALU.add).then_inc(c_ssp_done, 1)
                    dve.wait_ge(c_o_done, a.done())
                    dve.wait_ge(c_ready2[k], a.landed(0, 3))
                    after(dve, c_stored[a.slot(U, 2)], a.landed(2, T))
                    dve.tensor_tensor(c_res[:, s], c_y2[:, k], tiles(C_O), ALU.add).then_inc(c_res_done, 1)
                walk(dve, EG, c_step, [0], parts=(1, 3, T))

            @block.scalar
            def _(act):

                def b_step(a, lag):
                    s = a.slot(2)
                    if lag == 0:
                        b_xst.wait_mean(act, a)
                        b_xst.on_scalar(act, a)
                        act.wait_ge(b_arg_done, a.done())
                        act.activation(b_ex[:], b_arg[:], ACT.Exp, scale=-1.0).then_inc(b_ex_done, 1)
                        b_wst.wait_mean(act, a)
                        b_wst.on_scalar(act, a)
                        act.wait_ge(b_utr_done, a.done())
                        act.activation(b_unT[:], bank[:, B_TR], ACT.Copy).then_inc(b_unT_done, 1)
                        act.wait_ge(b_z_done, a.done())
                        after(act, b_o_done, a.done(1))
                        for h in range(H2):
                            last = act.activation(b_rz[:, h], bank[:, B_Z + h], ACT.Relu, bias=z_bias[:, h:h + 1])
                        last.then_inc(b_rz_done, 1)
                    if lag == 1:
                        act.wait_ge(b_fl_done, a.done())
                        act.activation(b_abs[:], bank[0:FF, B_F], ACT.Abs, bias=bf1_col[:, 0:1]).then_inc(b_abs_done, 1)
                        after(act, b_ssp_done, a.done(1))
                        act.activation(b_pos[:], bank[0:FF, B_F], ACT.Relu, bias=bf1_col[:, 0:1]).then_inc(b_pos_done, 1)
                        act.wait_ge(b_abs_done, a.done())
                        act.activation(b_exp[:], b_abs[:], ACT.Exp, scale=-1.0).then_inc(b_exp_done, 1)
                        act.wait_ge(b_exp_done, a.done())
                        act.activation(b_ln[:], b_exp[:], ACT.Ln, scale=0.5, bias=half_col[0:FF, 0:1]).then_inc(b_ln_done, 1)
                        b_yst.wait_mean(act, a)
                        b_yst.on_scalar(act, a)
                        act.wait_ge(b_nm_done, a.done())
                        after(act, b_x1_done, a.done(1))
                        for j in range(T):
                            last = act.activation(b_yn[:, j], b_y[:, j], ACT.Identity, bias=b_nm[:, j:j + 1],
                                                  scale=b_yst.rstd[:, s, j:j + 1])
                        last.then_inc(b_yn_done, 1)
                        b_zst.wait_mean(act, a)
                        b_zst.on_scalar(act, a)
                        act.wait_ge(b_u1tr_done, a.done())
                        act.activation(b_u1T[:], bank[:, B_HE], ACT.Copy).then_inc(b_u1T_done, 1)
                        act.wait_ge(b_tot_done, a.done())
                        after(act, b_added[a.slot(U, 2)], a.landed(2, T))
                        act.activation(b_tot[:, s], bank[:, B_T, 0:T * FF].rearrange("p (j f) -> p j f", j=T), ACT.Copy)\
                           .then_inc(b_totc_done, 1)
                walk(act, EG, b_step, [0, 1], parts=(1, T))
                edges_over(act)

                def c_step(a, lag):
                    act.wait_ge(c_tr_done, a.done())
                    act.activation(c_aT[:], bank[0:FF, C_TR], ACT.Copy).then_inc(c_aT_done, 1)
                    act.wait_ge(c_z_done, a.done())
                    act.activation(c_abs[:], bank[:, C_Z], ACT.Abs, bias=b_o1_col[:, 0:1]).then_inc(c_abs_done, 1)
                    after(act, c_ssp_done, a.done(1))
                    act.activation(c_pos[:], bank[:, C_Z], ACT.Relu, bias=b_o1_col[:, 0:1]).then_inc(c_pos_done, 1)
                    act.wait_ge(c_abs_done, a.done())
                    act.activation(c_exp[:], c_abs[:], ACT.Exp, scale=-1.0).then_inc(c_exp_done, 1)
                    act.wait_ge(c_exp_done, a.done())
                    act.activation(c_ln[:], c_exp[:], ACT.Ln, scale=0.5, bias=half_col[:, 0:1]).then_inc(c_ln_done, 1)
                walk(act, EG, c_step, [0])

            @block.tensor
            def _(pe):

                def b_step(a, lag):
                    s, k = a.slot(2), a.slot(U)
                    if lag == 0:
                        pe.wait_ge(b_g_done, a.done())
                        after(pe, b_u1T_done, a.done(2))
                        after(pe, b_a_done, a.done(1))
                        for j in range(T):
                            pe.transpose(tiles(B_HE)[:, j], b_g[:, s, j * P:(j + 1) * P], ident[:])
                        after(pe, b_idx_done, a.done(2))
                        after(pe, b_totc_done, a.done(2))
                        for j in range(T):
                            last = pe.matmul(bank[:, B_T, GATE + j:GATE + j + 1], b_g[:, s, j * P:(j + 1) * P], wb_he_col[:],
                                             start=True, stop=True)
                        last.then_inc(b_tr_done, 1)
                        pe.wait_ge(b_un_done, a.done())
                        for j in range(T):
                            last = pe.transpose(tiles(B_TR)[:, j], b_un[:, j], ident[:])
                        last.then_inc(b_utr_done, 1)
                        pe.wait_ge(b_unT_done, a.done())
                        for h in range(H2):
                            last = pe.matmul(bank[:, B_Z + h], w1_g[:, h * P:(h + 1) * P], b_unT[:], start=True, stop=True)
                        last.then_inc(b_z_done, 1)
                        pe.wait_ge(b_rz_done, a.done())
                        after(pe, b_y_done, a.done(1))
                        for j in range(T):
                            for h in range(H2):
                                last = pe.matmul(tiles(B_O)[:, j], b_rz[:, h, j * P:(j + 1) * P], w2_sb[:, h],
                                                 start=(h == 0), stop=(h == H2 - 1))
                        last.then_inc(b_o_done, 1)
                    if lag == 1:
                        pe.wait_ge(b_loaded[k], a.landed(0, 9))
                        after(pe, b_abs_done, a.done(1))
                        after(pe, b_pos_done, a.done(1))
                        pe.matmul(bank[0:FF, B_F], wf1_sb[:], b_f[:, k], start=True, stop=True).then_inc(b_fl_done, 1)
                        pe.wait_ge(b_ssp_done, a.done())
                        after(pe, b_xij_done, a.done(1))
                        for j in range(T):
                            last = pe.matmul(bank[:, B_W, (T + j) * FF:(T + j + 1) * FF], b_ssp[:, j * P:(j + 1) * P], wf2_sb[:],
                                             start=True, stop=True)
                        last.then_inc(b_w2_done, 1)
                        pe.wait_ge(b_u1_done, a.done())
                        for j in range(T):
                            last = pe.transpose(tiles(B_HE)[:, j], b_u1[:, j], ident[:])
                        last.then_inc(b_u1tr_done, 1)
                        pe.wait_ge(b_u1T_done, a.done())
                        for j in range(T):
                            last = pe.matmul(bank[:, B_W, j * FF:(j + 1) * FF], b_u1T[:, j * P:(j + 1) * P], w_in_sb[:],
                                             start=True, stop=True)
                        last.then_inc(b_hh_done, 1)
                        pe.wait_ge(b_xij_done, a.done())
                        pe.wait_ge(b_tri_done, a.done())
                        for i in range(T):
                            here = slice(i * P, (i + 1) * P)
                            for j in range(T):
                                pe.matmul(bank[:, B_T, i * FF:(i + 1) * FF], b_eq[:, j, here], b_xij[:, j],
                                          start=(j == 0), stop=(j == T - 1))
                            for j in range(i + 1):
                                last = pe.matmul(bank[:, B_T, CNT + i:CNT + i + 1], b_tri[:, i] if j == i else b_eq[:, j, here],
                                                 ones_col[:], start=(j == 0), stop=(j == i))
                        last.then_inc(b_tot_done, 1)
                walk(pe, EG, b_step, [0, 1], parts=(1, 9))
                edges_over(pe)

                def c_step(a, lag):
                    k = a.slot(U)
                    held(pe, pe_passed, c_got2[k], a.landed(0, T))
                    held(pe, pe_passed, c_aT_done, a.done(1))
                    for j in range(T):
                        last = pe.transpose(bank[0:FF, C_TR, j * P:(j + 1) * P], c_agg[:, k, j], ident[:])
                    last.then_inc(c_tr_done, 1)
                    pe.wait_ge(c_aT_done, a.done())
                    after(pe, c_abs_done, a.done(1))
                    after(pe, c_pos_done, a.done(1))
                    pe.matmul(bank[:, C_Z], wo1_sb[:], c_aT[:], start=True, stop=True).then_inc(c_z_done, 1)
                    pe.wait_ge(c_ssp_done, a.done())
                    after(pe, c_res_done, a.done(1))
                    for j in range(T):
                        last = pe.matmul(tiles(C_O)[:, j], c_ssp[:, j * P:(j + 1) * P], w_o2_sb[:], start=True, stop=True)
                    last.then_inc(c_o_done, 1)
                walk(pe, EG, c_step, [0], parts=(1, T))



_WEIGHTS = ['Wk', 'Wq', 'Wv', 'W_dis', 'W_beta', 'ln1_g', 'ln1_b', 'W_ff1', 'W_ff2']
_WEIGHTS_1 = ['w_in', 'b_in', 'w_f1', 'b_f1', 'w_f2', 'b_f2', 'w_o1', 'b_o1', 'w_o2', 'b_o2']


def kernel(**inputs):
    import numpy as _np
    import concourse.bacc as _bacc
    from concourse import mybir as _mybir
    from concourse.bass_utils import run_bass_kernel_spmd as _run

    given = {k: _np.asarray(v) for k, v in inputs.items()}
    n, e = given['x'].shape[0], given['src'].shape[0]
    groups = -(-e // R)
    slots = groups * R

    def filled(v, fill):
        full = _np.full((slots,) + v.shape[1:], fill, v.dtype)
        full[:e] = v
        return full

    def by_partition(v):
        return v.reshape(groups, T, P).transpose(0, 2, 1).reshape(groups * P, T)

    src, dst, weight = filled(given['src'], n), filled(given['dst'], n), filled(given['edge_weight'], 0)
    edges = _np.full((1, slots + 2), n + 1, dst.dtype)
    edges[0, 0] = -1
    edges[0, 1:-1] = dst
    laid = {
        'x': given['x'], 'attrT': filled(given['edge_attr_128'], 0).T, 'fT': filled(given['edge_attr_32'], 0).T,
        'w_col': by_partition(weight), 'w_row': weight[None, :], 'src_col': by_partition(src),
        'dst_col': by_partition(dst), 'next_col': by_partition(edges[0, 2:]), 'src_row': src[None, :], 'dst_row': edges,
    }
    for name in _WEIGHTS:
        laid['L0_' + name] = given['L0_gnn_' + name]
    for name in _WEIGHTS_1:
        laid['L1_' + name] = given['L1_gnn_' + name]
    nc = _bacc.Bacc("TRN2", target_bir_lowering=False, num_devices=1)
    arrays, args = {}, []
    for name, a in laid.items():
        a = _np.ascontiguousarray(a)
        arrays[f"in_{name}_dram"] = a
        args.append(nc.dram_tensor(f"in_{name}_dram", a.shape, _mybir.dt.from_np(a.dtype), kind="ExternalInput").ap())
    args.append(nc.dram_tensor("out_0_dram", given['x'].shape, _mybir.dt.float32, kind="ExternalOutput").ap())
    build(nc, *args)
    r = _run(nc, [arrays], core_ids=[0])
    return r.results[0]["out_0_dram"]
```

```python
import concourse.bass as bass
from concourse import mybir
from contextlib import ExitStack

F32 = mybir.dt.float32
I32 = mybir.dt.int32
ALU = mybir.AluOpType
ACT = mybir.ActivationFunctionType

P = 128
T = 4
R = P * T
U = 4
EPS = 1e-5
FAR = 1e30


class Groups:

    def __init__(self, every, slots):
        self.every, self.slots = every, slots


class At:

    def __init__(self, rounds, m, per_round, slots, ones, sixteens):
        self.rounds, self.m, self.per_round, self.slots = rounds, m, per_round, slots
        self.ones, self.sixteens = ones, sixteens

    def slot(self, n, back=0):
        return (self.m - back) % n

    def done(self, back=0):
        return self.ones(self.m - back + 1)

    def landed(self, back=0, parts=1):
        return self.sixteens((self.m - back) // self.slots + 1, parts)

    def count(self, per, j, back=0):
        return self.rounds * (self.per_round * per) + ((self.m - back) * per + j)

    def row(self, eng, per):
        if isinstance(self.rounds, int):
            return self.m * per
        return eng.snap(self.rounds * (self.per_round * per) + self.m * per)

    def row_back(self, eng, groups, per):
        if isinstance(self.rounds, int):
            return (groups - 1 - self.m) * per
        return eng.snap((groups - 1 - self.m) * per - self.rounds * (self.per_round * per))


def walk(eng, ticks, pieces, parts=(1,), a_round=U, depth=5):
    last = max(lag for _, lag, _ in pieces)
    reach = max(lag + depth * kind.every for kind, lag, _ in pieces)
    first = -(-reach // a_round)
    rounds = (ticks - 1) // a_round

    def peeled(n):
        for kind, lag, step in pieces:
            if 0 <= n - lag < ticks and (n - lag) % kind.every == 0:
                step(At(0, (n - lag) // kind.every, 0, kind.slots, lambda c: c, lambda c, parts: 16 * parts * c))

    if rounds <= first:
        for n in range(ticks + last):
            peeled(n)
        return
    for n in range(first * a_round):
        peeled(n)
    with eng.Fori(first, rounds) as q:
        counts = {}
        for kind in dict.fromkeys(kind for kind, _, _ in pieces):
            per = a_round // kind.every
            turns = per // kind.slots
            low = -(reach // kind.every) - 1
            ones = {c: eng.snap(q * per + c) for c in range(low, per + 2)}
            sixteens = {(c, n): eng.snap(q * (16 * n * turns) + 16 * n * c)
                        for c in range(low // kind.slots, turns + 1) for n in parts}
            counts[kind] = (per, ones, sixteens)
        for m in range(a_round):
            for kind, lag, step in pieces:
                if (m - lag) % kind.every == 0:
                    per, ones, sixteens = counts[kind]
                    step(At(q, (m - lag) // kind.every, per, kind.slots, ones.__getitem__,
                            lambda c, n, table=sixteens: table[c, n]))
    for n in range(rounds * a_round, ticks + last):
        peeled(n)


EACH = Groups(1, U)
SPARSE = Groups(4, 2)
DEEP = 8
ROUND = 8


def after(eng, sem, value):
    if not isinstance(value, int) or value > 0:
        eng.wait_ge(sem, value)


def held(eng, passed, sem, value):
    if not isinstance(value, int):
        eng.wait_ge(sem, value)
        eng.sem_inc(passed, 1)
    elif value > 0:
        eng.wait_ge(sem, value)


def build(nc, x, attrT, fT, w_col, w_row, src_col, dst_col, next_col, src_row, dst_row,
          Wk, Wq, Wv, W_dis, W_beta, ln1_g, ln1_b, W_ff1, W_ff2,
          w_in, b_in, w_f1, b_f1, w_f2, b_f2, w_o1, b_o1, w_o2, b_o2, out):
    N, D = x.shape
    HEADS = W_dis.shape[1]
    F = W_ff1.shape[1]
    H2 = F // P
    FW, FF = w_f1.shape
    GROUPS = -(-N // R)
    EG = src_col.shape[0] // P
    assert GROUPS == SPARSE.every * EG
    TRASH = N + 1
    AGG_ROWS = -(-(TRASH + R) // (P * 8)) * P * 8

    agg = nc.dram_tensor("agg", [AGG_ROWS, FF], F32, kind="Internal").ap()
    xd_dram = nc.dram_tensor("xd_dram", [EG * P, T * D], F32, kind="Internal").ap()
    q_dram = nc.dram_tensor("q_dram", [P, EG * R], F32, kind="Internal").ap()
    lead_dram = nc.dram_tensor("lead_dram", [EG * P, T], I32, kind="Internal").ap()
    y_dram = nc.dram_tensor("y_dram", [EG * P, T * D], F32, kind="Internal").ap()

    ctx = ExitStack()
    with ctx:
        def sb(name, shape, dt=F32):
            return ctx.enter_context(nc.sbuf_tensor(name, shape, dt))

        signals = []

        def sem(name):
            signals.append(nc.alloc_semaphore(name=name))
            return signals[-1]

        def sems(*names):
            return [sem(n) for n in names]

        bank = ctx.enter_context(nc.psum_tensor("bank", [P, 8, R], F32))

        class Stats:

            def __init__(self, name, n, sb):
                self.n = n
                self.bn = sb(name + "_bn", [P, 2, n, 6])
                self.dif = sb(name + "_dif", [P, 2, n])
                self.spread = sb(name + "_spread", [P, 2, n])
                self.sq = sb(name + "_sq", [P, 2, n])
                self.mean = sb(name + "_mean", [P, 2, n])
                self.var = sb(name + "_var", [P, 2, n])
                self.ln = sb(name + "_ln", [P, 2, n])
                self.rstd = sb(name + "_rstd", [P, 2, n])
                self.read, self.steps, self.roots = sems(name + "_read", name + "_steps", name + "_roots")

            def on_vector(self, dve, a, src):
                self.statistics(dve, a, src)
                self.combine(dve, a)

            def statistics(self, dve, a, src):
                s = a.slot(2)
                for j in range(self.n):
                    last = dve.bn_stats(self.bn[:, s, j], src[:, j])
                last.then_inc(self.read, 1)

            def of(self, s, c):
                return self.bn[:, s, :, c]

            def combine(self, dve, a):
                s = a.slot(2)
                dve.wait_ge(self.read, a.done())
                dve.tensor_tensor(self.dif[:, s], self.of(s, 1), self.of(s, 4), ALU.subtract).then_inc(self.steps, 1)
                dve.tensor_tensor(self.spread[:, s], self.of(s, 2), self.of(s, 5), ALU.add)
                dve.wait_ge(self.steps, a.count(3, 1))
                dve.scalar_tensor_tensor(self.mean[:, s], self.dif[:, s], -0.5, self.of(s, 1), ALU.mult, ALU.add)
                dve.scalar_tensor_tensor(self.sq[:, s], self.dif[:, s], 0.25, self.dif[:, s], ALU.mult, ALU.mult)\
                   .then_inc(self.steps, 1)
                dve.wait_ge(self.steps, a.count(3, 2))
                dve.scalar_tensor_tensor(self.var[:, s], self.spread[:, s], 1.0 / D, self.sq[:, s], ALU.mult, ALU.add)\
                   .then_inc(self.steps, 1)

            def combine_on_pool(self, pool, a, passed):
                s = a.slot(2)
                held(pool, passed, self.read, a.done())
                pool.tensor_tensor(self.dif[:, s], self.of(s, 1), self.of(s, 4), ALU.subtract).then_inc(self.steps, 1)
                pool.tensor_tensor(self.spread[:, s], self.of(s, 2), self.of(s, 5), ALU.add)
                held(pool, passed, self.steps, a.count(4, 1))
                pool.tensor_tensor(self.sq[:, s], self.dif[:, s], self.dif[:, s], ALU.mult).then_inc(self.steps, 1)
                held(pool, passed, self.steps, a.count(4, 2))
                pool.tensor_scalar(self.mean[:, s], self.sq[:, s], D / 4.0, None, ALU.mult).then_inc(self.steps, 1)
                held(pool, passed, self.steps, a.count(4, 3))
                pool.tensor_tensor(self.var[:, s], self.mean[:, s], self.spread[:, s], ALU.add).then_inc(self.steps, 1)

            def on_scalar(self, act, a, var=None):
                s = a.slot(2)
                act.activation(self.ln[:, s], (self.var if var is None else var)[:, s], ACT.Ln, bias=eps_col[:, 0:1])\
                   .then_inc(self.roots, 1)
                act.wait_ge(self.roots, a.count(2, 1))
                act.activation(self.rstd[:, s], self.ln[:, s], ACT.Exp, scale=-0.5).then_inc(self.roots, 1)

            def wait_mean(self, eng, a):
                eng.wait_ge(self.steps, a.count(3, 3))

            def wait_rstd(self, eng, a):
                eng.wait_ge(self.roots, a.count(2, 2))

        ident = sb("ident", [P, P])
        upper = sb("upper", [P, P])
        ones_col = sb("ones_col", [P, 1])
        mean_of = sb("mean_of", [P, P])
        head_of = sb("head_of", [P, HEADS])
        head_to = sb("head_to", [HEADS, P])
        trash = sb("trash", [P, T])
        trash_i = sb("trash_i", [P, T], I32)
        w1_raw = sb("w1_raw", [P, F])
        w1_g = sb("w1_g", [P, F])
        w1_c = sb("w1_c", [P, F])
        w2_sb = sb("w2_sb", [P, H2, D])
        g_col = sb("g_col", [P, 1])
        b_col = sb("b_col", [P, 1])
        z_bias = sb("z_bias", [P, H2])
        eps_col = sb("eps_col", [P, 1])
        half_col = sb("half_col", [P, 1])
        tiny_col = sb("tiny_col", [HEADS, 1])
        wb_x = sb("wb_x", [P, D])
        wb_d = sb("wb_d", [P, D])
        wb_row = sb("wb_row", [P, D])
        wb_he = sb("wb_he", [P, 2])
        wb_he_col = sb("wb_he_col", [P, 1])
        w_o2_sb = sb("w_o2_sb", [P, D])
        b_o1_col = sb("b_o1_col", [P, 1])
        b_o2_row = sb("b_o2_row", [P, D])
        ssp_abs = sb("ssp_abs", [P, 1])
        ssp_exp = sb("ssp_exp", [P, 1])
        ssp_ln = sb("ssp_ln", [P, 1])
        ssp_b = sb("ssp_b", [P, 1])
        ssp_rep = sb("ssp_rep", [P, P])
        c_row = sb("c_row", [P, D])
        wk_sb = sb("wk_sb", [P, D])
        wq_sb = sb("wq_sb", [P, D])
        wv_sb = sb("wv_sb", [P, D])
        wdis_sb = sb("wdis_sb", [1, HEADS])
        w_in_sb = sb("w_in_sb", [P, FF])
        b_in_row = sb("b_in_row", [P, FF])
        wf1_sb = sb("wf1_sb", [FW, FF])
        bf1_col = sb("bf1_col", [FF, 1])
        wf2_sb = sb("wf2_sb", [FF + 1, FF])
        wo1_sb = sb("wo1_sb", [FF, D])
        zeros = sb("zeros", [P, 32 * FF])
        consts_loaded, made, sp_passed, pool_passed, pe_passed, made_too, c_dve, c_act, c_pe, zeroed, agg_zero = sems(
            "consts_loaded", "made", "sp_passed", "pool_passed", "pe_passed", "made_too", "c_dve", "c_act", "c_pe", "zeroed", "agg_zero")

        def row(v):
            return v.rearrange("(a d) -> a d", a=1).partition_broadcast(P)

        def col(v):
            return v.rearrange("(p a) -> p a", a=1)

        LOADS = ((w1_raw[:], W_ff1), (w2_sb[:], W_ff2.rearrange("(h p) d -> p h d", p=P)), (g_col[:], col(ln1_g)),
                 (b_col[:], col(ln1_b)), (wb_x[:], W_beta[D:2 * D, :].rearrange("d a -> a d").partition_broadcast(P)),
                 (wb_d[:], W_beta[2 * D:3 * D, :].rearrange("d a -> a d").partition_broadcast(P)),
                 (wb_he[:, 0:1], W_beta[0:D, :]), (wb_he[:, 1:2], W_beta[2 * D:3 * D, :]),
                 (w_o2_sb[:], w_o2), (b_o1_col[:], col(b_o1)), (b_o2_row[:], row(b_o2)),
                 (wk_sb[:], Wk), (wq_sb[:], Wq), (wv_sb[:], Wv), (wdis_sb[:], W_dis), (w_in_sb[:], w_in),
                 (b_in_row[:], row(b_in)), (wf1_sb[:], w_f1), (bf1_col[:], col(b_f1)), (wf2_sb[0:FF, :], w_f2),
                 (wf2_sb[FF:FF + 1, :], b_f2.rearrange("(a d) -> a d", a=1)), (wo1_sb[:], w_o1))
        ALL_LOADED = 16 * len(LOADS)

        def ring(name, slots=U):
            return [sem(f"{name}{k}") for k in range(slots)]

        def named(prefix, words):
            return sems(*(f"{prefix}_{w}" for w in words.split()))

        ROOM = 41 * 1024
        room = sb("room", [P, ROOM])
        taken = [0]

        def fsb(name, shape, dt=F32):
            sizes = dict(zip("abc", shape[1:]))
            width = 1
            for n in sizes.values():
                width *= n
            part = room[0:shape[0], taken[0]:taken[0] + width]
            taken[0] += width
            assert taken[0] <= ROOM, name
            part = part if dt == F32 else part.bitcast(dt)
            names = " ".join(sizes)
            return part.rearrange(f"p ({names}) -> p {names}", **sizes) if len(sizes) > 1 else part

        f_idx = fsb("f_idx", [P, 2, 2, T], I32)
        f_dst = fsb("f_dst", [HEADS, 2, R + 2], I32)
        f_w = fsb("f_w", [1, 2, R])
        f_attr = fsb("f_attr", [P, 2, R])
        f_x = fsb("f_x", [P, 2, 2 * T, D])
        f_xn = fsb("f_xn", [P, 2 * T, D])
        f_hT = fsb("f_hT", [P, 2, R])
        f_kT = fsb("f_kT", [P, R])
        f_vT = fsb("f_vT", [P, 2, R])
        f_prod = fsb("f_prod", [P, R])
        f_same = fsb("f_same", [HEADS, R])
        f_last = fsb("f_last", [HEADS, R])
        f_pen = fsb("f_pen", [HEADS, R])
        f_max = fsb("f_max", [HEADS, 2, R + 1])
        f_was = fsb("f_was", [HEADS, R])
        f_arg = fsb("f_arg", [HEADS, 2, R])
        f_ae = fsb("f_ae", [HEADS, 2, R])
        f_den = fsb("f_den", [HEADS, 2, R])
        f_lden = fsb("f_lden", [HEADS, R])
        f_rden = fsb("f_rden", [HEADS, R])
        f_rlast = fsb("f_rlast", [HEADS, R])
        f_ev = fsb("f_ev", [P, R])
        f_sum = fsb("f_sum", [P, 2, R])
        f_q = fsb("f_q", [P, 2, R])
        f_st = Stats("f_st", 2 * T, fsb)
        f_loaded, f_got, f_xd_out, f_q_out = (ring(n, 2) for n in ("f_loaded", "f_got", "f_xd_out", "f_q_out"))
        (f_xn_done, f_tr_done, f_h_done, f_kqv_done, f_kv_done, f_flags_done, f_prod_done, f_l_done, f_pen_done,
         f_carry_done, f_max_done, f_was_done, f_args_done, f_exps_done, f_den_done, f_lden_done, f_rden_done,
         f_rlast_done, f_spread_done, f_ev_done, f_sum_done, f_q_done) = named("f", (
             "xn_done tr_done h_done kqv_done kv_done flags_done prod_done l_done pen_done carry_done max_done was_done "
             "args_done exps_done den_done lden_done rden_done rlast_done spread_done ev_done sum_done q_done"))
        TR_S = K_ = A_ = 4
        TR_D = Q_ = E_ = 5
        V_ = R_ = 6
        L_ = 7

        d_x = fsb("d_x", [P, U, T, D])
        d_xc = fsb("d_xc", [P, DEEP, T, D])
        d_out = fsb("d_out", [P, U, T, D])
        d_u = fsb("d_u", [P, DEEP, T, D])
        d_un = fsb("d_un", [P, 2, T, D])
        d_unT = fsb("d_unT", [P, R])
        d_rz = fsb("d_rz", [P, H2, R])
        d_y = fsb("d_y", [P, 2, T, D])
        d_yn = fsb("d_yn", [P, 2, T, D])
        d_junk = fsb("d_junk", [P, T, D])
        d_scale = fsb("d_scale", [P, U, T])
        (d_dot, d_arg, d_ex, d_exp1, d_beta, d_scale2, d_uvar, d_t, d_ysum, d_ymean, d_ysq, d_yln, d_yrstd, d_nm) = (
            fsb("d_" + n, [P, 2, T]) for n in "dot arg ex exp1 beta scale2 uvar t ysum ymean ysq yln yrstd nm".split())
        d_squares = fsb("d_squares", [P, T, D])
        d_xst, d_ust = Stats("d_xst", T, fsb), Stats("d_ust", T, fsb)
        d_loaded, d_stored = ring("d_loaded"), ring("d_stored")
        (d_u_done, d_dot_done, d_arg_done, d_ex_done, d_exp1_done, d_beta_done, d_scale_done, d_scale2_done, d_uvar_done,
         d_t_done, d_un_done, d_tr_done, d_unT_done, d_z_done, d_rz_done, d_o_done, d_y_done, d_nm_done, d_yn_done,
         d_xc_done, d_out_done, d_ymean_done, d_squares_done, d_yroots) = named("d", (
             "u_done dot_done arg_done ex_done exp1_done beta_done scale_done scale2_done uvar_done t_done un_done "
             "tr_done unT_done z_done rz_done o_done y_done nm_done yn_done xc_done out_done ymean_done squares_done yroots"))
        D_TR, D_Z, D_O = 0, 1, 3



        def all_of(eng, ring, count, parts=1):
            for k, landed in enumerate(ring):
                eng.wait_ge(landed, 16 * parts * ((count - 1 - k) // len(ring) + 1))

        def nxt(eng, sem, a, groups):
            if isinstance(a.rounds, int) and a.m == groups - 1:
                eng.wait_ge(sem, a.done())
            else:
                eng.wait_ge(sem, a.done(-1))

        def first_of(a):
            return isinstance(a.rounds, int) and a.m == 0

        def nodes_stored(eng):
            all_of(eng, f_q_out, EG)
            all_of(eng, f_xd_out, EG)
            all_of(eng, d_stored, GROUPS)

        def edges_over(eng):
            for done in (b_totc_done, b_out_done, b_idx_done):
                eng.wait_ge(done, EG)

        def node_rows(dram, at):
            at = min(at, N - R) if isinstance(at, int) else at
            return dram[bass.ds(at, R), :].rearrange("(p j) d -> p j d", j=T)

        def spill(dram, at):
            return dram[bass.ds(at, P), :].rearrange("p (j d) -> p j d", j=T)

        def col_of(dram, at):
            return dram[bass.ds(at, P), :]

        def tiles(b):
            return bank[:, b].rearrange("p (j d) -> p j d", j=T)

        def gather(pool, to, dram, index, last_row, signal):
            pool.indirect_dma_start(to, None, dram, bass.IndirectOffsetOnAxis(ap=index, axis=0),
                                    bounds_check=last_row, oob_is_err=False).then_inc(signal, 16)

        def scatter(pool, dram, index, rows, last_row, signal):
            pool.indirect_dma_start(dram, bass.IndirectOffsetOnAxis(ap=index, axis=0), rows, None,
                                    bounds_check=last_row, oob_is_err=False).then_inc(signal, 16)

        c_b = c_row[:].rearrange("p (a d) -> p a d", a=1).to_broadcast([P, T, D])

        with nc.Block() as block:
            @block.sync
            def _(sp):
                for dst, src in LOADS:
                    sp.dma_start(dst, src).then_inc(consts_loaded, 16)
                sp.wait_ge(zeroed, 1)
                table = agg.rearrange("(p c) f -> p (c f)", p=P)
                per, piece = AGG_ROWS // P * FF, 32 * FF
                for lo in range(0, per, piece):
                    hi = min(lo + piece, per)
                    sp.dma_start(table[:, lo:hi], zeros[:, 0:hi - lo]).then_inc(agg_zero, 16)
                sp.wait_ge(agg_zero, 16 * -(-per // piece))

                def f_load(a):
                    k = a.slot(2)
                    at_p, at_r = a.row(sp, P), a.row(sp, R)
                    held(sp, sp_passed, f_l_done, a.done(2))
                    sp.dma_start(f_idx[:, k, 0], col_of(src_col, at_p)).then_inc(f_loaded[k], 16)
                    sp.dma_start(f_idx[:, k, 1], col_of(dst_col, at_p)).then_inc(f_loaded[k], 16)
                    sp.dma_start(f_dst[:, k], dst_row[:, bass.ds(at_r, R + 2)].partition_broadcast(HEADS)).then_inc(f_loaded[k], 16)
                    sp.dma_start(f_w[:, k], w_row[:, bass.ds(at_r, R)]).then_inc(f_loaded[k], 16)
                    sp.dma_start(f_attr[:, k], attrT[:, bass.ds(at_r, R)]).then_inc(f_loaded[k], 16)

                def f_spill_rows(a):
                    at_p = a.row(sp, P)
                    held(sp, sp_passed, f_got[a.slot(2)], a.landed(0, 2 * T))
                    sp.dma_start(spill(xd_dram, at_p), f_x[:, a.slot(2), T:]).then_inc(f_xd_out[a.slot(2)], 16)

                def f_spill_q(a):
                    at_r = a.row(sp, R)
                    held(sp, sp_passed, f_q_done, a.done())
                    sp.dma_start(q_dram[:, bass.ds(at_r, R)], f_q[:, a.slot(2)]).then_inc(f_q_out[a.slot(2)], 16)

                def d_load(a):
                    k, at = a.slot(U), a.row(sp, R)
                    held(sp, sp_passed, d_u_done, a.done(U))
                    held(sp, sp_passed, d_xc_done, a.done(U))
                    sp.dma_start(d_x[:, k], node_rows(x, at)).then_inc(d_loaded[k], 16)

                def d_store(a):
                    k, at = a.slot(U), a.row(sp, R)
                    held(sp, sp_passed, d_out_done, a.done())
                    if isinstance(at, int) and at > N - R:
                        held(sp, sp_passed, d_stored[a.slot(U, 1)], a.landed(1))
                    sp.dma_start(node_rows(out, at), d_out[:, k]).then_inc(d_stored[k], 16)

                walk(sp, GROUPS, [(SPARSE, 3, f_load), (EACH, 0, d_load), (SPARSE, 9, f_spill_rows), (SPARSE, 18, f_spill_q),
                                  (EACH, 9, d_store)], (1, 2 * T), ROUND)
                nodes_stored(sp)

            @block.gpsimd
            def _(pool):
                pool.memset(ident[:], 0.0)
                pool.memset(upper[:], 1.0)
                pool.memset(mean_of[:], 1.0 / D)
                pool.memset(head_of[:], float(D // HEADS) ** -0.5)
                pool.memset(head_to[:], 1.0)
                pool.memset(zeros[:], 0.0).then_inc(zeroed, 1)
                pool.iota(trash_i[:], pattern=[[P, T]], base=TRASH, channel_multiplier=1).then_inc(made, 1)
                pool.wait_ge(zeroed, 1)
                pool.affine_select(out=ident[:], in_=ident[:], compare_op=ALU.not_equal, fill=1.0, base=0,
                                   pattern=[[-1, P]], channel_multiplier=1).then_inc(made, 1)
                pool.affine_select(out=upper[:], in_=upper[:], compare_op=ALU.is_gt, fill=0.0, base=0,
                                   pattern=[[1, P]], channel_multiplier=-1).then_inc(made, 1)
                wide = D // HEADS
                pool.affine_select(out=head_of[:], in_=head_of[:], compare_op=ALU.is_ge, fill=0.0, base=0,
                                   pattern=[[-wide, HEADS]], channel_multiplier=1)
                pool.affine_select(out=head_to[:], in_=head_to[:], compare_op=ALU.is_ge, fill=0.0, base=0,
                                   pattern=[[1, P]], channel_multiplier=-wide).then_inc(made, 1)
                pool.wait_ge(made, 4)
                pool.affine_select(out=head_of[:], in_=head_of[:], compare_op=ALU.is_ge, fill=0.0, base=wide - 1,
                                   pattern=[[wide, HEADS]], channel_multiplier=-1)
                pool.affine_select(out=head_to[:], in_=head_to[:], compare_op=ALU.is_ge, fill=0.0, base=wide - 1,
                                   pattern=[[-1, P]], channel_multiplier=wide)
                pool.tensor_copy(trash[:], trash_i[:]).then_inc(made_too, 1)

                pool.wait_ge(c_dve, 5)

                def f_gathers(tiles_of_rows):
                    def step(a):
                        k = a.slot(2)
                        if tiles_of_rows[0] == 0:
                            held(pool, pool_passed, f_loaded[k], a.landed(0, 5))
                            held(pool, pool_passed, f_xn_done, a.done(2))
                            held(pool, pool_passed, f_xd_out[k], a.landed(2))
                        for i in tiles_of_rows:
                            gather(pool, f_x[:, k, i], x, f_idx[:, k, i // T, i % T:i % T + 1], N - 1, f_got[k])
                    return step

                def d_base(a):
                    held(pool, pool_passed, d_out_done, a.done(DEEP))
                    held(pool, pool_passed, d_loaded[a.slot(U)], a.landed())
                    pool.tensor_tensor(d_xc[:, a.slot(DEEP)], d_x[:, a.slot(U)], c_b, ALU.add).then_inc(d_xc_done, 1)

                def d_moments(a):
                    d_ust.combine_on_pool(pool, a, pool_passed)

                def d_normed(a):
                    s = a.slot(2)
                    held(pool, pool_passed, d_t_done, a.done())
                    held(pool, pool_passed, d_tr_done, a.done(2))
                    t = d_t[:, s].rearrange("p (j a) -> p j a", a=1).to_broadcast([P, T, D])
                    pool.tensor_tensor(d_un[:, s], d_u[:, a.slot(DEEP)], t, ALU.mult).then_inc(d_un_done, 1)

                def d_result(a):
                    held(pool, pool_passed, d_yn_done, a.done())
                    held(pool, pool_passed, d_xc_done, a.done())
                    held(pool, pool_passed, d_stored[a.slot(U)], a.landed(U))
                    pool.tensor_tensor(d_out[:, a.slot(U)], d_yn[:, a.slot(2)], d_xc[:, a.slot(DEEP)], ALU.add)\
                        .then_inc(d_out_done, 1)

                walk(pool, GROUPS, [(SPARSE, 1, f_gathers((0, 1, 2))), (SPARSE, 2, f_gathers((3, 4, 5))), (SPARSE, 3, f_gathers((6, 7))),
                                    (EACH, 0, d_base), (EACH, 1, d_normed), (EACH, 0, d_moments), (EACH, 5, d_result)],
                     (1, 5), ROUND)

            @block.vector
            def _(dve):
                dve.memset(eps_col[:], EPS)
                dve.memset(tiny_col[:], 1e-16)
                dve.memset(ones_col[:], 1.0)
                dve.memset(half_col[:], 0.5).then_inc(c_dve, 1)
                dve.wait_ge(consts_loaded, ALL_LOADED)
                dve.tensor_scalar(w1_g[:], w1_raw[:], g_col[:, 0:1], None, ALU.mult)
                dve.tensor_tensor(wb_he_col[:], wb_he[:, 0:1], wb_he[:, 1:2], ALU.add)
                dve.tensor_tensor(wb_row[:], wb_x[:], wb_d[:], ALU.subtract).then_inc(c_dve, 1)
                dve.wait_ge(c_act, 3)
                dve.scalar_tensor_tensor(ssp_b[:], b_o1_col[:], 0.0, ssp_ln[:], ALU.max, ALU.add).then_inc(c_dve, 1)
                dve.wait_ge(c_dve, 3)
                dve.tensor_copy(ssp_rep[:], ssp_b[:, 0:1].to_broadcast([P, P])).then_inc(c_dve, 1)
                dve.wait_ge(c_pe, 1)
                dve.tensor_copy(z_bias[:], bank[:, 0, 0:H2])
                dve.tensor_tensor(w1_c[:], w1_g[:], bank[:, 2, 0:F], ALU.subtract)
                dve.tensor_tensor(c_row[:], bank[:, 1, 0:D], b_o2_row[:], ALU.add).then_inc(c_dve, 1)

                def f_stats(a):
                    dve.wait_ge(f_got[a.slot(2)], a.landed(0, 2 * T))
                    f_st.on_vector(dve, a, f_x[:, a.slot(2)])

                def f_normed(a):
                    s = a.slot(2)
                    f_st.wait_rstd(dve, a)
                    after(dve, f_tr_done, a.done(1))
                    for j in range(2 * T):
                        last = dve.tensor_scalar(f_xn[:, j], f_x[:, s, j], f_st.mean[:, s, j:j + 1],
                                                 f_st.rstd[:, s, j:j + 1], ALU.subtract, ALU.mult)
                    last.then_inc(f_xn_done, 1)

                def f_flags(a):
                    s = k = a.slot(2)
                    dve.wait_ge(f_loaded[k], a.landed(0, 5))
                    after(dve, f_rlast_done, a.done(1))
                    dve.tensor_tensor(f_same[:], f_dst[:, k, 1:R + 1], f_dst[:, k, 0:R], ALU.is_equal)
                    dve.tensor_tensor(f_last[:], f_dst[:, k, 1:R + 1], f_dst[:, k, 2:R + 2], ALU.not_equal)\
                       .then_inc(f_flags_done, 1)
                    if first_of(a):
                        dve.memset(f_max[:, s, 0:1], -FAR).then_inc(f_carry_done, 1)
                    else:
                        dve.wait_ge(f_max_done, a.done(1))
                        dve.tensor_copy(f_max[:, s, 0:1], f_max[:, 1 - s, R:R + 1]).then_inc(f_carry_done, 1)
                    dve.wait_ge(f_flags_done, a.done())
                    dve.tensor_scalar(f_pen[:], f_same[:], 1.0, FAR, ALU.subtract, ALU.mult).then_inc(f_pen_done, 1)

                def f_products(a):
                    dve.wait_ge(f_kv_done, a.done())
                    after(dve, f_l_done, a.done(1))
                    dve.tensor_tensor(f_prod[:], f_kT[:], bank[:, Q_], ALU.mult).then_inc(f_prod_done, 1)

                def f_maxima(a):
                    s = a.slot(2)
                    dve.wait_ge(f_l_done, a.done())
                    dve.wait_ge(f_pen_done, a.done())
                    dve.wait_ge(f_carry_done, a.done())
                    dve.tensor_tensor_scan(f_max[:, s, 1:R + 1], f_pen[:], bank[0:HEADS, L_], f_max[:, s, 0:1], ALU.add,
                                           ALU.max).then_inc(f_max_done, 1)
                    dve.tensor_tensor(f_was[:, 0:1], f_max[:, s, 0:1], f_pen[:, 0:1], ALU.add)
                    dve.wait_ge(f_max_done, a.done())
                    dve.tensor_tensor(f_was[:, 1:R], f_max[:, s, 1:R], f_pen[:, 1:R], ALU.add).then_inc(f_was_done, 1)
                    after(dve, f_exps_done, a.done(1))
                    dve.tensor_tensor(f_arg[:, 1], bank[0:HEADS, L_], f_max[:, s, 1:R + 1], ALU.subtract)
                    dve.wait_ge(f_was_done, a.done())
                    dve.tensor_tensor(f_arg[:, 0], f_was[:], f_max[:, s, 1:R + 1], ALU.subtract).then_inc(f_args_done, 1)

                def f_denominators(a):
                    s = a.slot(2)
                    dve.wait_ge(f_exps_done, a.done())
                    dve.tensor_tensor_scan(f_den[:, s], f_ae[:, 0], f_ae[:, 1], 0.0 if first_of(a) else f_den[:, 1 - s, R - 1:R],
                                           ALU.mult, ALU.add).then_inc(f_den_done, 1)

                def f_divisors(a):
                    dve.wait_ge(f_rden_done, a.done())
                    after(dve, f_spread_done, a.done(1))
                    dve.tensor_tensor(f_rlast[:], f_rden[:], f_last[:], ALU.mult).then_inc(f_rlast_done, 1)

                def f_sums(a):
                    s = a.slot(2)
                    dve.wait_ge(f_spread_done, a.done())
                    after(dve, f_sum_done, a.done(1))
                    dve.tensor_tensor(f_ev[:], f_vT[:, s], bank[:, E_], ALU.mult).then_inc(f_ev_done, 1)
                    dve.wait_ge(f_ev_done, a.done())
                    after(dve, f_q_done, a.done(2))
                    dve.tensor_tensor_scan(f_sum[:, s], bank[:, A_], f_ev[:], 0.0 if first_of(a) else f_sum[:, 1 - s, R - 1:R],
                                           ALU.mult, ALU.add).then_inc(f_sum_done, 1)
                    dve.wait_ge(f_sum_done, a.done())
                    after(dve, f_q_out[s], a.landed(2))
                    dve.tensor_tensor(f_q[:, s], f_sum[:, s], bank[:, R_], ALU.mult).then_inc(f_q_done, 1)

                def d_stats(a):
                    dve.wait_ge(d_loaded[a.slot(U)], a.landed())
                    d_xst.on_vector(dve, a, d_x[:, a.slot(U)])

                def d_centred(a):
                    s, k, deep = a.slot(2), a.slot(U), a.slot(DEEP)
                    d_xst.wait_mean(dve, a)
                    after(dve, d_y_done, a.done(DEEP))
                    for j in range(T):
                        last = dve.tensor_scalar(d_u[:, deep, j], d_x[:, k, j], d_xst.mean[:, s, j:j + 1], 0.0, ALU.subtract, ALU.max)
                    last.then_inc(d_u_done, 1)
                    dve.wait_ge(d_u_done, a.done())
                    after(dve, d_uvar_done, a.done(2))
                    d_ust.statistics(dve, a, d_u[:, deep])

                def d_dots(a):
                    s, k = a.slot(2), a.slot(DEEP)
                    dve.wait_ge(d_u_done, a.done())
                    for j in range(T):
                        last = dve.scalar_tensor_tensor(d_junk[:, j], d_u[:, k, j], 1.0, wb_row[:], ALU.mult, ALU.mult,
                                                        accum_out=d_dot[:, s, j:j + 1])
                    last.then_inc(d_dot_done, 1)

                def d_logits(a):
                    s = a.slot(2)
                    dve.wait_ge(d_dot_done, a.done())
                    d_xst.wait_rstd(dve, a)
                    dve.tensor_tensor(d_arg[:, s], d_dot[:, s], d_xst.rstd[:, s], ALU.mult).then_inc(d_arg_done, 1)

                def d_gates(a):
                    s = a.slot(2)
                    dve.wait_ge(d_ex_done, a.done())
                    dve.tensor_scalar(d_exp1[:, s], d_ex[:, s], 1.0, None, ALU.add).then_inc(d_exp1_done, 1)
                    dve.wait_ge(d_exp1_done, a.done())
                    dve.reciprocal(d_beta[:, s], d_exp1[:, s]).then_inc(d_beta_done, 1)
                    dve.wait_ge(d_beta_done, a.done())
                    dve.tensor_tensor(d_scale[:, a.slot(U)], d_beta[:, s], d_xst.rstd[:, s], ALU.mult).then_inc(d_scale_done, 1)
                    dve.wait_ge(d_scale_done, a.done())
                    dve.tensor_tensor(d_scale2[:, s], d_scale[:, a.slot(U)], d_scale[:, a.slot(U)], ALU.mult).then_inc(d_scale2_done, 1)
                    dve.wait_ge(d_scale2_done, a.done())
                    dve.wait_ge(d_ust.steps, a.count(4, 4))
                    dve.scalar_tensor_tensor(d_uvar[:, s], d_scale2[:, s], 1.0 / D, d_ust.var[:, s], ALU.mult, ALU.mult)\
                       .then_inc(d_uvar_done, 1)

                def d_normed(a):
                    s = a.slot(2)
                    d_ust.wait_rstd(dve, a)
                    after(dve, d_un_done, a.done(2))
                    dve.tensor_tensor(d_t[:, s], d_scale[:, a.slot(U)], d_ust.rstd[:, s], ALU.mult).then_inc(d_t_done, 1)

                def d_residual(a):
                    s, k = a.slot(2), a.slot(DEEP)
                    dve.wait_ge(d_o_done, a.done())
                    after(dve, d_yn_done, a.done(2))
                    for j in range(T):
                        last = dve.scalar_tensor_tensor(d_y[:, s, j], d_u[:, k, j], d_scale[:, a.slot(U), j:j + 1],
                                                        tiles(D_O)[:, j], ALU.mult, ALU.add, accum_out=d_ysum[:, s, j:j + 1])
                    last.then_inc(d_y_done, 1)
                    dve.wait_ge(d_y_done, a.done())
                    dve.tensor_scalar(d_ymean[:, s], d_ysum[:, s], -1.0 / D, None, ALU.mult).then_inc(d_ymean_done, 1)

                def d_shift(a):
                    s = a.slot(2)
                    dve.wait_ge(d_yroots, a.count(2, 2))
                    dve.tensor_tensor(d_nm[:, s], d_ymean[:, s], d_yrstd[:, s], ALU.mult).then_inc(d_nm_done, 1)

                walk(dve, GROUPS, [(EACH, 5, d_shift), (EACH, 1, d_logits), (EACH, 4, d_residual),
                                   (SPARSE, 8, f_products), (EACH, 0, d_stats), (EACH, 1, d_gates), (SPARSE, 6, f_normed),
                                   (EACH, 0, d_centred), (EACH, 1, d_normed), (EACH, 0, d_dots), (SPARSE, 4, f_stats),
                                   (SPARSE, 13, f_sums), (SPARSE, 11, f_divisors), (SPARSE, 7, f_flags), (SPARSE, 9, f_maxima),
                                   (SPARSE, 10, f_denominators)], (1, 5, 2 * T), ROUND)

            @block.scalar
            def _(act):
                act.preload_act_table_set("natural_log_exp_and_others")
                act.wait_ge(consts_loaded, ALL_LOADED)
                act.wait_ge(c_dve, 1)
                act.activation(ssp_abs[:], b_o1_col[:], ACT.Abs).then_inc(c_act, 1)
                act.wait_ge(c_act, 1)
                act.activation(ssp_exp[:], ssp_abs[:], ACT.Exp, scale=-1.0).then_inc(c_act, 1)
                act.wait_ge(c_act, 2)
                act.activation(ssp_ln[:], ssp_exp[:], ACT.Ln, scale=0.5, bias=half_col[:, 0:1]).then_inc(c_act, 1)
                act.wait_ge(c_dve, 5)

                def f_roots(a):
                    f_st.wait_mean(act, a)
                    f_st.on_scalar(act, a)

                def f_relus(a):
                    act.wait_ge(f_tr_done, a.done())
                    act.activation(f_hT[:, 0], bank[:, TR_S], ACT.Relu)
                    act.activation(f_hT[:, 1], bank[:, TR_D], ACT.Relu).then_inc(f_h_done, 1)

                def f_keys(a):
                    act.wait_ge(f_kqv_done, a.done())
                    after(act, f_prod_done, a.done(1))
                    after(act, f_ev_done, a.done(2))
                    act.activation(f_kT[:], bank[:, K_], ACT.Copy)
                    act.activation(f_vT[:, a.slot(2)], bank[:, V_], ACT.Copy).then_inc(f_kv_done, 1)

                def f_exps(a):
                    act.wait_ge(f_args_done, a.done())
                    after(act, f_spread_done, a.done(1))
                    act.activation(f_ae[:], f_arg[:], ACT.Exp).then_inc(f_exps_done, 1)

                def f_reciprocals(a):
                    act.wait_ge(f_den_done, a.done())
                    act.activation(f_lden[:], f_den[:, a.slot(2)], ACT.Ln, bias=tiny_col[:, 0:1]).then_inc(f_lden_done, 1)
                    act.wait_ge(f_lden_done, a.done())
                    after(act, f_rlast_done, a.done(1))
                    act.activation(f_rden[:], f_lden[:], ACT.Exp, scale=-1.0).then_inc(f_rden_done, 1)

                def d_exps(a):
                    s = a.slot(2)
                    act.wait_ge(d_arg_done, a.done())
                    act.activation(d_ex[:, s], d_arg[:, s], ACT.Exp, scale=-1.0).then_inc(d_ex_done, 1)

                def d_roots(a):
                    d_xst.wait_mean(act, a)
                    d_xst.on_scalar(act, a)

                def d_roots_of_w(a):
                    act.wait_ge(d_uvar_done, a.done())
                    d_ust.on_scalar(act, a, d_uvar)

                def d_transposed(a):
                    act.wait_ge(d_tr_done, a.done())
                    act.activation(d_unT[:], bank[:, D_TR], ACT.Copy).then_inc(d_unT_done, 1)

                def d_hidden(a):
                    act.wait_ge(d_z_done, a.done())
                    after(act, d_o_done, a.done(1))
                    for h in range(H2):
                        last = act.activation(d_rz[:, h], bank[:, D_Z + h], ACT.Relu, bias=z_bias[:, h:h + 1])
                    last.then_inc(d_rz_done, 1)

                def d_roots_of_y(a):
                    s = a.slot(2)
                    act.wait_ge(d_ymean_done, a.done())
                    after(act, d_squares_done, a.done(1))
                    for j in range(T):
                        last = act.activation(d_squares[:, j], d_y[:, s, j], ACT.Square, bias=d_ymean[:, s, j:j + 1],
                                              accum_out=d_ysq[:, s, j:j + 1])
                    last.then_inc(d_squares_done, 1)
                    act.wait_ge(d_squares_done, a.done())
                    act.activation(d_yln[:, s], d_ysq[:, s], ACT.Ln, scale=1.0 / D, bias=eps_col[:, 0:1]).then_inc(d_yroots, 1)
                    act.wait_ge(d_yroots, a.count(2, 1))
                    act.activation(d_yrstd[:, s], d_yln[:, s], ACT.Exp, scale=-0.5).then_inc(d_yroots, 1)

                def d_last_norm(a):
                    s = a.slot(2)
                    act.wait_ge(d_nm_done, a.done())
                    after(act, d_out_done, a.done(2))
                    for j in range(T):
                        last = act.activation(d_yn[:, s, j], d_y[:, s, j], ACT.Identity, bias=d_nm[:, s, j:j + 1],
                                              scale=d_yrstd[:, s, j:j + 1])
                    last.then_inc(d_yn_done, 1)

                walk(act, GROUPS, [(EACH, 1, d_exps), (EACH, 3, d_hidden), (EACH, 2, d_transposed), (SPARSE, 5, f_roots),
                                   (SPARSE, 10, f_exps), (SPARSE, 11, f_reciprocals), (EACH, 0, d_roots),
                                   (EACH, 1, d_roots_of_w), (EACH, 4, d_roots_of_y), (SPARSE, 6, f_relus),
                                   (EACH, 5, d_last_norm), (SPARSE, 7, f_keys)], (1,), ROUND)

            @block.tensor
            def _(pe):
                pe.wait_ge(consts_loaded, ALL_LOADED)
                pe.wait_ge(c_dve, 4)
                pe.wait_ge(made_too, 1)
                for h in range(H2):
                    pe.matmul(bank[:, 0, h:h + 1], w1_raw[:, h * P:(h + 1) * P], b_col[:], start=True, stop=True)
                pe.matmul(bank[:, 2, 0:F], mean_of[:], w1_g[:], start=True, stop=True)
                pe.matmul(bank[:, 1, 0:D], ssp_rep[:], w_o2_sb[:], start=True, stop=True).then_inc(c_pe, 1)
                pe.wait_ge(c_dve, 5)

                def f_transposes(a):
                    pe.wait_ge(f_xn_done, a.done())
                    after(pe, f_q_done, a.done(2))
                    for e, to in enumerate((TR_S, TR_D)):
                        for j in range(T):
                            last = pe.transpose(bank[:, to, j * P:(j + 1) * P], f_xn[:, e * T + j], ident[:])
                    last.then_inc(f_tr_done, 1)

                def f_products(a):
                    k = a.slot(2)
                    pe.wait_ge(f_loaded[k], a.landed(0, 5))
                    after(pe, f_q_done, a.done(2))
                    pe.matmul(bank[:, V_], wv_sb[:], f_attr[:, k], start=True, stop=True)
                    pe.wait_ge(f_h_done, a.done())
                    pe.matmul(bank[:, Q_], wq_sb[:], f_hT[:, 1], start=True, stop=True)
                    pe.matmul(bank[:, K_], wk_sb[:], f_hT[:, 0], start=True, stop=True).then_inc(f_kqv_done, 1)

                def f_logits(a):
                    pe.wait_ge(f_prod_done, a.done())
                    after(pe, f_args_done, a.done(1))
                    pe.matmul(bank[0:HEADS, L_], head_of[:], f_prod[:], start=True, stop=False)
                    pe.matmul(bank[0:HEADS, L_], wdis_sb[:], f_w[:, a.slot(2)], start=False, stop=True).then_inc(f_l_done, 1)

                def f_spreads(a):
                    pe.wait_ge(f_rlast_done, a.done())
                    nxt(pe, f_prod_done, a, EG)
                    pe.matmul(bank[:, A_], head_to[:], f_ae[:, 0], start=True, stop=True)
                    pe.matmul(bank[:, E_], head_to[:], f_ae[:, 1], start=True, stop=True)
                    pe.matmul(bank[:, R_], head_to[:], f_rlast[:], start=True, stop=True).then_inc(f_spread_done, 1)

                def d_transposes(a):
                    s = a.slot(2)
                    pe.wait_ge(d_un_done, a.done())
                    after(pe, d_unT_done, a.done(1))
                    for j in range(T):
                        last = pe.transpose(bank[:, D_TR, j * P:(j + 1) * P], d_un[:, s, j], ident[:])
                    last.then_inc(d_tr_done, 1)

                def d_up(a):
                    pe.wait_ge(d_unT_done, a.done())
                    after(pe, d_rz_done, a.done(1))
                    for h in range(H2):
                        last = pe.matmul(bank[:, D_Z + h], w1_c[:, h * P:(h + 1) * P], d_unT[:], start=True, stop=True)
                    last.then_inc(d_z_done, 1)

                def d_down(a):
                    pe.wait_ge(d_rz_done, a.done())
                    after(pe, d_y_done, a.done(1))
                    for j in range(T):
                        for h in range(H2):
                            last = pe.matmul(tiles(D_O)[:, j], d_rz[:, h, j * P:(j + 1) * P], w2_sb[:, h],
                                             start=(h == 0), stop=(h == H2 - 1))
                    last.then_inc(d_o_done, 1)

                walk(pe, GROUPS, [(EACH, 2, d_transposes), (EACH, 3, d_down), (EACH, 2, d_up), (SPARSE, 12, f_spreads),
                                  (SPARSE, 8, f_logits), (SPARSE, 6, f_transposes), (SPARSE, 6, f_products)], (1, 5), ROUND)

        nc.clear_and_free_semaphores(signals)
        nc.all_engine_barrier()
        signals.clear()
        taken[0] = 0
        sp_passed, pool_passed, pe_passed = sems("sp_passed_too", "pool_passed_too", "pe_passed_too")

        b_q = fsb("b_q", [P, U, R])
        b_x = fsb("b_x", [P, U, T, D])
        b_dst = fsb("b_dst", [P, U, R + 1], I32)
        b_src = fsb("b_src", [P, U, R], I32)
        b_idx = fsb("b_idx", [P, U, 3, T], I32)
        b_more = fsb("b_more", [P, T])
        b_out_idx = fsb("b_out_idx", [P, U, T], I32)
        b_wc = fsb("b_wc", [P, U, T])
        b_f = fsb("b_f", [FW, U, R])
        b_next = fsb("b_next", [P, R])
        b_g = fsb("b_g", [P, 2, R])
        b_u = fsb("b_u", [P, T, D])
        b_a = fsb("b_a", [P, T, D])
        b_w = fsb("b_w", [P, 2, T, D])
        b_un = fsb("b_un", [P, T, D])
        b_unT = fsb("b_unT", [P, R])
        b_rz = fsb("b_rz", [P, H2, R])
        b_y = fsb("b_y", [P, T, D])
        b_yn = fsb("b_yn", [P, T, D])
        b_x1 = fsb("b_x1", [P, T, D])
        b_out = fsb("b_out", [P, 2, T, D])
        b_u1 = fsb("b_u1", [P, T, D])
        b_u1T = fsb("b_u1T", [P, R])
        b_junk = fsb("b_junk", [P, T, D])
        b_abs = fsb("b_abs", [FF, R])
        b_exp = fsb("b_exp", [FF, R])
        b_ln = fsb("b_ln", [FF, R])
        b_pos = fsb("b_pos", [FF, R])
        b_ssp = fsb("b_ssp", [FF + 1, R])
        b_hh = fsb("b_hh", [P, T, FF])
        b_xij = fsb("b_xij", [P, T, FF])
        b_eq = fsb("b_eq", [P, T, R])
        b_tri = fsb("b_tri", [P, T, P])
        b_tot = fsb("b_tot", [P, 2, T, FF])
        b_srcf = fsb("b_srcf", [P, 2, T])
        b_agg_idx = fsb("b_agg_idx", [P, U, T], I32)
        (b_dot, b_arg0, b_arg, b_ex, b_exp1, b_beta, b_nbeta, b_scale, b_nm, b_flag, b_away, b_jump) = (
            fsb("b_" + n, [P, T]) for n in "dot arg0 arg ex exp1 beta nbeta scale nm flag away jump".split())
        b_xst, b_wst, b_yst, b_zst = (Stats(n, T, fsb) for n in ("b_xst", "b_wst", "b_yst", "b_zst"))
        b_loaded, b_put, b_added, b_lead_out = ring("b_loaded"), ring("b_put"), ring("b_added"), ring("b_lead_out")
        (b_next_done, b_g_done, b_tr_done, b_u_done, b_dot_done, b_arg0_done, b_arg_done, b_ex_done, b_exp1_done,
         b_beta_done, b_nbeta_done, b_a_done, b_w_done, b_un_done, b_utr_done, b_unT_done, b_z_done,
         b_rz_done, b_o_done, b_y_done, b_nm_done, b_yn_done, b_x1_done, b_out_done, b_u1_done, b_u1tr_done, b_u1T_done,
         b_hh_done, b_fl_done, b_abs_done, b_exp_done, b_ln_done, b_pos_done, b_ssp_done, b_w2_done, b_hb_done,
         b_xij_done, b_srcf_done, b_eq_done, b_tri_done, b_tot_done, b_totc_done, b_away_done,
         b_jump_done, b_idx_done, b_more_done, b_out_idx_done) = named("b", (
             "next_done g_done tr_done u_done dot_done arg0_done arg_done ex_done exp1_done beta_done nbeta_done "
             "a_done w_done un_done utr_done unT_done z_done rz_done o_done y_done nm_done yn_done x1_done "
             "out_done u1_done u1tr_done u1T_done hh_done fl_done abs_done exp_done ln_done pos_done ssp_done w2_done "
             "hb_done xij_done srcf_done eq_done tri_done tot_done totc_done away_done jump_done idx_done more_done out_idx_done"))
        B_HE, B_TR, B_Z, B_O, B_F, B_W, B_T = 0, 1, 2, 4, 5, 6, 7
        CNT, GATE = T * FF, T * FF + T

        c_idx = fsb("c_idx", [P, U, T], I32)
        c_y = fsb("c_y", [P, U, T, D])
        c_idx2 = fsb("c_idx2", [P, U, T], I32)
        c_lead = fsb("c_lead", [P, U, T], I32)
        c_agg = fsb("c_agg", [P, U, T, FF])
        c_y2 = fsb("c_y2", [P, U, T, D])
        c_aT = fsb("c_aT", [FF, R])
        c_abs = fsb("c_abs", [P, R])
        c_exp = fsb("c_exp", [P, R])
        c_ln = fsb("c_ln", [P, R])
        c_pos = fsb("c_pos", [P, R])
        c_ssp = fsb("c_ssp", [P, R])
        c_res = fsb("c_res", [P, 2, T, D])
        c_ready, c_got, c_spilled = ring("c_ready"), ring("c_got"), ring("c_spilled")
        c_ready2, c_got2, c_stored = ring("c_ready2"), ring("c_got2"), ring("c_stored")
        (c_tr_done, c_aT_done, c_z_done, c_abs_done, c_exp_done, c_ln_done, c_pos_done, c_ssp_done, c_o_done,
         c_res_done) = named("c", "tr_done aT_done z_done abs_done exp_done ln_done pos_done ssp_done o_done res_done")
        C_TR, C_Z, C_O = 0, 1, 2

        with nc.Block() as block:
            @block.sync
            def _(sp):

                def b_load(a):
                    k = a.slot(U)
                    at_p, at_r = a.row_back(sp, EG, P), a.row_back(sp, EG, R)
                    held(sp, sp_passed, b_xij_done, a.done(U))
                    sp.dma_start(b_q[:, k], q_dram[:, bass.ds(at_r, R)]).then_inc(b_loaded[k], 16)
                    sp.dma_start(b_x[:, k], spill(xd_dram, at_p)).then_inc(b_loaded[k], 16)
                    sp.dma_start(b_dst[:, k], dst_row[:, bass.ds(at_r + 1, R + 1)].partition_broadcast(P)).then_inc(b_loaded[k], 16)
                    sp.dma_start(b_src[:, k], src_row[:, bass.ds(at_r, R)].partition_broadcast(P)).then_inc(b_loaded[k], 16)
                    sp.dma_start(b_idx[:, k, 0], col_of(src_col, at_p)).then_inc(b_loaded[k], 16)
                    sp.dma_start(b_idx[:, k, 1], col_of(dst_col, at_p)).then_inc(b_loaded[k], 16)
                    sp.dma_start(b_idx[:, k, 2], col_of(next_col, at_p)).then_inc(b_loaded[k], 16)
                    sp.dma_start(b_wc[:, k], col_of(w_col, at_p)).then_inc(b_loaded[k], 16)
                    sp.dma_start(b_f[:, k], fT[:, bass.ds(at_r, R)]).then_inc(b_loaded[k], 16)

                def b_spill_lead(a):
                    at_p = a.row_back(sp, EG, P)
                    held(sp, sp_passed, b_idx_done, a.done())
                    sp.dma_start(col_of(lead_dram, at_p), b_agg_idx[:, a.slot(U)]).then_inc(b_lead_out[a.slot(U)], 16)

                walk(sp, EG, [(EACH, 0, b_load), (EACH, 6, b_spill_lead)], (1, T))
                all_of(sp, b_lead_out, EG)

                def c1_step(a, lag):
                    k = a.slot(U)
                    at_p = a.row(sp, P)
                    if lag == 0:
                        held(sp, sp_passed, c_got[k], a.landed(U, T))
                        sp.dma_start(c_idx[:, k], col_of(src_col, at_p)).then_inc(c_ready[k], 16)
                    if lag == 3:
                        held(sp, sp_passed, c_got[k], a.landed(0, T))
                        sp.dma_start(spill(y_dram, at_p), c_y[:, k]).then_inc(c_spilled[k], 16)
                walk(sp, EG, [(EACH, 0, lambda a: c1_step(a, 0)), (EACH, 3, lambda a: c1_step(a, 3))], parts=(1, T))
                all_of(sp, c_spilled, EG)

                def c2_step(a, lag):
                    k = a.slot(U)
                    at_p = a.row(sp, P)
                    held(sp, sp_passed, c_stored[k], a.landed(U, T))
                    sp.dma_start(c_idx2[:, k], col_of(src_col, at_p)).then_inc(c_ready2[k], 16)
                    sp.dma_start(c_y2[:, k], spill(y_dram, at_p)).then_inc(c_ready2[k], 16)
                    sp.dma_start(c_lead[:, k], col_of(lead_dram, at_p)).then_inc(c_ready2[k], 16)
                walk(sp, EG, [(EACH, 0, lambda a: c2_step(a, 0))], parts=(1, T))
                all_of(sp, c_stored, EG, T)

            @block.gpsimd
            def _(pool):

                def b_store(a):
                    k, s = a.slot(U), a.slot(2)
                    held(pool, pool_passed, b_x1_done, a.done())
                    held(pool, pool_passed, b_put[a.slot(U, 2)], a.landed(2, T))
                    pool.tensor_tensor(b_out[:, s], b_x1[:], c_b, ALU.add).then_inc(b_out_done, 1)
                    held(pool, pool_passed, b_out_done, a.done())
                    held(pool, pool_passed, b_out_idx_done, a.done())
                    for j in range(T):
                        scatter(pool, out, b_out_idx[:, k, j:j + 1], b_out[:, s, j], N - 1, b_put[k])

                def b_add(a):
                    k, s = a.slot(U), a.slot(2)
                    held(pool, pool_passed, b_idx_done, a.done())
                    held(pool, pool_passed, b_totc_done, a.done())
                    held(pool, pool_passed, b_added[a.slot(U, 1)], a.landed(1, T))
                    for j in range(T):
                        pool.indirect_dma_start(agg, bass.IndirectOffsetOnAxis(ap=b_agg_idx[:, k, j:j + 1], axis=0),
                                                b_tot[:, s, j], None, bounds_check=AGG_ROWS - 1, oob_is_err=True,
                                                compute_op=ALU.add).then_inc(b_added[k], 16)

                walk(pool, EG, [(EACH, 3, b_add), (EACH, 2, b_store)], (1, T))
                all_of(pool, b_put, EG, T)
                all_of(pool, b_added, EG, T)

                def c1_step(a, lag):
                    k = a.slot(U)
                    held(pool, pool_passed, c_ready[k], a.landed())
                    held(pool, pool_passed, c_spilled[k], a.landed(U))
                    for j in range(T):
                        gather(pool, c_y[:, k, j], out, c_idx[:, k, j:j + 1], N - 1, c_got[k])
                walk(pool, EG, [(EACH, 0, lambda a: c1_step(a, 0))])
                all_of(pool, c_got, EG, T)

                def c2_step(a, lag):
                    k = a.slot(U)
                    if lag == 0:
                        held(pool, pool_passed, c_ready2[k], a.landed(0, 3))
                        held(pool, pool_passed, c_tr_done, a.done(U))
                        for j in range(T):
                            gather(pool, c_agg[:, k, j], agg, c_idx2[:, k, j:j + 1], N - 1, c_got2[k])
                    if lag == 2:
                        held(pool, pool_passed, c_res_done, a.done())
                        held(pool, pool_passed, c_stored[a.slot(U, 1)], a.landed(1, T))
                        for j in range(T):
                            scatter(pool, out, c_lead[:, k, j:j + 1], c_res[:, a.slot(2), j], N - 1, c_stored[k])
                walk(pool, EG, [(EACH, 0, lambda a: c2_step(a, 0)), (EACH, 2, lambda a: c2_step(a, 2))], parts=(1, 3, T))

            @block.vector
            def _(dve):
                dve.memset(b_ssp[FF:FF + 1, :], 1.0)

                def b_back(a):
                    s, k = a.slot(2), a.slot(U)
                    dve.wait_ge(b_loaded[k], a.landed(0, 9))
                    after(dve, b_g_done, a.done(1))
                    dve.tensor_tensor(b_next[:], b_dst[:, k, 0:R], b_dst[:, k, 1:R + 1], ALU.is_equal).then_inc(b_next_done, 1)
                    dve.wait_ge(b_next_done, a.done())
                    after(dve, b_tr_done, a.done(2))
                    dve.tensor_tensor_scan(b_g[:, s, ::-1], b_next[:, ::-1], b_q[:, k, ::-1],
                                           0.0 if first_of(a) else b_g[:, 1 - s, 0:1], ALU.mult, ALU.add).then_inc(b_g_done, 1)

                def b_centred(a):
                    s, k = a.slot(2), a.slot(U)
                    xs = b_x[:, k]
                    b_xst.on_vector(dve, a, xs)
                    b_xst.wait_mean(dve, a)
                    after(dve, b_w_done, a.done(1))
                    for j in range(T):
                        last = dve.tensor_scalar(b_u[:, j], xs[:, j], b_xst.mean[:, s, j:j + 1], 0.0, ALU.subtract, ALU.max)
                    last.then_inc(b_u_done, 1)
                    dve.wait_ge(b_u_done, a.done())
                    for j in range(T):
                        last = dve.scalar_tensor_tensor(b_junk[:, j], b_u[:, j], 1.0, wb_row[:], ALU.mult, ALU.mult,
                                                        accum_out=b_dot[:, j:j + 1])
                    last.then_inc(b_dot_done, 1)

                def b_logits(a):
                    s = a.slot(2)
                    b_xst.wait_rstd(dve, a)
                    dve.wait_ge(b_dot_done, a.done())
                    dve.tensor_tensor(b_arg0[:], b_dot[:], b_xst.rstd[:, s], ALU.mult).then_inc(b_arg0_done, 1)
                    dve.wait_ge(b_arg0_done, a.done())
                    dve.wait_ge(b_tr_done, a.done())
                    dve.tensor_tensor(b_arg[:], b_arg0[:], bank[:, B_T, GATE:GATE + T], ALU.add).then_inc(b_arg_done, 1)

                def b_gates(a):
                    s = a.slot(2)
                    dve.wait_ge(b_ex_done, a.done())
                    dve.tensor_scalar(b_exp1[:], b_ex[:], 1.0, None, ALU.add).then_inc(b_exp1_done, 1)
                    dve.wait_ge(b_exp1_done, a.done())
                    dve.reciprocal(b_beta[:], b_exp1[:]).then_inc(b_beta_done, 1)
                    dve.wait_ge(b_beta_done, a.done())
                    dve.tensor_tensor(b_scale[:], b_beta[:], b_xst.rstd[:, s], ALU.mult)
                    dve.tensor_scalar(b_nbeta[:], b_beta[:], -1.0, 1.0, ALU.mult, ALU.add).then_inc(b_nbeta_done, 1)
                    dve.wait_ge(b_nbeta_done, a.done())
                    for j in range(T):
                        last = dve.tensor_scalar(b_a[:, j], tiles(B_HE)[:, j], b_nbeta[:, j:j + 1], None, ALU.mult)
                    last.then_inc(b_a_done, 1)
                    dve.wait_ge(b_a_done, a.done())
                    after(dve, b_y_done, a.done(2))
                    for j in range(T):
                        last = dve.scalar_tensor_tensor(b_w[:, s, j], b_u[:, j], b_scale[:, j:j + 1], b_a[:, j],
                                                        ALU.mult, ALU.add)
                    last.then_inc(b_w_done, 1)
                    dve.wait_ge(b_w_done, a.done())
                    b_wst.on_vector(dve, a, b_w[:, s])

                def b_normed(a):
                    s = a.slot(2)
                    b_wst.wait_rstd(dve, a)
                    after(dve, b_utr_done, a.done(1))
                    for j in range(T):
                        last = dve.tensor_scalar(b_un[:, j], b_w[:, s, j], b_wst.mean[:, s, j:j + 1],
                                                 b_wst.rstd[:, s, j:j + 1], ALU.subtract, ALU.mult)
                    last.then_inc(b_un_done, 1)

                def b_residual(a):
                    s = a.slot(2)
                    dve.wait_ge(b_o_done, a.done())
                    after(dve, b_yn_done, a.done(1))
                    dve.tensor_tensor(b_y[:], b_w[:, s], tiles(B_O), ALU.add).then_inc(b_y_done, 1)
                    dve.wait_ge(b_y_done, a.done())
                    b_yst.on_vector(dve, a, b_y)

                def b_sources(a):
                    s, k = a.slot(2), a.slot(U)
                    dve.wait_ge(b_loaded[k], a.landed(0, 9))
                    dve.tensor_copy(b_srcf[:, s], b_idx[:, k, 0]).then_inc(b_srcf_done, 1)
                    dve.tensor_tensor(b_more[:], b_idx[:, k, 1], b_idx[:, k, 2], ALU.is_equal).then_inc(b_more_done, 1)
                    dve.wait_ge(b_more_done, a.done())
                    after(dve, b_put[k], a.landed(U, T))
                    dve.scalar_tensor_tensor(b_out_idx[:, k], b_more[:], float(N + 1), b_idx[:, k, 1], ALU.mult, ALU.add)\
                       .then_inc(b_out_idx_done, 1)
                    dve.wait_ge(b_srcf_done, a.done())
                    after(dve, b_tot_done, a.done(1))
                    for j in range(T):
                        last = dve.tensor_scalar(b_eq[:, j], b_src[:, k], b_srcf[:, s, j:j + 1], None, ALU.is_equal)
                    last.then_inc(b_eq_done, 1)
                    dve.wait_ge(b_eq_done, a.done())
                    for j in range(T):
                        last = dve.tensor_tensor(b_tri[:, j], b_eq[:, j, j * P:(j + 1) * P], upper[:], ALU.mult)
                    last.then_inc(b_tri_done, 1)

                def b_filters(a):
                    dve.wait_ge(b_ln_done, a.done())
                    after(dve, b_w2_done, a.done(1))
                    dve.tensor_tensor(b_ssp[0:FF, :], b_pos[:], b_ln[:], ALU.add).then_inc(b_ssp_done, 1)

                def b_shift(a):
                    s = a.slot(2)
                    b_yst.wait_rstd(dve, a)
                    dve.scalar_tensor_tensor(b_nm[:], b_yst.mean[:, s], -1.0, b_yst.rstd[:, s], ALU.mult, ALU.mult)\
                       .then_inc(b_nm_done, 1)

                def b_result(a):
                    s, k = a.slot(2), a.slot(U)
                    dve.wait_ge(b_yn_done, a.done())
                    after(dve, b_out_done, a.done(1))
                    dve.tensor_tensor(b_x1[:], b_yn[:], b_x[:, k], ALU.add).then_inc(b_x1_done, 1)
                    dve.wait_ge(b_x1_done, a.done())
                    b_zst.on_vector(dve, a, b_x1)
                    b_zst.wait_mean(dve, a)
                    after(dve, b_u1tr_done, a.done(1))
                    for j in range(T):
                        last = dve.tensor_scalar(b_u1[:, j], b_x1[:, j], b_zst.mean[:, s, j:j + 1], 0.0, ALU.subtract, ALU.max)
                    last.then_inc(b_u1_done, 1)

                def b_messages(a):
                    s, k = a.slot(2), a.slot(U)
                    dve.wait_ge(b_hh_done, a.done())
                    b_zst.wait_rstd(dve, a)
                    for j in range(T):
                        last = dve.scalar_tensor_tensor(b_hh[:, j], bank[:, B_W, j * FF:(j + 1) * FF],
                                                        b_zst.rstd[:, s, j:j + 1], b_in_row[:], ALU.mult, ALU.add)
                    last.then_inc(b_hb_done, 1)
                    dve.wait_ge(b_hb_done, a.done())
                    for j in range(T):
                        last = dve.scalar_tensor_tensor(b_xij[:, j], bank[:, B_W, (T + j) * FF:(T + j + 1) * FF],
                                                        b_wc[:, k, j:j + 1], b_hh[:, j], ALU.mult, ALU.mult)
                    last.then_inc(b_xij_done, 1)

                def b_rows(a):
                    s, k = a.slot(2), a.slot(U)
                    dve.wait_ge(b_totc_done, a.done())
                    dve.tensor_scalar(b_flag[:], bank[:, B_T, CNT:CNT + T], 1.0, None, ALU.min)
                    dve.tensor_tensor(b_away[:], trash[:], b_srcf[:, s], ALU.subtract).then_inc(b_away_done, 1)
                    dve.wait_ge(b_away_done, a.done())
                    dve.tensor_tensor(b_jump[:], b_flag[:], b_away[:], ALU.mult).then_inc(b_jump_done, 1)
                    dve.wait_ge(b_jump_done, a.done())
                    after(dve, b_added[k], a.landed(U, T))
                    after(dve, b_lead_out[k], a.landed(U))
                    dve.tensor_tensor(b_agg_idx[:, k], b_srcf[:, s], b_jump[:], ALU.add).then_inc(b_idx_done, 1)

                walk(dve, EG, [(EACH, 0, b_back), (EACH, 2, b_shift), (EACH, 1, b_normed), (EACH, 0, b_centred), (EACH, 2, b_result),
                               (EACH, 0, b_logits), (EACH, 2, b_filters), (EACH, 2, b_sources), (EACH, 0, b_gates),
                               (EACH, 3, b_rows), (EACH, 1, b_residual), (EACH, 2, b_messages)], (1, T, 9))
                edges_over(dve)

                def c_step(a, lag):
                    k, s = a.slot(U), a.slot(2)
                    dve.wait_ge(c_ln_done, a.done())
                    after(dve, c_o_done, a.done(1))
                    dve.scalar_tensor_tensor(c_ssp[:], c_ln[:], ssp_b[:, 0:1], c_pos[:], ALU.subtract, ALU.add).then_inc(c_ssp_done, 1)
                    dve.wait_ge(c_o_done, a.done())
                    dve.wait_ge(c_ready2[k], a.landed(0, 3))
                    after(dve, c_stored[a.slot(U, 2)], a.landed(2, T))
                    dve.tensor_tensor(c_res[:, s], c_y2[:, k], tiles(C_O), ALU.add).then_inc(c_res_done, 1)
                walk(dve, EG, [(EACH, 0, lambda a: c_step(a, 0))], parts=(1, 3, T))

            @block.scalar
            def _(act):

                def b_roots(a):
                    b_xst.wait_mean(act, a)
                    b_xst.on_scalar(act, a)

                def b_exps(a):
                    act.wait_ge(b_arg_done, a.done())
                    act.activation(b_ex[:], b_arg[:], ACT.Exp, scale=-1.0).then_inc(b_ex_done, 1)

                def b_roots_of_w(a):
                    b_wst.wait_mean(act, a)
                    b_wst.on_scalar(act, a)

                def b_transposed(a):
                    act.wait_ge(b_utr_done, a.done())
                    act.activation(b_unT[:], bank[:, B_TR], ACT.Copy).then_inc(b_unT_done, 1)

                def b_hidden(a):
                    act.wait_ge(b_z_done, a.done())
                    after(act, b_o_done, a.done(1))
                    for h in range(H2):
                        last = act.activation(b_rz[:, h], bank[:, B_Z + h], ACT.Relu, bias=z_bias[:, h:h + 1])
                    last.then_inc(b_rz_done, 1)

                def b_softplus(a):
                    act.wait_ge(b_fl_done, a.done())
                    act.activation(b_abs[:], bank[0:FF, B_F], ACT.Abs, bias=bf1_col[:, 0:1]).then_inc(b_abs_done, 1)
                    after(act, b_ssp_done, a.done(1))
                    act.activation(b_pos[:], bank[0:FF, B_F], ACT.Relu, bias=bf1_col[:, 0:1]).then_inc(b_pos_done, 1)
                    act.wait_ge(b_abs_done, a.done())
                    act.activation(b_exp[:], b_abs[:], ACT.Exp, scale=-1.0).then_inc(b_exp_done, 1)
                    act.wait_ge(b_exp_done, a.done())
                    act.activation(b_ln[:], b_exp[:], ACT.Ln, scale=0.5, bias=half_col[0:FF, 0:1]).then_inc(b_ln_done, 1)

                def b_roots_of_y(a):
                    b_yst.wait_mean(act, a)
                    b_yst.on_scalar(act, a)

                def b_last_norm(a):
                    s = a.slot(2)
                    act.wait_ge(b_nm_done, a.done())
                    after(act, b_x1_done, a.done(1))
                    for j in range(T):
                        last = act.activation(b_yn[:, j], b_y[:, j], ACT.Identity, bias=b_nm[:, j:j + 1],
                                              scale=b_yst.rstd[:, s, j:j + 1])
                    last.then_inc(b_yn_done, 1)

                def b_roots_of_x1(a):
                    b_zst.wait_mean(act, a)
                    b_zst.on_scalar(act, a)

                def b_x1_transposed(a):
                    act.wait_ge(b_u1tr_done, a.done())
                    act.activation(b_u1T[:], bank[:, B_F], ACT.Copy).then_inc(b_u1T_done, 1)

                def b_totals(a):
                    act.wait_ge(b_tot_done, a.done())
                    after(act, b_added[a.slot(U, 2)], a.landed(2, T))
                    act.activation(b_tot[:, a.slot(2)], bank[:, B_T, 0:T * FF].rearrange("p (j f) -> p j f", j=T), ACT.Copy)\
                       .then_inc(b_totc_done, 1)

                walk(act, EG, [(EACH, 2, b_last_norm), (EACH, 3, b_totals), (EACH, 1, b_transposed), (EACH, 0, b_roots),
                               (EACH, 1, b_hidden), (EACH, 2, b_roots_of_x1), (EACH, 0, b_exps), (EACH, 2, b_x1_transposed),
                               (EACH, 1, b_softplus), (EACH, 0, b_roots_of_w), (EACH, 1, b_roots_of_y)], (1, T))
                edges_over(act)

                def c_step(a, lag):
                    act.wait_ge(c_tr_done, a.done())
                    act.activation(c_aT[:], bank[0:FF, C_TR], ACT.Copy).then_inc(c_aT_done, 1)
                    act.wait_ge(c_z_done, a.done())
                    act.activation(c_abs[:], bank[:, C_Z], ACT.Abs, bias=b_o1_col[:, 0:1]).then_inc(c_abs_done, 1)
                    after(act, c_ssp_done, a.done(1))
                    act.activation(c_pos[:], bank[:, C_Z], ACT.Relu, bias=b_o1_col[:, 0:1]).then_inc(c_pos_done, 1)
                    act.wait_ge(c_abs_done, a.done())
                    act.activation(c_exp[:], c_abs[:], ACT.Exp, scale=-1.0).then_inc(c_exp_done, 1)
                    act.wait_ge(c_exp_done, a.done())
                    act.activation(c_ln[:], c_exp[:], ACT.Ln, scale=0.5, bias=half_col[:, 0:1]).then_inc(c_ln_done, 1)
                walk(act, EG, [(EACH, 0, lambda a: c_step(a, 0))])

            @block.tensor
            def _(pe):

                def b_aggregates(a):
                    s = a.slot(2)
                    pe.wait_ge(b_g_done, a.done())
                    after(pe, b_a_done, a.done(1))
                    for j in range(T):
                        pe.transpose(tiles(B_HE)[:, j], b_g[:, s, j * P:(j + 1) * P], ident[:])

                def b_logits(a):
                    s = a.slot(2)
                    after(pe, b_totc_done, a.done(3))
                    for j in range(T):
                        last = pe.matmul(bank[:, B_T, GATE + j:GATE + j + 1], b_g[:, s, j * P:(j + 1) * P], wb_he_col[:],
                                         start=True, stop=True)
                    last.then_inc(b_tr_done, 1)

                def b_transposes(a):
                    pe.wait_ge(b_un_done, a.done())
                    after(pe, b_unT_done, a.done(1))
                    for j in range(T):
                        last = pe.transpose(tiles(B_TR)[:, j], b_un[:, j], ident[:])
                    last.then_inc(b_utr_done, 1)

                def b_up(a):
                    pe.wait_ge(b_unT_done, a.done())
                    after(pe, b_rz_done, a.done(1))
                    for h in range(H2):
                        last = pe.matmul(bank[:, B_Z + h], w1_g[:, h * P:(h + 1) * P], b_unT[:], start=True, stop=True)
                    last.then_inc(b_z_done, 1)

                def b_down(a):
                    pe.wait_ge(b_rz_done, a.done())
                    after(pe, b_y_done, a.done(1))
                    for j in range(T):
                        for h in range(H2):
                            last = pe.matmul(tiles(B_O)[:, j], b_rz[:, h, j * P:(j + 1) * P], w2_sb[:, h],
                                             start=(h == 0), stop=(h == H2 - 1))
                    last.then_inc(b_o_done, 1)

                def b_filters_hidden(a):
                    k = a.slot(U)
                    pe.wait_ge(b_loaded[k], a.landed(0, 9))
                    after(pe, b_u1T_done, a.done(1))
                    pe.matmul(bank[0:FF, B_F], wf1_sb[:], b_f[:, k], start=True, stop=True).then_inc(b_fl_done, 1)

                def b_filters(a):
                    pe.wait_ge(b_ssp_done, a.done())
                    after(pe, b_xij_done, a.done(1))
                    for j in range(T):
                        last = pe.matmul(bank[:, B_W, (T + j) * FF:(T + j + 1) * FF], b_ssp[:, j * P:(j + 1) * P], wf2_sb[:],
                                         start=True, stop=True)
                    last.then_inc(b_w2_done, 1)

                def b_x1_transposes(a):
                    pe.wait_ge(b_u1_done, a.done())
                    pe.wait_ge(b_pos_done, a.done())
                    for j in range(T):
                        last = pe.transpose(tiles(B_F)[:, j], b_u1[:, j], ident[:])
                    last.then_inc(b_u1tr_done, 1)

                def b_products(a):
                    pe.wait_ge(b_u1T_done, a.done())
                    for j in range(T):
                        last = pe.matmul(bank[:, B_W, j * FF:(j + 1) * FF], b_u1T[:, j * P:(j + 1) * P], w_in_sb[:],
                                         start=True, stop=True)
                    last.then_inc(b_hh_done, 1)

                def b_totals(a):
                    pe.wait_ge(b_xij_done, a.done())
                    pe.wait_ge(b_tri_done, a.done())
                    after(pe, b_idx_done, a.done(1))
                    for i in range(T):
                        here = slice(i * P, (i + 1) * P)
                        for j in range(T):
                            pe.matmul(bank[:, B_T, i * FF:(i + 1) * FF], b_eq[:, j, here], b_xij[:, j],
                                      start=(j == 0), stop=(j == T - 1))
                        for j in range(i + 1):
                            last = pe.matmul(bank[:, B_T, CNT + i:CNT + i + 1], b_tri[:, i] if j == i else b_eq[:, j, here],
                                             ones_col[:], start=(j == 0), stop=(j == i))
                    last.then_inc(b_tot_done, 1)

                walk(pe, EG, [(EACH, 0, b_aggregates), (EACH, 0, b_logits), (EACH, 1, b_transposes), (EACH, 1, b_up), (EACH, 2, b_x1_transposes),
                              (EACH, 1, b_down), (EACH, 2, b_filters), (EACH, 2, b_products), (EACH, 1, b_filters_hidden),
                              (EACH, 2, b_totals)], (1, 9))
                edges_over(pe)

                def c_step(a, lag):
                    k = a.slot(U)
                    held(pe, pe_passed, c_got2[k], a.landed(0, T))
                    held(pe, pe_passed, c_aT_done, a.done(1))
                    for j in range(T):
                        last = pe.transpose(bank[0:FF, C_TR, j * P:(j + 1) * P], c_agg[:, k, j], ident[:])
                    last.then_inc(c_tr_done, 1)
                    pe.wait_ge(c_aT_done, a.done())
                    after(pe, c_abs_done, a.done(1))
                    after(pe, c_pos_done, a.done(1))
                    pe.matmul(bank[:, C_Z], wo1_sb[:], c_aT[:], start=True, stop=True).then_inc(c_z_done, 1)
                    pe.wait_ge(c_ssp_done, a.done())
                    after(pe, c_res_done, a.done(1))
                    for j in range(T):
                        last = pe.matmul(tiles(C_O)[:, j], c_ssp[:, j * P:(j + 1) * P], w_o2_sb[:], start=True, stop=True)
                    last.then_inc(c_o_done, 1)
                walk(pe, EG, [(EACH, 0, lambda a: c_step(a, 0))], parts=(1, T))



_WEIGHTS = ['Wk', 'Wq', 'Wv', 'W_dis', 'W_beta', 'ln1_g', 'ln1_b', 'W_ff1', 'W_ff2']
_WEIGHTS_1 = ['w_in', 'b_in', 'w_f1', 'b_f1', 'w_f2', 'b_f2', 'w_o1', 'b_o1', 'w_o2', 'b_o2']


def kernel(**inputs):
    import numpy as _np
    import concourse.bacc as _bacc
    from concourse import mybir as _mybir
    from concourse.bass_utils import run_bass_kernel_spmd as _run

    given = {k: _np.asarray(v) for k, v in inputs.items()}
    n, e = given['x'].shape[0], given['src'].shape[0]
    groups = -(-e // R)
    slots = groups * R

    def filled(v, fill):
        full = _np.full((slots,) + v.shape[1:], fill, v.dtype)
        full[:e] = v
        return full

    def by_partition(v):
        return v.reshape(groups, T, P).transpose(0, 2, 1).reshape(groups * P, T)

    src, dst, weight = filled(given['src'], n), filled(given['dst'], n), filled(given['edge_weight'], 0)
    edges = _np.full((1, slots + 2), n + 1, dst.dtype)
    edges[0, 0] = -1
    edges[0, 1:-1] = dst
    laid = {
        'x': given['x'], 'attrT': filled(given['edge_attr_128'], 0).T, 'fT': filled(given['edge_attr_32'], 0).T,
        'w_col': by_partition(weight), 'w_row': weight[None, :], 'src_col': by_partition(src),
        'dst_col': by_partition(dst), 'next_col': by_partition(edges[0, 2:]), 'src_row': src[None, :], 'dst_row': edges,
    }
    for name in _WEIGHTS:
        laid['L0_' + name] = given['L0_gnn_' + name]
    for name in _WEIGHTS_1:
        laid['L1_' + name] = given['L1_gnn_' + name]
    nc = _bacc.Bacc("TRN2", target_bir_lowering=False, num_devices=1)
    arrays, args = {}, []
    for name, a in laid.items():
        a = _np.ascontiguousarray(a)
        arrays[f"in_{name}_dram"] = a
        args.append(nc.dram_tensor(f"in_{name}_dram", a.shape, _mybir.dt.from_np(a.dtype), kind="ExternalInput").ap())
    args.append(nc.dram_tensor("out_0_dram", given['x'].shape, _mybir.dt.float32, kind="ExternalOutput").ap())
    build(nc, *args)
    r = _run(nc, [arrays], core_ids=[0])
    return r.results[0]["out_0_dram"]
```

```python
import concourse.bass as bass
from concourse import mybir
from contextlib import ExitStack

F32 = mybir.dt.float32
I32 = mybir.dt.int32
ALU = mybir.AluOpType
ACT = mybir.ActivationFunctionType

P = 128
T = 4
R = P * T
U = 4
EPS = 1e-5
FAR = 1e30




class Groups:

    def __init__(self, every, slots):
        self.every, self.slots = every, slots


class At:

    def __init__(self, rounds, m, per_round, slots, ones, sixteens):
        self.rounds, self.m, self.per_round, self.slots = rounds, m, per_round, slots
        self.ones, self.sixteens = ones, sixteens

    def slot(self, n, back=0):
        return (self.m - back) % n

    def done(self, back=0):
        return self.ones(self.m - back + 1)

    def landed(self, back=0, parts=1):
        return self.sixteens((self.m - back) // self.slots + 1, parts)

    def count(self, per, j, back=0):
        return self.rounds * (self.per_round * per) + ((self.m - back) * per + j)

    def row(self, eng, per):
        if isinstance(self.rounds, int):
            return self.m * per
        return eng.snap(self.rounds * (self.per_round * per) + self.m * per)

    def row_back(self, eng, groups, per):
        if isinstance(self.rounds, int):
            return (groups - 1 - self.m) * per
        return eng.snap((groups - 1 - self.m) * per - self.rounds * (self.per_round * per))


def walk(eng, ticks, pieces, parts=(1,), a_round=U, depth=5):
    last = max(lag for _, lag, _ in pieces)
    reach = max(lag + depth * kind.every for kind, lag, _ in pieces)
    first = -(-reach // a_round)
    rounds = (ticks - 1) // a_round

    def peeled(n):
        for kind, lag, step in pieces:
            if 0 <= n - lag < ticks and (n - lag) % kind.every == 0:
                step(At(0, (n - lag) // kind.every, 0, kind.slots, lambda c: c, lambda c, parts: 16 * parts * c))

    if rounds <= first:
        for n in range(ticks + last):
            peeled(n)
        return
    for n in range(first * a_round):
        peeled(n)
    with eng.Fori(first, rounds) as q:
        counts = {}
        for kind in dict.fromkeys(kind for kind, _, _ in pieces):
            per = a_round // kind.every
            turns = per // kind.slots
            low = -(reach // kind.every) - 1
            ones = {c: eng.snap(q * per + c) for c in range(low, per + 1)}
            sixteens = {(c, n): eng.snap(q * (16 * n * turns) + 16 * n * c)
                        for c in range(low // kind.slots, turns + 1) for n in parts}
            counts[kind] = (per, ones, sixteens)
        for m in range(a_round):
            for kind, lag, step in pieces:
                if (m - lag) % kind.every == 0:
                    per, ones, sixteens = counts[kind]
                    step(At(q, (m - lag) // kind.every, per, kind.slots, ones.__getitem__,
                            lambda c, n, table=sixteens: table[c, n]))
    for n in range(rounds * a_round, ticks + last):
        peeled(n)


EACH = Groups(1, U)
SPARSE = Groups(4, 2)
DEEP = 8
ROUND = 8


def after(eng, sem, value):
    if not isinstance(value, int) or value > 0:
        eng.wait_ge(sem, value)


def held(eng, passed, sem, value):
    if not isinstance(value, int):
        eng.wait_ge(sem, value)
        eng.sem_inc(passed, 1)
    elif value > 0:
        eng.wait_ge(sem, value)


def build(nc, x, attrT, fT, w_col, w_row, src_col, dst_col, next_col, src_row, dst_row,
          Wk, Wq, Wv, W_dis, W_beta, ln1_g, ln1_b, W_ff1, W_ff2,
          w_in, b_in, w_f1, b_f1, w_f2, b_f2, w_o1, b_o1, w_o2, b_o2, out):
    N, D = x.shape
    HEADS = W_dis.shape[1]
    F = W_ff1.shape[1]
    H2 = F // P
    FW, FF = w_f1.shape
    GROUPS = -(-N // R)
    EG = src_col.shape[0] // P
    assert GROUPS == SPARSE.every * EG
    TRASH = N + 1
    AGG_ROWS = -(-(TRASH + R) // (P * 8)) * P * 8

    AW = FF + 1
    agg = nc.dram_tensor("agg", [AGG_ROWS, AW], F32, kind="Internal").ap()
    TABLE = AGG_ROWS // P * AW
    ZERO_PIECE = 2048
    table = agg.rearrange("(p c) f -> p (c f)", p=P)
    xd_dram = nc.dram_tensor("xd_dram", [EG * P, T * D], F32, kind="Internal").ap()
    q_dram = nc.dram_tensor("q_dram", [P, EG * R], F32, kind="Internal").ap()
    lead_dram = nc.dram_tensor("lead_dram", [EG * P, T], I32, kind="Internal").ap()

    ctx = ExitStack()
    with ctx:
        def sb(name, shape, dt=F32):
            return ctx.enter_context(nc.sbuf_tensor(name, shape, dt))

        signals = []

        def sem(name):
            signals.append(nc.alloc_semaphore(name=name))
            return signals[-1]

        def sems(*names):
            return [sem(n) for n in names]

        bank = ctx.enter_context(nc.psum_tensor("bank", [P, 8, R], F32))

        class Stats:

            def __init__(self, name, n, sb):
                self.n = n
                self.bn = sb(name + "_bn", [P, 2, n, 6])
                self.dif = sb(name + "_dif", [P, 2, n])
                self.spread = sb(name + "_spread", [P, 2, n])
                self.sq = sb(name + "_sq", [P, 2, n])
                self.part = sb(name + "_part", [P, 2, n])
                self.nmean = sb(name + "_nmean", [P, 2, n])
                self.var = sb(name + "_var", [P, 2, n])
                self.ln = sb(name + "_ln", [P, 2, n])
                self.rstd = sb(name + "_rstd", [P, 2, n])
                self.read, self.steps, self.roots = sems(name + "_read", name + "_steps", name + "_roots")

            def on_vector(self, dve, a, src):
                self.statistics(dve, a, src)
                self.combine(dve, a)

            def statistics(self, dve, a, src):
                s = a.slot(2)
                for j in range(self.n):
                    last = dve.bn_stats(self.bn[:, s, j], src[:, j])
                last.then_inc(self.read, 1)

            def of(self, s, c):
                return self.bn[:, s, :, c]

            def combine(self, dve, a):
                s = a.slot(2)
                dve.wait_ge(self.read, a.done())
                dve.tensor_tensor(self.dif[:, s], self.of(s, 1), self.of(s, 4), ALU.subtract).then_inc(self.steps, 1)
                dve.tensor_tensor(self.spread[:, s], self.of(s, 2), self.of(s, 5), ALU.add)
                dve.wait_ge(self.steps, a.count(3, 1))
                dve.scalar_tensor_tensor(self.nmean[:, s], self.dif[:, s], 0.5, self.of(s, 1), ALU.mult, ALU.subtract)
                dve.scalar_tensor_tensor(self.sq[:, s], self.dif[:, s], 0.25, self.dif[:, s], ALU.mult, ALU.mult)\
                   .then_inc(self.steps, 1)
                dve.wait_ge(self.steps, a.count(3, 2))
                dve.scalar_tensor_tensor(self.var[:, s], self.spread[:, s], 1.0 / D, self.sq[:, s], ALU.mult, ALU.add)\
                   .then_inc(self.steps, 1)

            def combine_on_pool(self, pool, a, passed):
                s = a.slot(2)
                held(pool, passed, self.read, a.done())
                pool.tensor_tensor(self.dif[:, s], self.of(s, 1), self.of(s, 4), ALU.subtract).then_inc(self.steps, 1)
                pool.tensor_tensor(self.spread[:, s], self.of(s, 2), self.of(s, 5), ALU.add)
                held(pool, passed, self.steps, a.count(4, 1))
                pool.tensor_tensor(self.sq[:, s], self.dif[:, s], self.dif[:, s], ALU.mult).then_inc(self.steps, 1)
                held(pool, passed, self.steps, a.count(4, 2))
                pool.tensor_scalar(self.part[:, s], self.sq[:, s], D / 4.0, None, ALU.mult).then_inc(self.steps, 1)
                held(pool, passed, self.steps, a.count(4, 3))
                pool.tensor_tensor(self.var[:, s], self.part[:, s], self.spread[:, s], ALU.add).then_inc(self.steps, 1)

            def on_scalar(self, act, a, var=None):
                s = a.slot(2)
                act.activation(self.ln[:, s], (self.var if var is None else var)[:, s], ACT.Ln, bias=eps_col[:, 0:1])\
                   .then_inc(self.roots, 1)
                act.wait_ge(self.roots, a.count(2, 1))
                act.activation(self.rstd[:, s], self.ln[:, s], ACT.Exp, scale=-0.5).then_inc(self.roots, 1)

            def wait_mean(self, eng, a):
                eng.wait_ge(self.steps, a.count(3, 3))

            def wait_rstd(self, eng, a):
                eng.wait_ge(self.roots, a.count(2, 2))

        ident = sb("ident", [P, P])
        upper = sb("upper", [P, P])
        ones_col = sb("ones_col", [P, 1])
        mean_of = sb("mean_of", [P, P])
        head_of = sb("head_of", [P, HEADS])
        head_to = sb("head_to", [HEADS, P])
        trash = sb("trash", [P, T])
        trash_i = sb("trash_i", [P, T], I32)
        w1_raw = sb("w1_raw", [P, F])
        w1_g = sb("w1_g", [P, F])
        w1_c = sb("w1_c", [P, F])
        w2_sb = sb("w2_sb", [P, H2, D])
        g_col = sb("g_col", [P, 1])
        b_col = sb("b_col", [P, 1])
        z_bias = sb("z_bias", [P, H2])
        eps_col = sb("eps_col", [P, 1])
        half_col = sb("half_col", [P, 1])
        tiny_col = sb("tiny_col", [HEADS, 1])
        wb_x = sb("wb_x", [P, D])
        wb_d = sb("wb_d", [P, D])
        wb_row = sb("wb_row", [P, D])
        wb_he = sb("wb_he", [P, 2])
        wb_he_col = sb("wb_he_col", [P, 1])
        w_o2_sb = sb("w_o2_sb", [P, D])
        b_o1_col = sb("b_o1_col", [P, 1])
        b_o2_row = sb("b_o2_row", [P, D])
        ssp_abs = sb("ssp_abs", [P, 1])
        ssp_exp = sb("ssp_exp", [P, 1])
        ssp_ln = sb("ssp_ln", [P, 1])
        ssp_b = sb("ssp_b", [P, 1])
        ssp_rep = sb("ssp_rep", [P, P])
        c_row = sb("c_row", [P, D])
        wk_sb = sb("wk_sb", [P, D])
        wq_sb = sb("wq_sb", [P, D])
        wv_sb = sb("wv_sb", [P, D])
        wdis_sb = sb("wdis_sb", [1, HEADS])
        w_in_sb = sb("w_in_sb", [P, FF])
        b_in_row = sb("b_in_row", [P, FF])
        wf1_sb = sb("wf1_sb", [FW, FF])
        bf1_col = sb("bf1_col", [FF, 1])
        wf2_sb = sb("wf2_sb", [FF + 1, FF])
        wo1_sb = sb("wo1_sb", [FF, D])
        zeros = sb("zeros", [P, ZERO_PIECE])
        consts_loaded, made, sp_passed, pool_passed, pe_passed, made_too, c_dve, c_act, c_pe, zeroed, agg_zero = sems(
            "consts_loaded", "made", "sp_passed", "pool_passed", "pe_passed", "made_too", "c_dve", "c_act", "c_pe", "zeroed", "agg_zero")

        def row(v):
            return v.rearrange("(a d) -> a d", a=1).partition_broadcast(P)

        def col(v):
            return v.rearrange("(p a) -> p a", a=1)

        LOADS = ((w1_raw[:], W_ff1), (w2_sb[:], W_ff2.rearrange("(h p) d -> p h d", p=P)), (g_col[:], col(ln1_g)),
                 (b_col[:], col(ln1_b)), (wb_x[:], W_beta[D:2 * D, :].rearrange("d a -> a d").partition_broadcast(P)),
                 (wb_d[:], W_beta[2 * D:3 * D, :].rearrange("d a -> a d").partition_broadcast(P)),
                 (wb_he[:, 0:1], W_beta[0:D, :]), (wb_he[:, 1:2], W_beta[2 * D:3 * D, :]),
                 (w_o2_sb[:], w_o2), (b_o1_col[:], col(b_o1)), (b_o2_row[:], row(b_o2)),
                 (wk_sb[:], Wk), (wq_sb[:], Wq), (wv_sb[:], Wv), (wdis_sb[:], W_dis), (w_in_sb[:], w_in),
                 (b_in_row[:], row(b_in)), (wf1_sb[:], w_f1), (bf1_col[:], col(b_f1)), (wf2_sb[0:FF, :], w_f2),
                 (wf2_sb[FF:FF + 1, :], b_f2.rearrange("(a d) -> a d", a=1)), (wo1_sb[:], w_o1))
        ALL_LOADED = 16 * len(LOADS)

        def ring(name, slots=U):
            return [sem(f"{name}{k}") for k in range(slots)]

        def named(prefix, words):
            return sems(*(f"{prefix}_{w}" for w in words.split()))

        ROOM = 41 * 1024
        room = sb("room", [P, ROOM])
        taken = [0]

        def fsb(name, shape, dt=F32):
            sizes = dict(zip("abc", shape[1:]))
            width = 1
            for n in sizes.values():
                width *= n
            part = room[0:shape[0], taken[0]:taken[0] + width]
            taken[0] += width
            assert taken[0] <= ROOM, name
            part = part if dt == F32 else part.bitcast(dt)
            names = " ".join(sizes)
            return part.rearrange(f"p ({names}) -> p {names}", **sizes) if len(sizes) > 1 else part

        f_idx = fsb("f_idx", [P, 2, 2, T], I32)
        f_dst = fsb("f_dst", [HEADS, 2, R + 2], I32)
        f_w = fsb("f_w", [1, 2, R])
        f_attr = fsb("f_attr", [P, 2, R])
        f_x = fsb("f_x", [P, 2, 2 * T, D])
        f_xn = fsb("f_xn", [P, 2 * T, D])
        f_hT = fsb("f_hT", [P, 2, R])
        f_kT = fsb("f_kT", [P, R])
        f_vT = fsb("f_vT", [P, 2, R])
        f_prod = fsb("f_prod", [P, R])
        f_same = fsb("f_same", [HEADS, R])
        f_last = fsb("f_last", [HEADS, R])
        f_pen = fsb("f_pen", [HEADS, R])
        f_max = fsb("f_max", [HEADS, 2, R + 1])
        f_was = fsb("f_was", [HEADS, R])
        f_arg = fsb("f_arg", [HEADS, 2, R])
        f_ae = fsb("f_ae", [HEADS, 2, R])
        f_den = fsb("f_den", [HEADS, 2, R])
        f_lden = fsb("f_lden", [HEADS, R])
        f_rden = fsb("f_rden", [HEADS, R])
        f_rlast = fsb("f_rlast", [HEADS, R])
        f_ev = fsb("f_ev", [P, R])
        f_sum = fsb("f_sum", [P, 2, R])
        f_q = fsb("f_q", [P, 2, R])
        f_st = Stats("f_st", 2 * T, fsb)
        f_loaded, f_got, f_xd_out, f_q_out = (ring(n, 2) for n in ("f_loaded", "f_got", "f_xd_out", "f_q_out"))
        (f_xn_done, f_tr_done, f_h_done, f_kqv_done, f_kv_done, f_flags_done, f_prod_done, f_l_done, f_pen_done,
         f_carry_done, f_max_done, f_was_done, f_args_done, f_exps_done, f_den_done, f_lden_done, f_rden_done,
         f_rlast_done, f_spread_done, f_ev_done, f_sum_done, f_q_done) = named("f", (
             "xn_done tr_done h_done kqv_done kv_done flags_done prod_done l_done pen_done carry_done max_done was_done "
             "args_done exps_done den_done lden_done rden_done rlast_done spread_done ev_done sum_done q_done"))
        TR_S = K_ = A_ = 4
        TR_D = Q_ = E_ = 5
        V_ = R_ = 6
        L_ = 7

        d_x = fsb("d_x", [P, U, T, D])
        d_xc = fsb("d_xc", [P, DEEP, T, D])
        d_out = fsb("d_out", [P, U, T, D])
        d_u = fsb("d_u", [P, DEEP, T, D])
        d_un = fsb("d_un", [P, 2, T, D])
        d_unT = fsb("d_unT", [P, R])
        d_rz = fsb("d_rz", [P, H2, R])
        d_y = fsb("d_y", [P, 2, T, D])
        d_yn = fsb("d_yn", [P, 2, T, D])
        d_junk = fsb("d_junk", [P, T, D])
        d_scale = fsb("d_scale", [P, U, T])
        (d_dot, d_arg, d_ex, d_exp1, d_beta, d_scale2, d_uvar, d_t, d_ysum, d_ymean, d_ysq, d_yln, d_yrstd, d_nm) = (
            fsb("d_" + n, [P, 2, T]) for n in "dot arg ex exp1 beta scale2 uvar t ysum ymean ysq yln yrstd nm".split())
        d_squares = fsb("d_squares", [P, T, D])
        d_xst, d_ust = Stats("d_xst", T, fsb), Stats("d_ust", T, fsb)
        d_loaded, d_stored = ring("d_loaded"), ring("d_stored")
        (d_u_done, d_dot_done, d_arg_done, d_ex_done, d_exp1_done, d_beta_done, d_scale_done, d_scale2_done, d_uvar_done,
         d_t_done, d_un_done, d_tr_done, d_unT_done, d_z_done, d_rz_done, d_o_done, d_y_done, d_nm_done, d_yn_done,
         d_xc_done, d_out_done, d_ymean_done, d_squares_done, d_yroots) = named("d", (
             "u_done dot_done arg_done ex_done exp1_done beta_done scale_done scale2_done uvar_done t_done un_done "
             "tr_done unT_done z_done rz_done o_done y_done nm_done yn_done xc_done out_done ymean_done squares_done yroots"))
        D_TR, D_Z, D_O = 0, 1, 3

        def all_of(eng, ring, count, parts=1):
            for k, landed in enumerate(ring):
                eng.wait_ge(landed, 16 * parts * ((count - 1 - k) // len(ring) + 1))

        def nxt(eng, sem, a, groups, ahead=1):
            if isinstance(a.rounds, int):
                eng.wait_ge(sem, min(a.done(-ahead), groups))
            else:
                eng.wait_ge(sem, a.done(-ahead))

        def first_of(a):
            return isinstance(a.rounds, int) and a.m == 0

        def nodes_stored(eng):
            eng.wait_ge(agg_zero, 16 * -(-TABLE // ZERO_PIECE))
            all_of(eng, f_q_out, EG)
            all_of(eng, f_xd_out, EG)
            all_of(eng, d_stored, GROUPS)

        def edges_over(eng):
            for done in (b_totc_done, b_out_done, b_idx_done):
                eng.wait_ge(done, EG)

        def node_rows(dram, at):
            at = min(at, N - R) if isinstance(at, int) else at
            return dram[bass.ds(at, R), :].rearrange("(p j) d -> p j d", j=T)

        def spill(dram, at):
            return dram[bass.ds(at, P), :].rearrange("p (j d) -> p j d", j=T)

        def col_of(dram, at):
            return dram[bass.ds(at, P), :]

        def tiles(b):
            return bank[:, b].rearrange("p (j d) -> p j d", j=T)

        def gather(pool, to, dram, index, last_row, signal):
            pool.indirect_dma_start(to, None, dram, bass.IndirectOffsetOnAxis(ap=index, axis=0),
                                    bounds_check=last_row, oob_is_err=False).then_inc(signal, 16)

        def scatter(pool, dram, index, rows, last_row, signal):
            pool.indirect_dma_start(dram, bass.IndirectOffsetOnAxis(ap=index, axis=0), rows, None,
                                    bounds_check=last_row, oob_is_err=False).then_inc(signal, 16)

        c_b = c_row[:].rearrange("p (a d) -> p a d", a=1).to_broadcast([P, T, D])

        with nc.Block() as block:
            @block.sync
            def _(sp):
                for dst, src in LOADS:
                    sp.dma_start(dst, src).then_inc(consts_loaded, 16)

                def f_load(a):
                    k = a.slot(2)
                    at_p, at_r = a.row(sp, P), a.row(sp, R)
                    held(sp, sp_passed, f_l_done, a.done(2))
                    sp.dma_start(f_idx[:, k, 0], col_of(src_col, at_p)).then_inc(f_loaded[k], 16)
                    sp.dma_start(f_idx[:, k, 1], col_of(dst_col, at_p)).then_inc(f_loaded[k], 16)
                    sp.dma_start(f_dst[:, k], dst_row[:, bass.ds(at_r, R + 2)].partition_broadcast(HEADS)).then_inc(f_loaded[k], 16)
                    sp.dma_start(f_w[:, k], w_row[:, bass.ds(at_r, R)]).then_inc(f_loaded[k], 16)
                    sp.dma_start(f_attr[:, k], attrT[:, bass.ds(at_r, R)]).then_inc(f_loaded[k], 16)

                def f_spill_rows(a):
                    at_p = a.row(sp, P)
                    held(sp, sp_passed, f_got[a.slot(2)], a.landed(0, 2 * T))
                    sp.dma_start(spill(xd_dram, at_p), f_x[:, a.slot(2), T:]).then_inc(f_xd_out[a.slot(2)], 16)

                def f_spill_q(a):
                    at_r = a.row(sp, R)
                    held(sp, sp_passed, f_q_done, a.done())
                    sp.dma_start(q_dram[:, bass.ds(at_r, R)], f_q[:, a.slot(2)]).then_inc(f_q_out[a.slot(2)], 16)

                def d_load(a):
                    k, at = a.slot(U), a.row(sp, R)
                    held(sp, sp_passed, d_u_done, a.done(U))
                    held(sp, sp_passed, d_xc_done, a.done(U))
                    sp.dma_start(d_x[:, k], node_rows(x, at)).then_inc(d_loaded[k], 16)

                def d_store(a):
                    k, at = a.slot(U), a.row(sp, R)
                    held(sp, sp_passed, d_out_done, a.done())
                    if isinstance(at, int) and at > N - R:
                        held(sp, sp_passed, d_stored[a.slot(U, 1)], a.landed(1))
                    sp.dma_start(node_rows(out, at), d_out[:, k]).then_inc(d_stored[k], 16)

                walk(sp, GROUPS, [(SPARSE, 3, f_load), (EACH, 0, d_load), (SPARSE, 9, f_spill_rows), (SPARSE, 18, f_spill_q),
                                  (EACH, 9, d_store)], (1, 2 * T), ROUND)
                nodes_stored(sp)

            @block.gpsimd
            def _(pool):
                pool.memset(ident[:], 0.0)
                pool.memset(upper[:], 1.0)
                pool.memset(mean_of[:], 1.0 / D)
                pool.memset(head_of[:], float(D // HEADS) ** -0.5)
                pool.memset(head_to[:], 1.0)
                pool.memset(zeros[:], 0.0).then_inc(zeroed, 1)
                pool.iota(trash_i[:], pattern=[[P, T]], base=TRASH, channel_multiplier=1).then_inc(made, 1)
                pool.wait_ge(zeroed, 1)
                pool.affine_select(out=ident[:], in_=ident[:], compare_op=ALU.not_equal, fill=1.0, base=0,
                                   pattern=[[-1, P]], channel_multiplier=1).then_inc(made, 1)
                pool.affine_select(out=upper[:], in_=upper[:], compare_op=ALU.is_gt, fill=0.0, base=0,
                                   pattern=[[1, P]], channel_multiplier=-1).then_inc(made, 1)
                wide = D // HEADS
                pool.affine_select(out=head_of[:], in_=head_of[:], compare_op=ALU.is_ge, fill=0.0, base=0,
                                   pattern=[[-wide, HEADS]], channel_multiplier=1)
                pool.affine_select(out=head_to[:], in_=head_to[:], compare_op=ALU.is_ge, fill=0.0, base=0,
                                   pattern=[[1, P]], channel_multiplier=-wide).then_inc(made, 1)
                pool.wait_ge(made, 4)
                pool.affine_select(out=head_of[:], in_=head_of[:], compare_op=ALU.is_ge, fill=0.0, base=wide - 1,
                                   pattern=[[wide, HEADS]], channel_multiplier=-1)
                pool.affine_select(out=head_to[:], in_=head_to[:], compare_op=ALU.is_ge, fill=0.0, base=wide - 1,
                                   pattern=[[-1, P]], channel_multiplier=wide)
                pool.tensor_copy(trash[:], trash_i[:]).then_inc(made_too, 1)

                pool.wait_ge(c_dve, 5)

                def f_gathers(tiles_of_rows):
                    def step(a):
                        k = a.slot(2)
                        if tiles_of_rows[0] == 0:
                            held(pool, pool_passed, f_loaded[k], a.landed(0, 5))
                            held(pool, pool_passed, f_xn_done, a.done(2))
                            held(pool, pool_passed, f_xd_out[k], a.landed(2))
                        for i in tiles_of_rows:
                            gather(pool, f_x[:, k, i], x, f_idx[:, k, i // T, i % T:i % T + 1], N - 1, f_got[k])
                    return step

                def d_base(a):
                    held(pool, pool_passed, d_out_done, a.done(DEEP))
                    held(pool, pool_passed, d_loaded[a.slot(U)], a.landed())
                    pool.tensor_tensor(d_xc[:, a.slot(DEEP)], d_x[:, a.slot(U)], c_b, ALU.add).then_inc(d_xc_done, 1)

                def d_moments(a):
                    d_ust.combine_on_pool(pool, a, pool_passed)

                def d_normed(a):
                    s = a.slot(2)
                    held(pool, pool_passed, d_t_done, a.done())
                    held(pool, pool_passed, d_tr_done, a.done(2))
                    t = d_t[:, s].rearrange("p (j a) -> p j a", a=1).to_broadcast([P, T, D])
                    pool.tensor_tensor(d_un[:, s], d_u[:, a.slot(DEEP)], t, ALU.mult).then_inc(d_un_done, 1)

                def d_result(a):
                    held(pool, pool_passed, d_yn_done, a.done())
                    held(pool, pool_passed, d_xc_done, a.done())
                    held(pool, pool_passed, d_stored[a.slot(U)], a.landed(U))
                    pool.tensor_tensor(d_out[:, a.slot(U)], d_yn[:, a.slot(2)], d_xc[:, a.slot(DEEP)], ALU.add)\
                        .then_inc(d_out_done, 1)

                walk(pool, GROUPS, [(SPARSE, 1, f_gathers((0, 1, 2))), (SPARSE, 2, f_gathers((3, 4, 5))), (SPARSE, 3, f_gathers((6, 7))),
                                    (EACH, 0, d_base), (EACH, 1, d_normed), (EACH, 0, d_moments), (EACH, 5, d_result)],
                     (1, 5), ROUND)

            @block.vector
            def _(dve):
                dve.memset(eps_col[:], EPS)
                dve.memset(tiny_col[:], 1e-16)
                dve.memset(ones_col[:], 1.0)
                dve.memset(half_col[:], 0.5).then_inc(c_dve, 1)
                dve.wait_ge(consts_loaded, ALL_LOADED)
                dve.tensor_scalar(w1_g[:], w1_raw[:], g_col[:, 0:1], None, ALU.mult)
                dve.tensor_tensor(wb_he_col[:], wb_he[:, 0:1], wb_he[:, 1:2], ALU.add)
                dve.tensor_tensor(wb_row[:], wb_x[:], wb_d[:], ALU.subtract).then_inc(c_dve, 1)
                dve.wait_ge(c_act, 3)
                dve.scalar_tensor_tensor(ssp_b[:], b_o1_col[:], 0.0, ssp_ln[:], ALU.max, ALU.add).then_inc(c_dve, 1)
                dve.wait_ge(c_dve, 3)
                dve.tensor_copy(ssp_rep[:], ssp_b[:, 0:1].to_broadcast([P, P])).then_inc(c_dve, 1)
                dve.wait_ge(c_pe, 1)
                dve.tensor_copy(z_bias[:], bank[:, 0, 0:H2])
                dve.tensor_tensor(w1_c[:], w1_g[:], bank[:, 2, 0:F], ALU.subtract)
                dve.tensor_tensor(c_row[:], bank[:, 1, 0:D], b_o2_row[:], ALU.add).then_inc(c_dve, 1)

                def f_stats(a):
                    dve.wait_ge(f_got[a.slot(2)], a.landed(0, 2 * T))
                    f_st.on_vector(dve, a, f_x[:, a.slot(2)])

                def f_normed(a):
                    s = a.slot(2)
                    f_st.wait_rstd(dve, a)
                    after(dve, f_tr_done, a.done(1))
                    for j in range(2 * T):
                        last = dve.tensor_scalar(f_xn[:, j], f_x[:, s, j], f_st.nmean[:, s, j:j + 1],
                                                 f_st.rstd[:, s, j:j + 1], ALU.add, ALU.mult)
                    last.then_inc(f_xn_done, 1)

                def f_flags(a):
                    s = k = a.slot(2)
                    dve.wait_ge(f_loaded[k], a.landed(0, 5))
                    after(dve, f_rlast_done, a.done(1))
                    dve.tensor_tensor(f_same[:], f_dst[:, k, 1:R + 1], f_dst[:, k, 0:R], ALU.is_equal)
                    dve.tensor_tensor(f_last[:], f_dst[:, k, 1:R + 1], f_dst[:, k, 2:R + 2], ALU.not_equal)\
                       .then_inc(f_flags_done, 1)
                    if first_of(a):
                        dve.memset(f_max[:, s, 0:1], -FAR).then_inc(f_carry_done, 1)
                    else:
                        dve.wait_ge(f_max_done, a.done(1))
                        dve.tensor_copy(f_max[:, s, 0:1], f_max[:, 1 - s, R:R + 1]).then_inc(f_carry_done, 1)
                    dve.wait_ge(f_flags_done, a.done())
                    dve.tensor_scalar(f_pen[:], f_same[:], 1.0, FAR, ALU.subtract, ALU.mult).then_inc(f_pen_done, 1)

                def f_products(a):
                    dve.wait_ge(f_kv_done, a.done())
                    after(dve, f_l_done, a.done(1))
                    dve.tensor_tensor(f_prod[:], f_kT[:], bank[:, Q_], ALU.mult).then_inc(f_prod_done, 1)

                def f_maxima(a):
                    s = a.slot(2)
                    dve.wait_ge(f_l_done, a.done())
                    dve.wait_ge(f_pen_done, a.done())
                    dve.wait_ge(f_carry_done, a.done())
                    dve.tensor_tensor_scan(f_max[:, s, 1:R + 1], f_pen[:], bank[0:HEADS, L_], f_max[:, s, 0:1], ALU.add,
                                           ALU.max).then_inc(f_max_done, 1)
                    dve.tensor_tensor(f_was[:, 0:1], f_max[:, s, 0:1], f_pen[:, 0:1], ALU.add)
                    dve.wait_ge(f_max_done, a.done())
                    dve.tensor_tensor(f_was[:, 1:R], f_max[:, s, 1:R], f_pen[:, 1:R], ALU.add).then_inc(f_was_done, 1)
                    after(dve, f_exps_done, a.done(1))
                    dve.tensor_tensor(f_arg[:, 1], bank[0:HEADS, L_], f_max[:, s, 1:R + 1], ALU.subtract)
                    dve.wait_ge(f_was_done, a.done())
                    dve.tensor_tensor(f_arg[:, 0], f_was[:], f_max[:, s, 1:R + 1], ALU.subtract).then_inc(f_args_done, 1)

                def f_denominators(a):
                    s = a.slot(2)
                    dve.wait_ge(f_exps_done, a.done())
                    dve.tensor_tensor_scan(f_den[:, s], f_ae[:, 0], f_ae[:, 1], 0.0 if first_of(a) else f_den[:, 1 - s, R - 1:R],
                                           ALU.mult, ALU.add).then_inc(f_den_done, 1)

                def f_divisors(a):
                    dve.wait_ge(f_rden_done, a.done())
                    after(dve, f_spread_done, a.done(1))
                    dve.tensor_tensor(f_rlast[:], f_rden[:], f_last[:], ALU.mult).then_inc(f_rlast_done, 1)

                def f_sums(a):
                    s = a.slot(2)
                    dve.wait_ge(f_spread_done, a.done())
                    after(dve, f_sum_done, a.done(1))
                    dve.tensor_tensor(f_ev[:], f_vT[:, s], bank[:, E_], ALU.mult).then_inc(f_ev_done, 1)
                    dve.wait_ge(f_ev_done, a.done())
                    after(dve, f_q_done, a.done(2))
                    dve.tensor_tensor_scan(f_sum[:, s], bank[:, A_], f_ev[:], 0.0 if first_of(a) else f_sum[:, 1 - s, R - 1:R],
                                           ALU.mult, ALU.add).then_inc(f_sum_done, 1)
                    dve.wait_ge(f_sum_done, a.done())
                    after(dve, f_q_out[s], a.landed(2))
                    dve.tensor_tensor(f_q[:, s], f_sum[:, s], bank[:, R_], ALU.mult).then_inc(f_q_done, 1)

                def d_stats(a):
                    dve.wait_ge(d_loaded[a.slot(U)], a.landed())
                    d_xst.on_vector(dve, a, d_x[:, a.slot(U)])

                def d_centred(a):
                    s, k, deep = a.slot(2), a.slot(U), a.slot(DEEP)
                    d_xst.wait_mean(dve, a)
                    after(dve, d_y_done, a.done(DEEP))
                    for j in range(T):
                        last = dve.tensor_scalar(d_u[:, deep, j], d_x[:, k, j], d_xst.nmean[:, s, j:j + 1], 0.0, ALU.add, ALU.max)
                    last.then_inc(d_u_done, 1)
                    dve.wait_ge(d_u_done, a.done())
                    after(dve, d_uvar_done, a.done(2))
                    d_ust.statistics(dve, a, d_u[:, deep])

                def d_dots(a):
                    s, k = a.slot(2), a.slot(DEEP)
                    dve.wait_ge(d_u_done, a.done())
                    for j in range(T):
                        last = dve.scalar_tensor_tensor(d_junk[:, j], d_u[:, k, j], 1.0, wb_row[:], ALU.mult, ALU.mult,
                                                        accum_out=d_dot[:, s, j:j + 1])
                    last.then_inc(d_dot_done, 1)

                def d_logits(a):
                    s = a.slot(2)
                    dve.wait_ge(d_dot_done, a.done())
                    d_xst.wait_rstd(dve, a)
                    dve.tensor_tensor(d_arg[:, s], d_dot[:, s], d_xst.rstd[:, s], ALU.mult).then_inc(d_arg_done, 1)

                def d_gates(a):
                    s = a.slot(2)
                    dve.wait_ge(d_ex_done, a.done())
                    dve.tensor_scalar(d_exp1[:, s], d_ex[:, s], 1.0, None, ALU.add).then_inc(d_exp1_done, 1)
                    dve.wait_ge(d_exp1_done, a.done())
                    dve.reciprocal(d_beta[:, s], d_exp1[:, s]).then_inc(d_beta_done, 1)
                    dve.wait_ge(d_beta_done, a.done())
                    dve.tensor_tensor(d_scale[:, a.slot(U)], d_beta[:, s], d_xst.rstd[:, s], ALU.mult).then_inc(d_scale_done, 1)
                    dve.wait_ge(d_scale_done, a.done())
                    dve.tensor_tensor(d_scale2[:, s], d_scale[:, a.slot(U)], d_scale[:, a.slot(U)], ALU.mult).then_inc(d_scale2_done, 1)
                    dve.wait_ge(d_scale2_done, a.done())
                    dve.wait_ge(d_ust.steps, a.count(4, 4))
                    dve.scalar_tensor_tensor(d_uvar[:, s], d_scale2[:, s], 1.0 / D, d_ust.var[:, s], ALU.mult, ALU.mult)\
                       .then_inc(d_uvar_done, 1)

                def d_normed(a):
                    s = a.slot(2)
                    d_ust.wait_rstd(dve, a)
                    after(dve, d_un_done, a.done(2))
                    dve.tensor_tensor(d_t[:, s], d_scale[:, a.slot(U)], d_ust.rstd[:, s], ALU.mult).then_inc(d_t_done, 1)

                def d_residual(a):
                    s, k = a.slot(2), a.slot(DEEP)
                    dve.wait_ge(d_o_done, a.done())
                    after(dve, d_yn_done, a.done(2))
                    for j in range(T):
                        last = dve.scalar_tensor_tensor(d_y[:, a.slot(2), j], d_u[:, k, j], d_scale[:, a.slot(U), j:j + 1],
                                                        tiles(D_O)[:, j], ALU.mult, ALU.add, accum_out=d_ysum[:, s, j:j + 1])
                    last.then_inc(d_y_done, 1)
                    dve.wait_ge(d_y_done, a.done())
                    dve.tensor_scalar(d_ymean[:, s], d_ysum[:, s], -1.0 / D, None, ALU.mult).then_inc(d_ymean_done, 1)

                def d_shift(a):
                    s = a.slot(2)
                    dve.wait_ge(d_yroots, a.count(2, 2))
                    after(dve, d_yn_done, a.done(2))
                    dve.tensor_tensor(d_nm[:, s], d_ymean[:, s], d_yrstd[:, s], ALU.mult).then_inc(d_nm_done, 1)

                walk(dve, GROUPS, [(EACH, 5, d_shift), (EACH, 1, d_logits), (EACH, 4, d_residual),
                                   (SPARSE, 8, f_products), (EACH, 0, d_stats), (EACH, 1, d_gates), (SPARSE, 6, f_normed),
                                   (EACH, 0, d_centred), (EACH, 1, d_normed), (EACH, 0, d_dots), (SPARSE, 4, f_stats),
                                   (SPARSE, 13, f_sums), (SPARSE, 11, f_divisors), (SPARSE, 7, f_flags), (SPARSE, 9, f_maxima),
                                   (SPARSE, 10, f_denominators)], (1, 5, 2 * T), ROUND)

            @block.scalar
            def _(act):
                act.preload_act_table_set("natural_log_exp_and_others")
                act.wait_ge(zeroed, 1)
                act.wait_ge(consts_loaded, ALL_LOADED)
                act.wait_ge(c_dve, 1)
                act.activation(ssp_abs[:], b_o1_col[:], ACT.Abs).then_inc(c_act, 1)
                act.wait_ge(c_act, 1)
                act.activation(ssp_exp[:], ssp_abs[:], ACT.Exp, scale=-1.0).then_inc(c_act, 1)
                act.wait_ge(c_act, 2)
                act.activation(ssp_ln[:], ssp_exp[:], ACT.Ln, scale=0.5, bias=half_col[:, 0:1]).then_inc(c_act, 1)
                act.wait_ge(c_dve, 5)

                def zero_piece(a):
                    lo = a.m * ZERO_PIECE
                    if isinstance(a.rounds, int) and lo < TABLE:
                        hi = min(lo + ZERO_PIECE, TABLE)
                        act.dma_start(table[:, lo:hi], zeros[:, 0:hi - lo]).then_inc(agg_zero, 16)

                def f_roots(a):
                    f_st.wait_mean(act, a)
                    f_st.on_scalar(act, a)

                def f_relus(a):
                    act.wait_ge(f_tr_done, a.done())
                    act.activation(f_hT[:, 0], bank[:, TR_S], ACT.Relu)
                    act.activation(f_hT[:, 1], bank[:, TR_D], ACT.Relu).then_inc(f_h_done, 1)

                def f_keys(a):
                    act.wait_ge(f_kqv_done, a.done())
                    after(act, f_prod_done, a.done(1))
                    after(act, f_ev_done, a.done(2))
                    act.activation(f_kT[:], bank[:, K_], ACT.Copy)
                    act.activation(f_vT[:, a.slot(2)], bank[:, V_], ACT.Copy).then_inc(f_kv_done, 1)

                def f_exps(a):
                    act.wait_ge(f_args_done, a.done())
                    after(act, f_spread_done, a.done(1))
                    act.activation(f_ae[:], f_arg[:], ACT.Exp).then_inc(f_exps_done, 1)

                def f_reciprocals(a):
                    act.wait_ge(f_den_done, a.done())
                    act.activation(f_lden[:], f_den[:, a.slot(2)], ACT.Ln, bias=tiny_col[:, 0:1]).then_inc(f_lden_done, 1)
                    act.wait_ge(f_lden_done, a.done())
                    after(act, f_rlast_done, a.done(1))
                    act.activation(f_rden[:], f_lden[:], ACT.Exp, scale=-1.0).then_inc(f_rden_done, 1)

                def d_exps(a):
                    s = a.slot(2)
                    act.wait_ge(d_arg_done, a.done())
                    act.activation(d_ex[:, s], d_arg[:, s], ACT.Exp, scale=-1.0).then_inc(d_ex_done, 1)

                def d_roots(a):
                    d_xst.wait_mean(act, a)
                    d_xst.on_scalar(act, a)

                def d_roots_of_w(a):
                    act.wait_ge(d_uvar_done, a.done())
                    d_ust.on_scalar(act, a, d_uvar)

                def d_transposed(a):
                    act.wait_ge(d_tr_done, a.done())
                    act.activation(d_unT[:], bank[:, D_TR], ACT.Copy).then_inc(d_unT_done, 1)

                def d_hidden(a):
                    act.wait_ge(d_z_done, a.done())
                    after(act, d_o_done, a.done(1))
                    for h in range(H2):
                        last = act.activation(d_rz[:, h], bank[:, D_Z + h], ACT.Relu, bias=z_bias[:, h:h + 1])
                    last.then_inc(d_rz_done, 1)

                def d_roots_of_y(a):
                    s = a.slot(2)
                    act.wait_ge(d_ymean_done, a.done())
                    after(act, d_squares_done, a.done(1))
                    for j in range(T):
                        last = act.activation(d_squares[:, j], d_y[:, a.slot(2), j], ACT.Square, bias=d_ymean[:, s, j:j + 1],
                                              accum_out=d_ysq[:, s, j:j + 1])
                    last.then_inc(d_squares_done, 1)
                    act.wait_ge(d_squares_done, a.done())
                    act.activation(d_yln[:, s], d_ysq[:, s], ACT.Ln, scale=1.0 / D, bias=eps_col[:, 0:1]).then_inc(d_yroots, 1)
                    act.wait_ge(d_yroots, a.count(2, 1))
                    act.activation(d_yrstd[:, s], d_yln[:, s], ACT.Exp, scale=-0.5).then_inc(d_yroots, 1)

                def d_last_norm(a):
                    s = a.slot(2)
                    act.wait_ge(d_nm_done, a.done())
                    after(act, d_out_done, a.done(2))
                    for j in range(T):
                        last = act.activation(d_yn[:, s, j], d_y[:, a.slot(2), j], ACT.Identity, bias=d_nm[:, s, j:j + 1],
                                              scale=d_yrstd[:, s, j:j + 1])
                    last.then_inc(d_yn_done, 1)

                walk(act, GROUPS, [(EACH, 0, zero_piece), (EACH, 1, d_exps), (EACH, 3, d_hidden), (EACH, 2, d_transposed), (SPARSE, 5, f_roots),
                                   (SPARSE, 10, f_exps), (SPARSE, 11, f_reciprocals), (EACH, 0, d_roots),
                                   (EACH, 1, d_roots_of_w), (EACH, 4, d_roots_of_y), (SPARSE, 6, f_relus),
                                   (EACH, 5, d_last_norm), (SPARSE, 7, f_keys)], (1,), ROUND)

            @block.tensor
            def _(pe):
                pe.wait_ge(consts_loaded, ALL_LOADED)
                pe.wait_ge(c_dve, 4)
                pe.wait_ge(made_too, 1)
                for h in range(H2):
                    pe.matmul(bank[:, 0, h:h + 1], w1_raw[:, h * P:(h + 1) * P], b_col[:], start=True, stop=True)
                pe.matmul(bank[:, 2, 0:F], mean_of[:], w1_g[:], start=True, stop=True)
                pe.matmul(bank[:, 1, 0:D], ssp_rep[:], w_o2_sb[:], start=True, stop=True).then_inc(c_pe, 1)
                pe.wait_ge(c_dve, 5)

                def f_transposes(a):
                    pe.wait_ge(f_xn_done, a.done())
                    after(pe, f_q_done, a.done(2))
                    for e, to in enumerate((TR_S, TR_D)):
                        for j in range(T):
                            last = pe.transpose(bank[:, to, j * P:(j + 1) * P], f_xn[:, e * T + j], ident[:])
                    last.then_inc(f_tr_done, 1)

                def f_products(a):
                    k = a.slot(2)
                    pe.wait_ge(f_loaded[k], a.landed(0, 5))
                    after(pe, f_q_done, a.done(2))
                    pe.matmul(bank[:, V_], wv_sb[:], f_attr[:, k], start=True, stop=True)
                    pe.wait_ge(f_h_done, a.done())
                    pe.matmul(bank[:, Q_], wq_sb[:], f_hT[:, 1], start=True, stop=True)
                    pe.matmul(bank[:, K_], wk_sb[:], f_hT[:, 0], start=True, stop=True).then_inc(f_kqv_done, 1)

                def f_logits(a):
                    pe.wait_ge(f_prod_done, a.done())
                    after(pe, f_args_done, a.done(1))
                    pe.matmul(bank[0:HEADS, L_], head_of[:], f_prod[:], start=True, stop=False)
                    pe.matmul(bank[0:HEADS, L_], wdis_sb[:], f_w[:, a.slot(2)], start=False, stop=True).then_inc(f_l_done, 1)

                def f_spreads(a):
                    pe.wait_ge(f_rlast_done, a.done())
                    nxt(pe, f_prod_done, a, EG)
                    pe.matmul(bank[:, A_], head_to[:], f_ae[:, 0], start=True, stop=True)
                    pe.matmul(bank[:, E_], head_to[:], f_ae[:, 1], start=True, stop=True)
                    pe.matmul(bank[:, R_], head_to[:], f_rlast[:], start=True, stop=True).then_inc(f_spread_done, 1)

                def d_transposes(a):
                    s = a.slot(2)
                    pe.wait_ge(d_un_done, a.done())
                    after(pe, d_unT_done, a.done(1))
                    for j in range(T):
                        last = pe.transpose(bank[:, D_TR, j * P:(j + 1) * P], d_un[:, s, j], ident[:])
                    last.then_inc(d_tr_done, 1)

                def d_up(a):
                    pe.wait_ge(d_unT_done, a.done())
                    after(pe, d_rz_done, a.done(1))
                    for h in range(H2):
                        last = pe.matmul(bank[:, D_Z + h], w1_c[:, h * P:(h + 1) * P], d_unT[:], start=True, stop=True)
                    last.then_inc(d_z_done, 1)

                def d_down(a):
                    pe.wait_ge(d_rz_done, a.done())
                    after(pe, d_y_done, a.done(1))
                    for j in range(T):
                        for h in range(H2):
                            last = pe.matmul(tiles(D_O)[:, j], d_rz[:, h, j * P:(j + 1) * P], w2_sb[:, h],
                                             start=(h == 0), stop=(h == H2 - 1))
                    last.then_inc(d_o_done, 1)

                walk(pe, GROUPS, [(EACH, 2, d_transposes), (EACH, 3, d_down), (EACH, 2, d_up), (SPARSE, 12, f_spreads),
                                  (SPARSE, 8, f_logits), (SPARSE, 6, f_transposes), (SPARSE, 6, f_products)], (1, 5), ROUND)

        nc.clear_and_free_semaphores(signals)
        nc.all_engine_barrier()
        signals.clear()
        taken[0] = 0
        sp_passed, pool_passed, pe_passed, b_ones = sems("sp_passed_too", "pool_passed_too", "pe_passed_too", "b_ones")

        b_q = fsb("b_q", [P, U, R])
        b_x = fsb("b_x", [P, U, T, D])
        b_dst = fsb("b_dst", [P, U, R + 1], I32)
        b_src = fsb("b_src", [P, U, R], I32)
        b_idx = fsb("b_idx", [P, U, 3, T], I32)
        b_more = fsb("b_more", [P, T])
        b_out_idx = fsb("b_out_idx", [P, U, T], I32)
        b_wc = fsb("b_wc", [P, U, T])
        b_f = fsb("b_f", [FW, U, R])
        b_next = fsb("b_next", [P, R])
        b_g = fsb("b_g", [P, 2, R])
        b_u = fsb("b_u", [P, T, D])
        b_a = fsb("b_a", [P, T, D])
        b_w = fsb("b_w", [P, 2, T, D])
        b_un = fsb("b_un", [P, T, D])
        b_unT = fsb("b_unT", [P, R])
        b_rz = fsb("b_rz", [P, H2, R])
        b_y = fsb("b_y", [P, T, D])
        b_yn = fsb("b_yn", [P, T, D])
        b_x1 = fsb("b_x1", [P, T, D])
        b_out = fsb("b_out", [P, 2, T, D])
        b_u1 = fsb("b_u1", [P, T, D])
        b_u1T = fsb("b_u1T", [P, R])
        b_junk = fsb("b_junk", [P, T, D])
        b_abs = fsb("b_abs", [FF, R])
        b_exp = fsb("b_exp", [FF, R])
        b_ln = fsb("b_ln", [FF, R])
        b_pos = fsb("b_pos", [FF, R])
        b_ssp = fsb("b_ssp", [FF + 1, R])
        b_hh = fsb("b_hh", [P, T, FF])
        b_xij = fsb("b_xij", [P, 2, T, AW])
        b_eq = fsb("b_eq", [P, 2, T * R])
        b_tri = fsb("b_tri", [P, 2, T, P])
        b_tot = fsb("b_tot", [P, 2, T, AW])
        b_srcf = fsb("b_srcf", [P, 2, T])
        b_agg_idx = fsb("b_agg_idx", [P, U, T], I32)
        (b_dot, b_arg0, b_arg, b_ex, b_exp1, b_beta, b_nbeta, b_scale, b_wnm, b_nm, b_flag, b_away, b_jump) = (
            fsb("b_" + n, [P, T]) for n in "dot arg0 arg ex exp1 beta nbeta scale wnm nm flag away jump".split())
        b_xst, b_wst, b_yst, b_zst = (Stats(n, T, fsb) for n in ("b_xst", "b_wst", "b_yst", "b_zst"))
        b_loaded, b_put, b_added, b_lead_out = ring("b_loaded"), ring("b_put"), ring("b_added"), ring("b_lead_out")
        (b_next_done, b_g_done, b_tr_done, b_u_done, b_dot_done, b_arg0_done, b_arg_done, b_ex_done, b_exp1_done,
         b_beta_done, b_nbeta_done, b_a_done, b_w_done, b_un_done, b_utr_done, b_unT_done, b_z_done,
         b_rz_done, b_o_done, b_y_done, b_nm_done, b_yn_done, b_x1_done, b_out_done, b_u1_done, b_u1tr_done, b_u1T_done,
         b_hh_done, b_fl_done, b_abs_done, b_exp_done, b_ln_done, b_pos_done, b_ssp_done, b_w2_done, b_hb_done,
         b_xij_done, b_srcf_done, b_eq_done, b_tri_done, b_tot_done, b_totc_done, b_away_done,
         b_jump_done, b_idx_done, b_more_done, b_out_idx_done, b_wnm_done) = named("b", (
             "next_done g_done tr_done u_done dot_done arg0_done arg_done ex_done exp1_done beta_done nbeta_done "
             "a_done w_done un_done utr_done unT_done z_done rz_done o_done y_done nm_done yn_done x1_done "
             "out_done u1_done u1tr_done u1T_done hh_done fl_done abs_done exp_done ln_done pos_done ssp_done w2_done "
             "hb_done xij_done srcf_done eq_done tri_done tot_done totc_done away_done jump_done idx_done more_done out_idx_done wnm_done"))
        B_HE, B_TR, B_Z, B_O, B_F, B_W, B_T = 0, 1, 2, 4, 5, 6, 7
        GATE = T * AW
        tots = bank[:, B_T, 0:GATE].rearrange("p (j f) -> p j f", j=T)

        c_idx = fsb("c_idx", [P, U, T], I32)
        c_lead = fsb("c_lead", [P, U, T], I32)
        c_agg = fsb("c_agg", [P, U, T, AW])
        c_share = fsb("c_share", [P, 2, T])
        c_aT = fsb("c_aT", [FF, R])
        c_abs = fsb("c_abs", [P, R])
        c_exp = fsb("c_exp", [P, R])
        c_ln = fsb("c_ln", [P, R])
        c_pos = fsb("c_pos", [P, R])
        c_ssp = fsb("c_ssp", [P, R])
        c_res = fsb("c_res", [P, U, T, D])
        c_ready, c_got, c_stored = ring("c_ready"), ring("c_got"), ring("c_stored")
        (c_tr_done, c_aT_done, c_z_done, c_abs_done, c_exp_done, c_ln_done, c_pos_done, c_ssp_done, c_o_done,
         c_res_done, c_share_done) = named("c", "tr_done aT_done z_done abs_done exp_done ln_done pos_done ssp_done o_done res_done share_done")
        C_TR, C_Z, C_O = 0, 1, 2

        with nc.Block() as block:
            @block.sync
            def _(sp):

                def b_load(a):
                    k = a.slot(U)
                    at_p, at_r = a.row_back(sp, EG, P), a.row_back(sp, EG, R)
                    held(sp, sp_passed, b_xij_done, a.done(U))
                    sp.dma_start(b_q[:, k], q_dram[:, bass.ds(at_r, R)]).then_inc(b_loaded[k], 16)
                    sp.dma_start(b_x[:, k], spill(xd_dram, at_p)).then_inc(b_loaded[k], 16)
                    sp.dma_start(b_dst[:, k], dst_row[:, bass.ds(at_r + 1, R + 1)].partition_broadcast(P)).then_inc(b_loaded[k], 16)
                    sp.dma_start(b_src[:, k], src_row[:, bass.ds(at_r, R)].partition_broadcast(P)).then_inc(b_loaded[k], 16)
                    sp.dma_start(b_idx[:, k, 0], col_of(src_col, at_p)).then_inc(b_loaded[k], 16)
                    sp.dma_start(b_idx[:, k, 1], col_of(dst_col, at_p)).then_inc(b_loaded[k], 16)
                    sp.dma_start(b_idx[:, k, 2], col_of(next_col, at_p)).then_inc(b_loaded[k], 16)
                    sp.dma_start(b_wc[:, k], col_of(w_col, at_p)).then_inc(b_loaded[k], 16)
                    sp.dma_start(b_f[:, k], fT[:, bass.ds(at_r, R)]).then_inc(b_loaded[k], 16)

                def b_spill_lead(a):
                    at_p = a.row_back(sp, EG, P)
                    held(sp, sp_passed, b_idx_done, a.done())
                    sp.dma_start(col_of(lead_dram, at_p), b_agg_idx[:, a.slot(U)]).then_inc(b_lead_out[a.slot(U)], 16)

                walk(sp, EG, [(EACH, 0, b_load), (EACH, 7, b_spill_lead)], (1, T))
                all_of(sp, b_lead_out, EG)

                def c_load(a):
                    k, at_p = a.slot(U), a.row(sp, P)
                    held(sp, sp_passed, c_stored[k], a.landed(U, T))
                    sp.dma_start(c_idx[:, k], col_of(src_col, at_p)).then_inc(c_ready[k], 16)
                    sp.dma_start(c_lead[:, k], col_of(lead_dram, at_p)).then_inc(c_ready[k], 16)

                walk(sp, EG, [(EACH, 0, c_load)], (1, T))
                all_of(sp, c_stored, EG, T)

            @block.gpsimd
            def _(pool):

                pool.memset(b_ssp[FF:FF + 1, :], 1.0).then_inc(b_ones, 1)
                pool.wait_ge(b_ones, 1)

                def b_result(a):
                    held(pool, pool_passed, b_yn_done, a.done())
                    held(pool, pool_passed, b_u1_done, a.done(1))
                    held(pool, pool_passed, b_out_done, a.done(1))
                    pool.tensor_tensor(b_x1[:], b_yn[:], b_x[:, a.slot(U)], ALU.add).then_inc(b_x1_done, 1)

                def b_filters(a):
                    held(pool, pool_passed, b_ln_done, a.done())
                    held(pool, pool_passed, b_w2_done, a.done(1))
                    pool.tensor_tensor(b_ssp[0:FF, :], b_pos[:], b_ln[:], ALU.add).then_inc(b_ssp_done, 1)

                def b_before(a):
                    s = a.slot(2)
                    held(pool, pool_passed, b_eq_done, a.done())
                    held(pool, pool_passed, b_tot_done, a.done(2))
                    for j in range(T):
                        last = pool.tensor_tensor(b_tri[:, s, j], b_eq[:, s, j * R + j * P:j * R + (j + 1) * P], upper[:], ALU.mult)
                    last.then_inc(b_tri_done, 1)

                def b_store(a):
                    k, s = a.slot(U), a.slot(2)
                    held(pool, pool_passed, b_x1_done, a.done())
                    held(pool, pool_passed, b_put[a.slot(U, 2)], a.landed(2, T))
                    pool.tensor_tensor(b_out[:, s], b_x1[:], c_b, ALU.add).then_inc(b_out_done, 1)
                    held(pool, pool_passed, b_out_done, a.done())
                    held(pool, pool_passed, b_out_idx_done, a.done())
                    for j in range(T):
                        scatter(pool, out, b_out_idx[:, k, j:j + 1], b_out[:, s, j], N - 1, b_put[k])

                def b_add(a):
                    k, s = a.slot(U), a.slot(2)
                    held(pool, pool_passed, b_idx_done, a.done())
                    held(pool, pool_passed, b_totc_done, a.done())
                    held(pool, pool_passed, b_added[a.slot(U, 1)], a.landed(1, T))
                    for j in range(T):
                        pool.indirect_dma_start(agg, bass.IndirectOffsetOnAxis(ap=b_agg_idx[:, k, j:j + 1], axis=0),
                                                b_tot[:, s, j], None, bounds_check=AGG_ROWS - 1, oob_is_err=True,
                                                compute_op=ALU.add).then_inc(b_added[k], 16)

                walk(pool, EG, [(EACH, 2, b_result), (EACH, 2, b_filters), (EACH, 4, b_add), (EACH, 2, b_store),
                                (EACH, 2, b_before)], (1, T))
                all_of(pool, b_put, EG, T)
                all_of(pool, b_added, EG, T)

                def c_gather(a):
                    k = a.slot(U)
                    held(pool, pool_passed, c_ready[k], a.landed(0, 2))
                    held(pool, pool_passed, c_tr_done, a.done(U))
                    held(pool, pool_passed, c_share_done, a.done(U))
                    for j in range(T):
                        gather(pool, c_agg[:, k, j], agg, c_idx[:, k, j:j + 1], N - 1, c_got[k])

                def c_store(a):
                    k = a.slot(U)
                    held(pool, pool_passed, c_res_done, a.done())
                    held(pool, pool_passed, c_stored[a.slot(U, 1)], a.landed(1, T))
                    for j in range(T):
                        pool.indirect_dma_start(out, bass.IndirectOffsetOnAxis(ap=c_lead[:, k, j:j + 1], axis=0),
                                                c_res[:, k, j], None, bounds_check=N - 1, oob_is_err=False,
                                                compute_op=ALU.add).then_inc(c_stored[k], 16)

                walk(pool, EG, [(EACH, 3, c_store), (EACH, 0, c_gather)], (1, 2, T))

            @block.vector
            def _(dve):
                dve.memset(b_tot[:, :, :, FF], 1.0)
                dve.memset(b_xij[:, :, :, FF], 1.0)

                def b_back(a):
                    s, k = a.slot(2), a.slot(U)
                    dve.wait_ge(b_loaded[k], a.landed(0, 9))
                    after(dve, b_g_done, a.done(1))
                    dve.tensor_tensor(b_next[:], b_dst[:, k, 0:R], b_dst[:, k, 1:R + 1], ALU.is_equal).then_inc(b_next_done, 1)
                    dve.wait_ge(b_next_done, a.done())
                    after(dve, b_tr_done, a.done(2))
                    dve.tensor_tensor_scan(b_g[:, s, ::-1], b_next[:, ::-1], b_q[:, k, ::-1],
                                           0.0 if first_of(a) else b_g[:, 1 - s, 0:1], ALU.mult, ALU.add).then_inc(b_g_done, 1)

                def b_stats(a):
                    b_xst.on_vector(dve, a, b_x[:, a.slot(U)])

                def b_dots(a):
                    dve.wait_ge(b_u_done, a.done())
                    for j in range(T):
                        last = dve.scalar_tensor_tensor(b_junk[:, j], b_u[:, j], 1.0, wb_row[:], ALU.mult, ALU.mult,
                                                        accum_out=b_dot[:, j:j + 1])
                    last.then_inc(b_dot_done, 1)

                def b_logits(a):
                    s = a.slot(2)
                    b_xst.wait_rstd(dve, a)
                    dve.wait_ge(b_dot_done, a.done())
                    dve.tensor_tensor(b_arg0[:], b_dot[:], b_xst.rstd[:, s], ALU.mult).then_inc(b_arg0_done, 1)
                    dve.wait_ge(b_arg0_done, a.done())
                    dve.wait_ge(b_tr_done, a.done())
                    dve.tensor_tensor(b_arg[:], b_arg0[:], bank[:, B_T, GATE:GATE + T], ALU.add).then_inc(b_arg_done, 1)

                def b_gates(a):
                    s = a.slot(2)
                    dve.wait_ge(b_ex_done, a.done())
                    dve.tensor_scalar(b_exp1[:], b_ex[:], 1.0, None, ALU.add).then_inc(b_exp1_done, 1)
                    dve.wait_ge(b_exp1_done, a.done())
                    dve.reciprocal(b_beta[:], b_exp1[:]).then_inc(b_beta_done, 1)
                    dve.wait_ge(b_beta_done, a.done())
                    dve.tensor_tensor(b_scale[:], b_beta[:], b_xst.rstd[:, s], ALU.mult)
                    dve.tensor_scalar(b_nbeta[:], b_beta[:], -1.0, 1.0, ALU.mult, ALU.add).then_inc(b_nbeta_done, 1)

                def b_mixed(a):
                    s = a.slot(2)
                    dve.wait_ge(b_a_done, a.done())
                    after(dve, b_y_done, a.done(2))
                    for j in range(T):
                        last = dve.scalar_tensor_tensor(b_w[:, s, j], b_u[:, j], b_scale[:, j:j + 1], b_a[:, j],
                                                        ALU.mult, ALU.add)
                    last.then_inc(b_w_done, 1)
                    dve.wait_ge(b_w_done, a.done())
                    b_wst.on_vector(dve, a, b_w[:, s])

                def b_shift_of_w(a):
                    s = a.slot(2)
                    b_wst.wait_rstd(dve, a)
                    dve.tensor_tensor(b_wnm[:], b_wst.nmean[:, s], b_wst.rstd[:, s], ALU.mult).then_inc(b_wnm_done, 1)

                def b_residual(a):
                    s = a.slot(2)
                    dve.wait_ge(b_o_done, a.done())
                    after(dve, b_yn_done, a.done(1))
                    dve.tensor_tensor(b_y[:], b_w[:, s], tiles(B_O), ALU.add).then_inc(b_y_done, 1)
                    dve.wait_ge(b_y_done, a.done())
                    b_yst.on_vector(dve, a, b_y)

                def b_sources(a):
                    s, k = a.slot(2), a.slot(U)
                    dve.wait_ge(b_loaded[k], a.landed(0, 9))
                    after(dve, b_idx_done, a.done(2))
                    dve.tensor_copy(b_srcf[:, s], b_idx[:, k, 0]).then_inc(b_srcf_done, 1)
                    dve.tensor_tensor(b_more[:], b_idx[:, k, 1], b_idx[:, k, 2], ALU.is_equal).then_inc(b_more_done, 1)
                    dve.wait_ge(b_more_done, a.done())
                    after(dve, b_put[k], a.landed(U, T))
                    dve.scalar_tensor_tensor(b_out_idx[:, k], b_more[:], float(N + 1), b_idx[:, k, 1], ALU.mult, ALU.add)\
                       .then_inc(b_out_idx_done, 1)
                    dve.wait_ge(b_srcf_done, a.done())
                    after(dve, b_tot_done, a.done(2))
                    for j in range(T):
                        last = dve.tensor_scalar(b_eq[:, s, j * R:(j + 1) * R], b_src[:, k], b_srcf[:, s, j:j + 1], None, ALU.is_equal)
                    last.then_inc(b_eq_done, 1)

                def b_shift(a):
                    s = a.slot(2)
                    b_yst.wait_rstd(dve, a)
                    dve.tensor_tensor(b_nm[:], b_yst.nmean[:, s], b_yst.rstd[:, s], ALU.mult).then_inc(b_nm_done, 1)

                def b_stats_of_x1(a):
                    dve.wait_ge(b_x1_done, a.done())
                    b_zst.on_vector(dve, a, b_x1)

                def b_messages(a):
                    s, k = a.slot(2), a.slot(U)
                    dve.wait_ge(b_hh_done, a.done())
                    b_zst.wait_rstd(dve, a)
                    for j in range(T):
                        last = dve.scalar_tensor_tensor(b_hh[:, j], bank[:, B_W, j * FF:(j + 1) * FF],
                                                        b_zst.rstd[:, s, j:j + 1], b_in_row[:], ALU.mult, ALU.add)
                    last.then_inc(b_hb_done, 1)
                    dve.wait_ge(b_hb_done, a.done())
                    after(dve, b_tot_done, a.done(2))
                    for j in range(T):
                        last = dve.scalar_tensor_tensor(b_xij[:, s, j, 0:FF], bank[:, B_W, (T + j) * FF:(T + j + 1) * FF],
                                                        b_wc[:, k, j:j + 1], b_hh[:, j], ALU.mult, ALU.mult)
                    last.then_inc(b_xij_done, 1)

                def b_rows(a):
                    s, k = a.slot(2), a.slot(U)
                    dve.wait_ge(b_totc_done, a.done())
                    dve.tensor_scalar(b_flag[:], tots[:, :, FF], 1.0, None, ALU.min)
                    dve.tensor_tensor(b_away[:], trash[:], b_srcf[:, s], ALU.subtract).then_inc(b_away_done, 1)
                    dve.wait_ge(b_away_done, a.done())
                    dve.tensor_tensor(b_jump[:], b_flag[:], b_away[:], ALU.mult).then_inc(b_jump_done, 1)
                    dve.wait_ge(b_jump_done, a.done())
                    after(dve, b_added[k], a.landed(U, T))
                    after(dve, b_lead_out[k], a.landed(U))
                    dve.tensor_tensor(b_agg_idx[:, k], b_srcf[:, s], b_jump[:], ALU.add).then_inc(b_idx_done, 1)

                walk(dve, EG, [(EACH, 2, b_shift), (EACH, 1, b_shift_of_w), (EACH, 0, b_back), (EACH, 0, b_stats), (EACH, 4, b_rows),
                               (EACH, 2, b_sources), (EACH, 0, b_dots), (EACH, 0, b_logits), (EACH, 2, b_stats_of_x1),
                               (EACH, 0, b_gates), (EACH, 0, b_mixed), (EACH, 1, b_residual), (EACH, 2, b_messages)], (1, T, 9))
                edges_over(dve)

                def c_hidden(a):
                    k, s = a.slot(U), a.slot(2)
                    dve.wait_ge(c_got[k], a.landed(0, T))
                    after(dve, c_res_done, a.done(2))
                    dve.reciprocal(c_share[:, s], c_agg[:, k, :, FF]).then_inc(c_share_done, 1)
                    dve.wait_ge(c_ln_done, a.done())
                    after(dve, c_o_done, a.done(1))
                    dve.scalar_tensor_tensor(c_ssp[:], c_ln[:], ssp_b[:, 0:1], c_pos[:], ALU.subtract, ALU.add).then_inc(c_ssp_done, 1)

                def c_result(a):
                    s, k = a.slot(2), a.slot(U)
                    dve.wait_ge(c_o_done, a.done())
                    dve.wait_ge(c_share_done, a.done())
                    after(dve, c_stored[k], a.landed(U, T))
                    for j in range(T):
                        last = dve.tensor_scalar(c_res[:, k, j], tiles(C_O)[:, j], c_share[:, s, j:j + 1], None, ALU.mult)
                    last.then_inc(c_res_done, 1)

                walk(dve, EG, [(EACH, 1, c_result), (EACH, 0, c_hidden)], (1, T))

            @block.scalar
            def _(act):

                def b_roots(a):
                    b_xst.wait_mean(act, a)
                    b_xst.on_scalar(act, a)

                def b_centred(a):
                    s, k = a.slot(2), a.slot(U)
                    after(act, b_w_done, a.done(1))
                    for j in range(T):
                        last = act.activation(b_u[:, j], b_x[:, k, j], ACT.Relu, bias=b_xst.nmean[:, s, j:j + 1])
                    last.then_inc(b_u_done, 1)

                def b_part_of_he(a):
                    act.wait_ge(b_nbeta_done, a.done())
                    after(act, b_w_done, a.done(1))
                    for j in range(T):
                        last = act.activation(b_a[:, j], tiles(B_HE)[:, j], ACT.Copy, scale=b_nbeta[:, j:j + 1])
                    last.then_inc(b_a_done, 1)

                def b_normed(a):
                    s = a.slot(2)
                    act.wait_ge(b_wnm_done, a.done())
                    after(act, b_utr_done, a.done(1))
                    for j in range(T):
                        last = act.activation(b_un[:, j], b_w[:, s, j], ACT.Identity, bias=b_wnm[:, j:j + 1],
                                              scale=b_wst.rstd[:, s, j:j + 1])
                    last.then_inc(b_un_done, 1)

                def b_x1_centred(a):
                    s = a.slot(2)
                    after(act, b_u1tr_done, a.done(1))
                    for j in range(T):
                        last = act.activation(b_u1[:, j], b_x1[:, j], ACT.Relu, bias=b_zst.nmean[:, s, j:j + 1])
                    last.then_inc(b_u1_done, 1)

                def b_exps(a):
                    act.wait_ge(b_arg_done, a.done())
                    act.activation(b_ex[:], b_arg[:], ACT.Exp, scale=-1.0).then_inc(b_ex_done, 1)

                def b_roots_of_w(a):
                    b_wst.wait_mean(act, a)
                    b_wst.on_scalar(act, a)

                def b_transposed(a):
                    act.wait_ge(b_utr_done, a.done())
                    act.activation(b_unT[:], bank[:, B_TR], ACT.Copy).then_inc(b_unT_done, 1)

                def b_hidden(a):
                    act.wait_ge(b_z_done, a.done())
                    after(act, b_o_done, a.done(1))
                    for h in range(H2):
                        last = act.activation(b_rz[:, h], bank[:, B_Z + h], ACT.Relu, bias=z_bias[:, h:h + 1])
                    last.then_inc(b_rz_done, 1)

                def b_softplus(a):
                    act.wait_ge(b_fl_done, a.done())
                    act.activation(b_abs[:], bank[0:FF, B_F], ACT.Abs, bias=bf1_col[:, 0:1]).then_inc(b_abs_done, 1)
                    after(act, b_ssp_done, a.done(1))
                    act.activation(b_pos[:], bank[0:FF, B_F], ACT.Relu, bias=bf1_col[:, 0:1]).then_inc(b_pos_done, 1)
                    act.wait_ge(b_abs_done, a.done())
                    act.activation(b_exp[:], b_abs[:], ACT.Exp, scale=-1.0).then_inc(b_exp_done, 1)
                    act.wait_ge(b_exp_done, a.done())
                    act.activation(b_ln[:], b_exp[:], ACT.Ln, scale=0.5, bias=half_col[0:FF, 0:1]).then_inc(b_ln_done, 1)

                def b_roots_of_y(a):
                    b_yst.wait_mean(act, a)
                    b_yst.on_scalar(act, a)

                def b_last_norm(a):
                    s = a.slot(2)
                    act.wait_ge(b_nm_done, a.done())
                    after(act, b_x1_done, a.done(1))
                    for j in range(T):
                        last = act.activation(b_yn[:, j], b_y[:, j], ACT.Identity, bias=b_nm[:, j:j + 1],
                                              scale=b_yst.rstd[:, s, j:j + 1])
                    last.then_inc(b_yn_done, 1)

                def b_roots_of_x1(a):
                    b_zst.wait_mean(act, a)
                    b_zst.on_scalar(act, a)

                def b_x1_transposed(a):
                    act.wait_ge(b_u1tr_done, a.done())
                    act.activation(b_u1T[:], bank[:, B_F], ACT.Copy).then_inc(b_u1T_done, 1)

                def b_totals(a):
                    act.wait_ge(b_tot_done, a.done())
                    after(act, b_added[a.slot(U, 2)], a.landed(2, T))
                    act.activation(b_tot[:, a.slot(2), :, 0:FF], tots[:, :, 0:FF], ACT.Copy)\
                       .then_inc(b_totc_done, 1)

                walk(act, EG, [(EACH, 4, b_totals), (EACH, 1, b_normed), (EACH, 2, b_last_norm), (EACH, 0, b_roots),
                               (EACH, 1, b_transposed), (EACH, 0, b_centred), (EACH, 0, b_exps), (EACH, 1, b_hidden),
                               (EACH, 0, b_part_of_he), (EACH, 2, b_roots_of_x1), (EACH, 2, b_x1_centred), (EACH, 2, b_x1_transposed),
                               (EACH, 1, b_softplus), (EACH, 0, b_roots_of_w), (EACH, 1, b_roots_of_y)], (1, T))
                edges_over(act)

                def c_softplus(a):
                    act.wait_ge(c_tr_done, a.done())
                    act.activation(c_aT[:], bank[0:FF, C_TR], ACT.Copy).then_inc(c_aT_done, 1)
                    act.wait_ge(c_z_done, a.done())
                    act.activation(c_abs[:], bank[:, C_Z], ACT.Abs, bias=b_o1_col[:, 0:1]).then_inc(c_abs_done, 1)
                    after(act, c_ssp_done, a.done(1))
                    act.activation(c_pos[:], bank[:, C_Z], ACT.Relu, bias=b_o1_col[:, 0:1]).then_inc(c_pos_done, 1)
                    act.wait_ge(c_abs_done, a.done())
                    act.activation(c_exp[:], c_abs[:], ACT.Exp, scale=-1.0).then_inc(c_exp_done, 1)
                    act.wait_ge(c_exp_done, a.done())
                    act.activation(c_ln[:], c_exp[:], ACT.Ln, scale=0.5, bias=half_col[:, 0:1]).then_inc(c_ln_done, 1)
                walk(act, EG, [(EACH, 0, c_softplus)])

            @block.tensor
            def _(pe):

                def b_aggregates(a):
                    s = a.slot(2)
                    pe.wait_ge(b_g_done, a.done())
                    after(pe, b_a_done, a.done(1))
                    for j in range(T):
                        pe.transpose(tiles(B_HE)[:, j], b_g[:, s, j * P:(j + 1) * P], ident[:])

                def b_logits(a):
                    s = a.slot(2)
                    after(pe, b_totc_done, a.done(4))
                    after(pe, b_idx_done, a.done(4))
                    for j in range(T):
                        last = pe.matmul(bank[:, B_T, GATE + j:GATE + j + 1], b_g[:, s, j * P:(j + 1) * P], wb_he_col[:],
                                         start=True, stop=True)
                    last.then_inc(b_tr_done, 1)

                def b_transposes(a):
                    pe.wait_ge(b_un_done, a.done())
                    after(pe, b_unT_done, a.done(1))
                    for j in range(T):
                        last = pe.transpose(tiles(B_TR)[:, j], b_un[:, j], ident[:])
                    last.then_inc(b_utr_done, 1)

                def b_up(a):
                    pe.wait_ge(b_unT_done, a.done())
                    after(pe, b_rz_done, a.done(1))
                    for h in range(H2):
                        last = pe.matmul(bank[:, B_Z + h], w1_g[:, h * P:(h + 1) * P], b_unT[:], start=True, stop=True)
                    last.then_inc(b_z_done, 1)

                def b_down(a):
                    pe.wait_ge(b_rz_done, a.done())
                    after(pe, b_y_done, a.done(1))
                    for j in range(T):
                        for h in range(H2):
                            last = pe.matmul(tiles(B_O)[:, j], b_rz[:, h, j * P:(j + 1) * P], w2_sb[:, h],
                                             start=(h == 0), stop=(h == H2 - 1))
                    last.then_inc(b_o_done, 1)

                def b_filters_hidden(a):
                    k = a.slot(U)
                    pe.wait_ge(b_loaded[k], a.landed(0, 9))
                    after(pe, b_u1T_done, a.done(1))
                    pe.matmul(bank[0:FF, B_F], wf1_sb[:], b_f[:, k], start=True, stop=True).then_inc(b_fl_done, 1)

                def b_filters(a):
                    pe.wait_ge(b_ssp_done, a.done())
                    after(pe, b_xij_done, a.done(1))
                    for j in range(T):
                        last = pe.matmul(bank[:, B_W, (T + j) * FF:(T + j + 1) * FF], b_ssp[:, j * P:(j + 1) * P], wf2_sb[:],
                                         start=True, stop=True)
                    last.then_inc(b_w2_done, 1)

                def b_x1_transposes(a):
                    pe.wait_ge(b_u1_done, a.done())
                    pe.wait_ge(b_pos_done, a.done())
                    for j in range(T):
                        last = pe.transpose(tiles(B_F)[:, j], b_u1[:, j], ident[:])
                    last.then_inc(b_u1tr_done, 1)

                def b_products(a):
                    pe.wait_ge(b_u1T_done, a.done())
                    for j in range(T):
                        last = pe.matmul(bank[:, B_W, j * FF:(j + 1) * FF], b_u1T[:, j * P:(j + 1) * P], w_in_sb[:],
                                         start=True, stop=True)
                    last.then_inc(b_hh_done, 1)

                def b_totals(a):
                    pe.wait_ge(b_xij_done, a.done())
                    pe.wait_ge(b_tri_done, a.done())
                    s = a.slot(2)
                    nxt(pe, b_arg_done, a, EG, 3)
                    after(pe, b_idx_done, a.done(1))
                    after(pe, b_totc_done, a.done(1))
                    last = pe.matmul(tots[:, 0, FF:AW], b_tri[:, s, 0], ones_col[:], start=True, stop=True)
                    for i in range(T):
                        for j in range(T):
                            if j == i > 0:
                                pe.matmul(tots[:, i, FF:AW], b_tri[:, s, i], ones_col[:], start=False, stop=False)
                            w = AW if j < i else FF
                            last = pe.matmul(tots[:, i, 0:w], b_eq[:, s, j * R + i * P:j * R + (i + 1) * P], b_xij[:, s, j, 0:w],
                                             start=(j == 0), stop=(j == T - 1))
                    last.then_inc(b_tot_done, 1)

                walk(pe, EG, [(EACH, 0, b_aggregates), (EACH, 1, b_transposes), (EACH, 0, b_logits), (EACH, 1, b_up),
                              (EACH, 1, b_down), (EACH, 2, b_x1_transposes), (EACH, 2, b_filters), (EACH, 2, b_products),
                              (EACH, 1, b_filters_hidden), (EACH, 3, b_totals)], (1, 9))
                edges_over(pe)

                def c_up(a):
                    k = a.slot(U)
                    held(pe, pe_passed, c_got[k], a.landed(0, T))
                    held(pe, pe_passed, c_aT_done, a.done(1))
                    for j in range(T):
                        last = pe.transpose(bank[0:FF, C_TR, j * P:(j + 1) * P], c_agg[:, k, j, 0:FF], ident[:])
                    last.then_inc(c_tr_done, 1)
                    pe.wait_ge(c_aT_done, a.done())
                    after(pe, c_abs_done, a.done(1))
                    after(pe, c_pos_done, a.done(1))
                    pe.matmul(bank[:, C_Z], wo1_sb[:], c_aT[:], start=True, stop=True).then_inc(c_z_done, 1)

                def c_down(a):
                    pe.wait_ge(c_ssp_done, a.done())
                    after(pe, c_res_done, a.done(1))
                    for j in range(T):
                        last = pe.matmul(tiles(C_O)[:, j], c_ssp[:, j * P:(j + 1) * P], w_o2_sb[:], start=True, stop=True)
                    last.then_inc(c_o_done, 1)
                walk(pe, EG, [(EACH, 1, c_down), (EACH, 0, c_up)], (1, T))


_WEIGHTS = ['Wk', 'Wq', 'Wv', 'W_dis', 'W_beta', 'ln1_g', 'ln1_b', 'W_ff1', 'W_ff2']
_WEIGHTS_1 = ['w_in', 'b_in', 'w_f1', 'b_f1', 'w_f2', 'b_f2', 'w_o1', 'b_o1', 'w_o2', 'b_o2']


def kernel(**inputs):
    import numpy as _np
    import concourse.bacc as _bacc
    from concourse import mybir as _mybir
    from concourse.bass_utils import run_bass_kernel_spmd as _run

    given = {k: _np.asarray(v) for k, v in inputs.items()}
    n, e = given['x'].shape[0], given['src'].shape[0]
    groups = -(-e // R)
    slots = groups * R

    def filled(v, fill):
        full = _np.full((slots,) + v.shape[1:], fill, v.dtype)
        full[:e] = v
        return full

    def by_partition(v):
        return v.reshape(groups, T, P).transpose(0, 2, 1).reshape(groups * P, T)

    src, dst, weight = filled(given['src'], n), filled(given['dst'], n), filled(given['edge_weight'], 0)
    edges = _np.full((1, slots + 2), n + 1, dst.dtype)
    edges[0, 0] = -1
    edges[0, 1:-1] = dst
    laid = {
        'x': given['x'], 'attrT': filled(given['edge_attr_128'], 0).T, 'fT': filled(given['edge_attr_32'], 0).T,
        'w_col': by_partition(weight), 'w_row': weight[None, :], 'src_col': by_partition(src),
        'dst_col': by_partition(dst), 'next_col': by_partition(edges[0, 2:]), 'src_row': src[None, :], 'dst_row': edges,
    }
    for name in _WEIGHTS:
        laid['L0_' + name] = given['L0_gnn_' + name]
    for name in _WEIGHTS_1:
        laid['L1_' + name] = given['L1_gnn_' + name]
    nc = _bacc.Bacc("TRN2", target_bir_lowering=False, num_devices=1)
    arrays, args = {}, []
    for name, a in laid.items():
        a = _np.ascontiguousarray(a)
        arrays[f"in_{name}_dram"] = a
        args.append(nc.dram_tensor(f"in_{name}_dram", a.shape, _mybir.dt.from_np(a.dtype), kind="ExternalInput").ap())
    args.append(nc.dram_tensor("out_0_dram", given['x'].shape, _mybir.dt.float32, kind="ExternalOutput").ap())
    build(nc, *args)
    r = _run(nc, [arrays], core_ids=[0])
    return r.results[0]["out_0_dram"]
```
